# Optimizing a Trainium2 kernel written in Bass

```python
import numpy as np
import jax
import jax.numpy as jnp

def _softmax(x, axis=-1):
    return jax.nn.softmax(x, axis=axis)

def _gelu(x):
    return jax.nn.gelu(x, approximate=True)

def _silu(x):
    return jax.nn.silu(x)

def _sigmoid(x):
    return jax.nn.sigmoid(x)

def _layernorm(x, axis=-1, eps=1e-05):
    m = jnp.mean(x, axis=axis, keepdims=True)
    v = jnp.var(x, axis=axis, keepdims=True)
    return (x - m) / jnp.sqrt(v + eps)

def _scatter_add(tgt, idx, src, axis=0):
    return tgt.at[idx].add(src)

def _segment_sum(src, seg, n):
    return jax.ops.segment_sum(src, seg, n)
kernel_name = 'mk_gps_d1_gnn_r16_3d0857'

def setup_inputs(seed: int=0):
    np.random.seed(seed)
    _w = jnp.asarray

    def _rec_inputs():
        import jax
        import jax.numpy as jnp
        _gk = jax.random.key(seed)
        x = -0.0003713 + 1 * jax.random.normal(jax.random.fold_in(_gk, 1), (3125, 256), jnp.float32)
        src = jax.random.randint(jax.random.fold_in(_gk, 2), (100000,), 0, 3125, jnp.int32)
        dst = jnp.minimum((3125 * jax.random.uniform(jax.random.fold_in(_gk, 3), (100000,)) ** 2.0).astype(jnp.int32), 49999)
        _o = jnp.argsort(dst, stable=True)
        src = src[_o]
        dst = dst[_o]
        edge_attr_3 = -0.000451519 + 1.00018 * jax.random.normal(jax.random.fold_in(_gk, 12), (100000, 3), jnp.float32)
        return (x, src, dst, edge_attr_3)
    x, src, dst, edge_attr_3 = _rec_inputs()

    def _L0_gnn_setup():
        import jax, jax.numpy as jnp
        import numpy as np
        N_NODES = 3125
        N_EDGES = 50000
        key = jax.random.key(seed)
        k = jax.random.split(key, 7)
        in_feat, inter_dim, out_feat = (256, 256, 256)
        h = jax.random.normal(k[0], (N_NODES, in_feat), dtype=jnp.float32)
        w = jax.random.normal(k[1], (N_EDGES, 3), dtype=jnp.float32)
        edge_src = jax.random.randint(k[2], (N_EDGES,), 0, N_NODES, dtype=jnp.int32)
        edge_dst = jax.random.randint(k[3], (N_EDGES,), 0, N_NODES, dtype=jnp.int32)
        W1 = jax.random.normal(k[4], (inter_dim, in_feat + 3), dtype=jnp.float32) * jnp.sqrt(2.0 / (in_feat + 3 + inter_dim))
        b1 = jnp.zeros((inter_dim,), dtype=jnp.float32)
        W2 = jax.random.normal(k[5], (out_feat, in_feat + inter_dim), dtype=jnp.float32) * jnp.sqrt(2.0 / (in_feat + inter_dim + out_feat))
        return {'h': h, 'w': w, 'edge_src': edge_src, 'edge_dst': edge_dst, 'W1': W1, 'b1': b1, 'W2': W2}
    _L0_gnn_all = _L0_gnn_setup()
    _L0_gnn_in = {k: v for k, v in _L0_gnn_all.items() if k in ('W1', 'b1', 'W2')}
    del _L0_gnn_all

    def _L0_mix_setup():
        import jax, jax.numpy as jnp
        import numpy as np
        EMB, HEADS, DEPTH, SEQ, BATCH = (256, 8, 4, 512, 4)
        DH = EMB // HEADS
        FF = 4 * EMB
        EPS = 1e-05

        def _layernorm(x, g, b):
            mu = x.mean(-1, keepdims=True)
            var = ((x - mu) ** 2).mean(-1, keepdims=True)
            return (x - mu) * jax.lax.rsqrt(var + EPS) * g + b

        def _linear_attn(x, Wq, Wk, Wv, Wo, bo):
            b, n, dm = x.shape
            split = lambda t: t.reshape(b, n, HEADS, DH).transpose(0, 2, 1, 3)
            scale = DH ** (-0.25)
            q = jax.nn.softmax(split(x @ Wq) * scale, axis=-1)
            k = jax.nn.softmax(split(x @ Wk) * scale, axis=-2)
            v = split(x @ Wv)
            context = jnp.einsum('bhnd,bhne->bhde', k, v)
            out = jnp.einsum('bhnd,bhde->bhne', q, context)
            out = out.transpose(0, 2, 1, 3).reshape(b, n, dm)
            return out @ Wo + bo

        def _forward(x, Wq, Wk, Wv, Wo, bo, ln1_g, ln1_b, W1, b1, W2, b2, ln2_g, ln2_b):
            for i in range(DEPTH):
                h = _layernorm(x, ln1_g[i], ln1_b[i])
                x = x + _linear_attn(h, Wq[i], Wk[i], Wv[i], Wo[i], bo[i])
                h = _layernorm(x, ln2_g[i], ln2_b[i])
                x = x + (jax.nn.gelu(h @ W1[i] + b1[i], approximate=False) @ W2[i] + b2[i])
            return x
        key = jax.random.key(seed)
        ks = jax.random.split(key, 8)
        w = lambda k, shape: jax.random.normal(k, shape, dtype=jnp.float32) * 0.02
        D = DEPTH
        return {'x': jax.random.normal(ks[0], (BATCH, SEQ, EMB), dtype=jnp.float32), 'Wq': w(ks[1], (D, EMB, EMB)), 'Wk': w(ks[2], (D, EMB, EMB)), 'Wv': w(ks[3], (D, EMB, EMB)), 'Wo': w(ks[4], (D, EMB, EMB)), 'bo': jnp.zeros((D, EMB), jnp.float32), 'ln1_g': jnp.ones((D, EMB), jnp.float32), 'ln1_b': jnp.zeros((D, EMB), jnp.float32), 'W1': w(ks[5], (D, EMB, FF)), 'b1': jnp.zeros((D, FF), jnp.float32), 'W2': w(ks[6], (D, FF, EMB)), 'b2': jnp.zeros((D, EMB), jnp.float32), 'ln2_g': jnp.ones((D, EMB), jnp.float32), 'ln2_b': jnp.zeros((D, EMB), jnp.float32)}
    _L0_mix_all = _L0_mix_setup()
    _L0_mix_in = {k: v for k, v in _L0_mix_all.items() if k in ('Wq', 'Wk', 'Wv', 'Wo', 'bo', 'ln1_g', 'ln1_b', 'W1', 'b1', 'W2', 'b2', 'ln2_g', 'ln2_b')}
    del _L0_mix_all

    def _L0_ffn_setup():
        import jax, jax.numpy as jnp
        import numpy as np
        B, S, H, F, E, K = (8, 256, 256, 512, 16, 2)
        EPS = 1e-05
        key = jax.random.key(seed)
        ks = jax.random.split(key, 9)
        sc = 0.02
        return {'x': jax.random.normal(ks[0], (B, S, H), dtype=jnp.float32), 'gate_w': jax.random.normal(ks[1], (H, E), dtype=jnp.float32) * sc, 'gate_b': jnp.zeros((E,), dtype=jnp.float32), 'w1': jax.random.normal(ks[2], (E, H, F), dtype=jnp.float32) * sc, 'b1': jnp.zeros((E, F), dtype=jnp.float32), 'w2': jax.random.normal(ks[3], (E, F, H), dtype=jnp.float32) * sc, 'b2': jnp.zeros((E, H), dtype=jnp.float32), 'gamma': jnp.ones((H,), dtype=jnp.float32), 'beta': jnp.zeros((H,), dtype=jnp.float32)}
    _L0_ffn_all = _L0_ffn_setup()
    _L0_ffn_in = {k: v for k, v in _L0_ffn_all.items() if k in ('gate_w', 'gate_b', 'w1', 'b1', 'w2', 'b2', 'gamma', 'beta')}
    del _L0_ffn_all
    return {'x': x, 'src': src, 'dst': dst, 'edge_attr_3': edge_attr_3, 'L0_gnn_W1': _L0_gnn_in['W1'], 'L0_gnn_b1': _L0_gnn_in['b1'], 'L0_gnn_W2': _L0_gnn_in['W2'], 'L0_mix_Wq': _L0_mix_in['Wq'], 'L0_mix_Wk': _L0_mix_in['Wk'], 'L0_mix_Wv': _L0_mix_in['Wv'], 'L0_mix_Wo': _L0_mix_in['Wo'], 'L0_mix_bo': _L0_mix_in['bo'], 'L0_mix_ln1_g': _L0_mix_in['ln1_g'], 'L0_mix_ln1_b': _L0_mix_in['ln1_b'], 'L0_mix_W1': _L0_mix_in['W1'], 'L0_mix_b1': _L0_mix_in['b1'], 'L0_mix_W2': _L0_mix_in['W2'], 'L0_mix_b2': _L0_mix_in['b2'], 'L0_mix_ln2_g': _L0_mix_in['ln2_g'], 'L0_mix_ln2_b': _L0_mix_in['ln2_b'], 'L0_ffn_gate_w': _L0_ffn_in['gate_w'], 'L0_ffn_gate_b': _L0_ffn_in['gate_b'], 'L0_ffn_w1': _L0_ffn_in['w1'], 'L0_ffn_b1': _L0_ffn_in['b1'], 'L0_ffn_w2': _L0_ffn_in['w2'], 'L0_ffn_b2': _L0_ffn_in['b2'], 'L0_ffn_gamma': _L0_ffn_in['gamma'], 'L0_ffn_beta': _L0_ffn_in['beta']}

def reference(x, src, dst, edge_attr_3, L0_gnn_W1, L0_gnn_b1, L0_gnn_W2, L0_mix_Wq, L0_mix_Wk, L0_mix_Wv, L0_mix_Wo, L0_mix_bo, L0_mix_ln1_g, L0_mix_ln1_b, L0_mix_W1, L0_mix_b1, L0_mix_W2, L0_mix_b2, L0_mix_ln2_g, L0_mix_ln2_b, L0_ffn_gate_w, L0_ffn_gate_b, L0_ffn_w1, L0_ffn_b1, L0_ffn_w2, L0_ffn_b2, L0_ffn_gamma, L0_ffn_beta):
    import jax
    import jax.numpy as jnp

    def _L0_gnn_ref(h, w, edge_src, edge_dst, W1, b1, W2):
        import jax, jax.numpy as jnp
        import numpy as np
        N_NODES = 3125
        N_EDGES = 50000
        m = jnp.concatenate([h[edge_src], w], axis=1)
        tmp = jax.nn.relu(m @ W1.T + b1)
        h_N = jax.ops.segment_sum(tmp, edge_dst, num_segments=h.shape[0])
        h_total = jnp.concatenate([h, h_N], axis=1)
        h_lin = jax.nn.relu(h_total @ W2.T)
        norm = jnp.linalg.norm(h_lin, axis=-1, keepdims=True)
        return h_lin / jnp.maximum(norm, 1e-12)

    def _L0_mix_ref(x, Wq, Wk, Wv, Wo, bo, ln1_g, ln1_b, W1, b1, W2, b2, ln2_g, ln2_b):
        import jax, jax.numpy as jnp
        import numpy as np
        EMB, HEADS, DEPTH, SEQ, BATCH = (256, 8, 4, 512, 4)
        DH = EMB // HEADS
        FF = 4 * EMB
        EPS = 1e-05

        def _layernorm(x, g, b):
            mu = x.mean(-1, keepdims=True)
            var = ((x - mu) ** 2).mean(-1, keepdims=True)
            return (x - mu) * jax.lax.rsqrt(var + EPS) * g + b

        def _linear_attn(x, Wq, Wk, Wv, Wo, bo):
            b, n, dm = x.shape
            split = lambda t: t.reshape(b, n, HEADS, DH).transpose(0, 2, 1, 3)
            scale = DH ** (-0.25)
            q = jax.nn.softmax(split(x @ Wq) * scale, axis=-1)
            k = jax.nn.softmax(split(x @ Wk) * scale, axis=-2)
            v = split(x @ Wv)
            context = jnp.einsum('bhnd,bhne->bhde', k, v)
            out = jnp.einsum('bhnd,bhde->bhne', q, context)
            out = out.transpose(0, 2, 1, 3).reshape(b, n, dm)
            return out @ Wo + bo

        def _forward(x, Wq, Wk, Wv, Wo, bo, ln1_g, ln1_b, W1, b1, W2, b2, ln2_g, ln2_b):
            for i in range(DEPTH):
                h = _layernorm(x, ln1_g[i], ln1_b[i])
                x = x + _linear_attn(h, Wq[i], Wk[i], Wv[i], Wo[i], bo[i])
                h = _layernorm(x, ln2_g[i], ln2_b[i])
                x = x + (jax.nn.gelu(h @ W1[i] + b1[i], approximate=False) @ W2[i] + b2[i])
            return x
        return _forward(x, Wq, Wk, Wv, Wo, bo, ln1_g, ln1_b, W1, b1, W2, b2, ln2_g, ln2_b)

    def _L0_ffn_ref(x, gate_w, gate_b, w1, b1, w2, b2, gamma, beta):
        import jax, jax.numpy as jnp
        import numpy as np
        B, S, H, F, E, K = (8, 256, 256, 512, 16, 2)
        EPS = 1e-05
        gate_logits = x @ gate_w + gate_b
        topk_vals, topk_idx = jax.lax.top_k(gate_logits, K)
        topk_w = jax.nn.softmax(topk_vals, axis=-1)
        h = jax.nn.relu(jnp.einsum('bsh,ehf->bsef', x, w1) + b1)
        expert_out = jnp.einsum('bsef,efh->bseh', h, w2) + b2
        sel = jnp.take_along_axis(expert_out, topk_idx[:, :, :, None], axis=2)
        moe = jnp.sum(topk_w[..., None] * sel, axis=2)
        y = x + moe
        mu = jnp.mean(y, axis=-1, keepdims=True)
        var = jnp.var(y, axis=-1, keepdims=True)
        return (y - mu) / jnp.sqrt(var + EPS) * gamma + beta
    xn = _layernorm(x, axis=-1)
    x = x + _L0_gnn_ref(xn, edge_attr_3, src, dst, L0_gnn_W1, L0_gnn_b1, L0_gnn_W2) + _L0_mix_ref(xn[None], L0_mix_Wq, L0_mix_Wk, L0_mix_Wv, L0_mix_Wo, L0_mix_bo, L0_mix_ln1_g, L0_mix_ln1_b, L0_mix_W1, L0_mix_b1, L0_mix_W2, L0_mix_b2, L0_mix_ln2_g, L0_mix_ln2_b)[0]
    x = x + _L0_ffn_ref(_layernorm(x, axis=-1)[None], L0_ffn_gate_w, L0_ffn_gate_b, L0_ffn_w1, L0_ffn_b1, L0_ffn_w2, L0_ffn_b2, L0_ffn_gamma, L0_ffn_beta)[0]
    return x

_drawn_inputs = setup_inputs


def setup_inputs(seed=0):
    import zlib

    import numpy as np

    out = dict(_drawn_inputs(seed))
    spreads = {'L0_gnn_b1': (0.0, 0.8),
     'L0_mix_bo': (0.0, 0.1),
     'L0_mix_ln1_g': (1.0, 0.6),
     'L0_mix_ln1_b': (0.0, 0.778),
     'L0_mix_b1': (0.0, 0.1),
     'L0_mix_b2': (0.0, 0.1),
     'L0_mix_ln2_g': (1.0, 0.6),
     'L0_mix_ln2_b': (0.0, 0.623),
     'L0_ffn_gate_b': (0.0, 0.35),
     'L0_ffn_b1': (0.0, 0.8),
     'L0_ffn_b2': (0.0, 0.33),
     'L0_ffn_gamma': (1.0, 0.2),
     'L0_ffn_beta': (0.0, 0.1)}
    factors = {'edge_attr_3': 8.0,
     'L0_gnn_W1': 5.954,
     'L0_mix_Wq': 8.0,
     'L0_mix_Wk': 8.0,
     'L0_mix_Wv': 2.798,
     'L0_ffn_w1': 2.771}
    for name, (base, spread) in spreads.items():
        noise = np.random.default_rng([zlib.crc32(name.encode()), seed]).standard_normal(out[name].shape)
        drawn = base * np.exp(spread * noise) if base else spread * noise
        out[name] = jnp.asarray(drawn.astype(out[name].dtype))
    for name, factor in factors.items():
        out[name] = (out[name] * factor).astype(out[name].dtype)
    return out
```

```python
import concourse.bass as bass
from concourse import mybir
from contextlib import ExitStack

INPUTS = ['x', 'src', 'dst', 'edge_attr_3', 'L0_gnn_W1', 'L0_gnn_b1', 'L0_gnn_W2',
          'L0_mix_Wq', 'L0_mix_Wk', 'L0_mix_Wv', 'L0_mix_Wo', 'L0_mix_bo', 'L0_mix_ln1_g', 'L0_mix_ln1_b',
          'L0_mix_W1', 'L0_mix_b1', 'L0_mix_W2', 'L0_mix_b2', 'L0_mix_ln2_g', 'L0_mix_ln2_b',
          'L0_ffn_gate_w', 'L0_ffn_gate_b', 'L0_ffn_w1', 'L0_ffn_b1', 'L0_ffn_w2', 'L0_ffn_b2',
          'L0_ffn_gamma', 'L0_ffn_beta']


def build(nc, x, src, dst, edge_attr, gnn_W1, gnn_b1, gnn_W2,
          Wq, Wk, Wv, Wo, bo, ln1_g, ln1_b, W1, b1, W2, b2, ln2_g, ln2_b,
          gate_w, gate_b, ew1, eb1, ew2, eb2, gamma, beta, out):
    f32, bf16, i32 = mybir.dt.float32, mybir.dt.bfloat16, mybir.dt.int32
    ALU, ACT, AX = mybir.AluOpType, mybir.ActivationFunctionType, mybir.AxisListType
    ds = bass.ds

    N, D = x.shape
    T = 125
    NT = N // T
    GT = 5
    NG = NT // GT
    KD = D // 128
    L = Wq.shape[0]
    H, DH = 8, D // 8
    FF = W1.shape[2]
    NF = FF // 128
    SCALE = DH ** -0.25
    EPS = 1e-5
    LOW = -3.0e38
    PC = ((0, 3), (3, 5))
    E = src.shape[0]
    ET = 125
    NET = E // ET
    EP = 100
    EC = NET // EP
    NPAIR = NET + NT - 1
    PG = 8
    NEG = NPAIR // PG
    PQ = NPAIR // EC
    ROUNDS = -(-NET * NT // NPAIR)
    EA = 3
    NE, F = ew1.shape[0], ew1.shape[2]
    NFE = F // 128
    SL = 128
    MT = (2 * N + NE * (SL - 1)) // SL
    assert N == T * NT and E == ET * NET and NPAIR == PG * NEG == PQ * EC and MT % 2 == 0

    def dram(name, shape, dt):
        return nc.dram_tensor(name, shape, dt, kind="Internal").ap()
    xn_d = dram("xn_d", (N, D), f32)
    P_d = dram("P_d", (N, D), f32)
    attr_d = dram("attr_d", (ET, NPAIR, 32), bf16)
    brow_d = dram("brow_d", (2 * L, 3, D), bf16)
    slot_in = dram("slot_in", (MT * SL, D), f32)
    slot_out = dram("slot_out", (MT * SL, D), f32)

    with ExitStack() as ctx:
        def sb(name, shape, dt=f32):
            return ctx.enter_context(nc.sbuf_tensor(name, shape, dt))

        def pb(name, shape, dt=f32):
            return ctx.enter_context(nc.psum_tensor(name, shape, dt))

        def sem(name):
            return ctx.enter_context(nc.semaphore(name))

        X = sb("X", [T, NT * D])
        agg = sb("agg", [T, NT * D])
        ident = sb("ident", [128, 128])
        identb = sb("identb", [128, 128], bf16)
        ones = sb("ones", [128, 128])
        onesb = sb("onesb", [128, 128], bf16)
        iota_n = sb("iota_n", [128, T])
        headmask = sb("headmask", [128, 128])
        epsc = sb("epsc", [128, 1])
        Wkv_s = [sb(f"W{n}_s", [128, KD, D]) for n in "qkvo"]
        Wq_s, Wk_s, Wv_s, Wo_s = Wkv_s
        W1_s = sb("W1_s", [128, KD, FF])
        W2_s = sb("W2_s", [128, NF, D])
        lnp = sb("lnp", [128, L * 8])
        b1_s = sb("b1_s", [128, L * NF])
        lnc = sb("lnc", [128, 8])
        b1c = sb("b1c", [128, NF])
        brow = sb("brow", [128, L * 2 * D], bf16)
        W1T = sb("W1T", [128, KD, D])
        W2T = sb("W2T", [128, 2 * KD, D])
        Wst = sb("Wst", [128, 4 * D], bf16)
        hn = sb("hn", [T, GT, D])
        es = sb("es", [T, GT, D])
        qe = sb("qe", [T, GT, D])
        TT = sb("TT", [128, KD, GT * T])
        QT = sb("QT", [128, KD, GT * T])
        V5 = sb("V5", [T, GT, KD, 129])
        eT = sb("eT", [128, KD, GT * T])
        hid = sb("hid", [128, NF, GT * T])
        M_s = sb("M_s", [128, KD, D])
        st5 = sb("st5", [T, GT, 6])
        mv5 = sb("mv5", [T, GT, 2])
        std5 = sb("std5", [T, GT])
        mean_t = sb("mean_t", [T, NT])
        rstd_t = sb("rstd_t", [T, NT])
        st5b = sb("st5b", [T, GT, 6])
        mv5b = sb("mv5b", [T, GT, 2])
        std5b = sb("std5b", [T, GT])
        rs5b = sb("rs5b", [T, GT])
        ctxS = sb("ctxS", [128, KD, 129])
        ctxN = sb("ctxN", [128, KD, 128])
        ctxT = sb("ctxT", [128, KD, 128])
        mO = sb("mO", [128, KD])
        mN = sb("mN", [128, KD])
        pm = sb("pm", [128, KD])
        nb = sb("nb", [128, 2, KD])
        cdiff = sb("cdiff", [128, 2, KD])
        corr = sb("corr", [128, 2, KD])
        rk = sb("rk", [128, KD])
        qm = sb("qm", [T, GT, H])
        qs = sb("qs", [T, GT, H])
        qr = sb("qr", [T, GT, H])
        src_T = sb("src_T", [ET, NPAIR], i32)
        dst_T = sb("dst_T", [ET, NPAIR])
        blk_row = sb("blk_row", [1, NPAIR], i32)
        stage = [sb(f"stage{i}", [ET, PG], i32) for i in range(2)]
        G = sb("G", [ET, PG, D])
        z = sb("z", [ET, 2, 2, 2 * D])
        onehot = sb("onehot", [ET, 2, 4, T])
        ATx = sb("ATx", [ET, 2, 128], bf16)
        aT = sb("aT", [128, 2, ET], bf16)
        cum = sb("cum", [PQ, NET])
        dg = sb("dg", [PQ, NET])
        lo0 = sb("lo0", [PQ, 1])
        pid = sb("pid", [PQ, EC])
        tile_f = sb("tile_f", [PQ, EC])
        tile_i = sb("tile_i", [PQ, EC], i32)
        gsum = sb("gsum", [PQ, EC])
        blk = sb("blk", [PQ, EC])
        blk125 = sb("blk125", [PQ, EC])
        blkc = sb("blkc", [PQ, EC])
        rounds_i = sb("rounds_i", [1, 1], i32)

        bank = [pb(f"bank{i}", [128, 512]) for i in range(8)]
        edge_bank, sum_bank, attr_ps = (bank[1], bank[2]), (bank[3], bank[1]), bank[2][:, 0:128].bitcast(bf16)
        RING = [bank[4], bank[6], bank[7]]
        ROW = [bank[5], bank[0]]

        SC = hid[:, :, :].rearrange("p f n -> p (f n)")
        LG = sb("LG", [T, NT * NE])
        V5x = eT[:, :, :].rearrange("p k n -> p (k n)")
        dst_tiles = eT[0:EP, :, :].rearrange("p k n -> p (k n)")[:, 0:EC * ET].bitcast(i32)
        n_bc, lo_bc, junk = SC[0:PQ, 0:NET], SC[0:PQ, NET:2 * NET], SC[0:PQ, 2 * NET:3 * NET]
        spread = SC[0:EP, 3 * NET:3 * NET + 2 * EC * EP].rearrange("p (c q) -> p c q", q=EP)
        above = SC[0:EP, 4000:4000 + 2 * EC * (NT - 1)].rearrange("p (c b) -> p c b", b=NT - 1)
        src_rows = SC[0:PQ, 0:EC * ET]
        dst_rows = SC[0:PQ, EC * ET:2 * EC * ET]
        attr_rows = SC[0:PQ, 2 * EC * ET:5 * EC * ET]
        spread_b = V5x[0:PQ, 0:EC * PQ].rearrange("p (c q) -> p c q", q=PQ)
        ATS = [G[:, :, :].rearrange("p j d -> p (j d)").bitcast(bf16)[:, 0:PQ * 32].rearrange("p (q r) -> p q r", r=32),
              z[:, :, :, :].rearrange("p a b d -> p (a b d)").bitcast(bf16)[:, 0:PQ * 32].rearrange("p (q r) -> p q r", r=32)]
        AR = [qe[:, 2 * i:2 * i + 2, :].rearrange("p j d -> p (j d)")[:, 0:PQ * EA].rearrange("p (q c) -> p q c", c=EA)
              for i in range(2)]
        thr = sb("thr", [EP, NT - 1])
        thr2 = sb("thr2", [1, ROUNDS])
        hl = sb("hl", [EP, 2 * EC])
        hlb = sb("hlb", [EP, 2 * EC])
        rcnt = sb("rcnt", [1, 1])
        rjunk = sb("rjunk", [1, ROUNDS])
        gW1 = W1_s[:, :, 0:D + EA]
        gW2 = W2_s[:, 0:4, :].rearrange("p (k a) d -> p k (a d)", k=KD)
        w4 = sb("w4", [128, KD, 4])
        w4r = sb("w4r", [128, KD, 4])
        wparts = sb("wparts", [128, 3, KD, 4], bf16)
        WS = QT[:, :, :].rearrange("p k n -> p (k n)").bitcast(bf16)[:, 0:KD * 512].rearrange("p (h q r) -> p h q r", h=KD, q=4)
        bparts = sb("bparts", [2 * L, 3, D], bf16)
        HL = SC[0:T, 0:GT * D].rearrange("p (j d) -> p j d", d=D)
        sqj = SC[0:T, GT * D:2 * GT * D].rearrange("p (j d) -> p j d", d=D)
        ss = sb("ss", [T, GT])
        nrm = sb("nrm", [T, GT])
        rn = sb("rn", [T, GT])
        gw_s = sb("gw_s", [128, KD, NE])
        gb_s = sb("gb_s", [T, NE])
        gam_s = sb("gam_s", [T, D])
        bet_s = sb("bet_s", [T, D])
        iota_e = sb("iota_e", [T, NE])
        tri = sb("tri", [T, T])
        m1 = sb("m1", [T, NT])
        m2 = sb("m2", [T, NT])
        i1 = sb("i1", [T, NT])
        w1t = sb("w1t", [T, NT])
        w2t = sb("w2t", [T, NT])
        e21 = sb("e21", [T, NT])
        ts3 = lambda k: SC[0:T, 400 * k:400 * k + 400].rearrange("p (t e) -> p t e", e=NE)
        sel1, sel2, rtmp, lg2, mask, tot, cumt, slotp = (ts3(k) for k in range(8))
        nge = SC[0:T, 3200:3200 + NE * NT].rearrange("p (e k) -> p e k", k=NT)
        thr3 = sb("thr3", [T, NT])
        jt = sb("jt", [T, MT])
        ejc = SC[0:1, 3720:3720 + MT * NE].rearrange("p (m e) -> p m e", e=NE)
        te = sb("te", [T, NE])
        ce = sb("ce", [T, NE])
        ste = sb("ste", [T, NE])
        onee = sb("onee", [T, NT])
        ejf = sb("ejf", [1, MT])
        ej_row = sb("ej_row", [1, MT], i32)
        pos1f = sb("pos1f", [T, NT])
        pos2f = sb("pos2f", [T, NT])
        pos1 = sb("pos1", [T, NT], i32)
        pos2 = sb("pos2", [T, NT], i32)
        ps1 = sb("ps1", [T, GT], i32)
        ps2 = sb("ps2", [T, GT], i32)
        W1e = [W1_s[:, :, F * i:F * i + F] for i in range(2)]
        W2e = [W2_s[:, NFE * i:NFE * i + NFE, :] for i in range(2)]
        b1e = [sb(f"b1e{i}", [128, NFE]) for i in range(2)]
        b2e = [sb(f"b2e{i}", [128, D]) for i in range(2)]
        xs = [sb(f"xs{i}", [128, D]) for i in range(2)]
        xT = [sb(f"xT{i}", [128, KD, SL]) for i in range(2)]
        hT = [QT[:, i, 0:NFE * SL].rearrange("p (c n) -> p c n", n=SL) for i in range(2)]
        yo = [sb(f"yo{i}", [128, D]) for i in range(2)]
        u5 = SC[0:T, 0:GT * D].rearrange("p (j d) -> p j d", d=D)
        zerob = yo[0]
        browf, browr = (xT[i][0:2 * L, :, :].rearrange("p k n -> p (k n)") for i in range(2))

        x_in = [sem(f"x_in{i}") for i in range(NG)]
        gw_in, par_in, dst_in, br_in, late_in = sem("gw_in"), sem("par_in"), sem("dst_in"), sem("br_in"), sem("late_in")
        consts, cdep, wparts_done, ws_done, wT_T, wT_cp = (sem(n) for n in ("consts", "cdep", "wparts_done", "ws_done", "wT_T", "wT_cp"))
        brp_done, brow_out, brow_z = sem("brp_done"), sem("brow_out"), sem("brow_z")
        pid_done, r_mask = sem("pid_done"), sem("r_mask")
        pstat, paggr, pstd, prstd, xcopied = (sem(n) for n in ("pstat", "paggr", "pstd", "prstd", "xcopied"))
        p_out = [sem(f"p_out{i}") for i in range(GT)]
        xn_out, slots_zero = sem("xn_out"), sem("slots_zero")
        zmade = sem("zmade")
        base_step, bc_ready, bc_cp = sem("base_step"), sem("bc_ready"), sem("bc_cp")
        t_step, t_idx, rows_in, t_cast, t_T, t_cp, t_aT, a_split, a_dup, rounds_done = (sem(n) for n in (
            "t_step", "t_idx", "rows_in", "t_cast", "t_T", "t_cp", "t_aT", "a_split", "a_dup", "rounds_done"))
        a_out = [sem(f"a_out{i}") for i in range(2)]
        st_ready, atx_in, at_T, at_c, e_done, z_done, r_done, oh_done, s_done, acc_done = (sem(n) for n in (
            "st_ready", "atx_in", "at_T", "at_c", "e_done", "z_done", "r_done", "oh_done", "s_done", "acc_done"))
        g_in = [sem(f"g_in{i}") for i in range(PG)]
        settle_pool, settle_dve, settle_act, settle_pe = (sem(f"settle_{n}") for n in ("pool", "dve", "act", "pe"))
        lnc_done = sem("lnc_done")
        ring_full, ring_act, row_full, row_dve = (sem(n) for n in ("ring_full", "ring_act", "row_full", "row_dve"))
        hn_done = sem("hn_done")
        wA_in, wQ_in, wF_in = sem("wA_in"), sem("wQ_in"), sem("wF_in")
        a_stat, a_aggr, a_std, a_rstd = (sem(n) for n in ("a_stat", "a_aggr", "a_std", "a_rstd"))
        b_stat, b_aggr, b_std, b_rstd = (sem(n) for n in ("b_stat", "b_aggr", "b_std", "b_rstd"))
        l_init, k_max, m_new, nb_done, cd_done, m_cp, corr_done = (sem(n) for n in (
            "l_init", "k_max", "m_new", "nb_done", "cd_done", "m_cp", "corr_done"))
        cn_done, rk_done = sem("cn_done"), sem("rk_done")
        q_max, q_exp, q_sum, q_rec, q_norm = (sem(n) for n in ("q_max", "q_exp", "q_sum", "q_rec", "q_norm"))
        c_in, c_agg, c_ss, c_nrm, c_rn, c_y, c_stat, c_aggr, c_std, c_rstd, c_zcp = (sem(n) for n in (
            "c_in", "c_agg", "c_ss", "c_nrm", "c_rn", "c_y", "c_stat", "c_aggr", "c_std", "c_rstd", "c_zcp"))
        r_step, r_exp, r_rank, r_pos, r_thr = (sem(n) for n in ("r_step", "r_exp", "r_rank", "r_pos", "r_thr"))
        zs_cp, zs_free, ps_cp, sc_out = sem("zs_cp"), sem("zs_free"), sem("ps_cp"), sem("sc_out")
        xs_in, w1_in, w2_in = ([sem(f"{n}_in{i}") for i in range(2)] for n in ("xs", "w1", "w2"))
        yo_out = [sem(f"yo_out{i}") for i in range(2)]
        fi_in, f_u, f_stat, f_aggr, f_std, f_rstd, f_n, out_done, fp_cp = (sem(n) for n in (
            "fi_in", "f_u", "f_stat", "f_aggr", "f_std", "f_rstd", "f_n", "out_done", "fp_cp"))

        def tile(buf, t, n=1):
            return buf[:, ds(t * D, n * D)]

        RING_GA, RING_GB = 2 * GT + 4, 3 * GT + 2 * NF
        ROW_GA, ROW_GB = GT + 2, 3 * GT
        RING_A, RING_L = NT, NG * RING_GA + 1 + NG * RING_GB
        ROW_A, ROW_L = NT, NG * ROW_GA + KD + NG * ROW_GB
        RING_C, ROW_C = RING_A + L * RING_L, ROW_A + L * ROW_L
        RING_E, ROW_E = RING_C + 3 * NT, ROW_C + 2 * NT
        HN_L = 3 * NT
        HN_C = NT + L * HN_L
        EG_FIRST = 2
        EG_L = NT


        def pe_attr(e, ge):
            nc.tensor.wait_ge(atx_in, ge * 16 + 16)
            nc.tensor.wait_ge(z_done, ge * 4 + 4)
            for i in range(2):
                ins = nc.tensor.transpose(attr_ps[:, 128 * i:128 * i + ET], ATx[:, i, :], identb[0:ET, 0:ET])
            ins.then_inc(at_T, 1)

        def act_attr(e, ge):
            nc.scalar.wait_ge(at_T, ge + 2)
            nc.scalar.activation(aT[:, :, :], attr_ps.rearrange("p (i n) -> p i n", i=2)[:, :, 0:ET], ACT.Copy).then_inc(at_c, 1)

        def pe_sums(e, ge, half, last=False):
            hs = ge * 2 + half
            nc.tensor.wait_ge(oh_done, hs + 1)
            for k in range(2):
                nc.tensor.wait_ge(r_done, hs * 2 + (k + 1))
                if k == 0:
                    nc.tensor.wait_ge(acc_done, hs * 4 + 3)
                elif last:
                    nc.tensor.wait_ge(acc_done, hs * 4 + 5)
                else:
                    nc.tensor.wait_ge(z_done, hs * 2 + 7)
                for i in (2 * k, 2 * k + 1):
                    nc.tensor.matmul(sum_bank[k][0:T, 256 * (i % 2):256 * (i % 2) + 256], onehot[:, half, i, :],
                                     z[:, half, k, 256 * (i % 2):256 * (i % 2) + 256], start=True, stop=True).then_inc(s_done, 1)

        def pe_edges(e, ge, half, first=False, second=False, attr=True):
            hs = ge * 2 + half
            nc.tensor.wait_ge(at_c, ge + 2)
            for k in range(2):
                if k == 0:
                    nc.tensor.wait_ge(acc_done, hs * 4 + 1)
                    if second:
                        nc.tensor.wait_ge(z_done, hs * 2 + 3)
                else:
                    nc.tensor.wait_ge(z_done, hs * 2 + 4)
                nc.tensor.matmul(edge_bank[k][0:ET, :], aT[:, half, :], Wst[:, 2 * k * D:2 * (k + 1) * D],
                                 start=True, stop=True).then_inc(e_done, 1)
            if not first:
                pe_sums(e - (1 - half), ge - (1 - half), 1 - half)
            if half == 1 and attr:
                pe_attr(e + 1, ge + 1)

        def act_edges(e, ge, half, attr=True):
            for k in range(2):
                nc.scalar.wait_ge(z_done, ge * 4 + (2 * half + k + 5))
                nc.scalar.activation(z[:, half, k, :], z[:, half, k, :], ACT.Relu).then_inc(r_done, 1)
            if half == 1 and attr:
                act_attr(e + 1, ge + 1)

        def dve_acc(e, ge, half, i, reg):
            gp = ge * PG + (4 * half + i)
            nc.vector.wait_ge(s_done, ge * PG + (4 * half + 2 * (i // 2) + 7))
            nc.vector.wait_ge(acc_done, gp + 5)
            part = agg[:, ds(reg * D, D)]
            nc.vector.tensor_tensor(part, sum_bank[i // 2][0:T, 256 * (i % 2):256 * (i % 2) + 256], part, ALU.add).then_inc(acc_done, 1)

        def blocks_of(e, half):
            return [nc.vector.value_load(blk_row[0:1, ds(e * PG + (4 * half + i), 1)], min_val=0, max_val=NT - 1) for i in range(4)]

        def dve_edges(e, ge, half, first=False):
            prev_e, prev_ge, prev_half = e - (1 - half), ge - (1 - half), 1 - half
            regs = None if first else blocks_of(prev_e, prev_half)
            nc.vector.wait_ge(s_done, ge * 8 + (4 * half + 1))
            nc.vector.tensor_tensor(onehot[:, half, :, :], iota_n[0:ET, :].unsqueeze(1).to_broadcast([ET, 4, T]),
                                    dst_T[:, ds(e * PG + 4 * half, 4)].unsqueeze(2).to_broadcast([ET, 4, T]),
                                    ALU.is_equal).then_inc(oh_done, 1)
            for k in range(2):
                nc.vector.wait_ge(e_done, ge * 4 + (2 * half + k + 1))
                for j in (4 * half + 2 * k, 4 * half + 2 * k + 1):
                    nc.vector.wait_ge(g_in[j], ge * 16 + 16)
                nc.vector.tensor_tensor(z[:, half, k, :], edge_bank[k][0:ET, :],
                                        G[:, 4 * half + 2 * k:4 * half + 2 * k + 2, :].rearrange("p j d -> p (j d)"),
                                        ALU.add).then_inc(z_done, 1)
            if not first:
                for i in range(4):
                    dve_acc(prev_e, prev_ge, prev_half, i, regs[i])

        def pool_edges(r):
            def group(e, ge, s):
                nc.gpsimd.tensor_copy(stage[s][:, :], src_T[:, ds(e * PG, PG)]).then_inc(st_ready, 1)
                v = nc.gpsimd.snap(ge + 1)
                nc.gpsimd.wait_ge(st_ready, v)
                nc.gpsimd.sem_inc(settle_pool, 1)
                for j in range(PG):
                    if j % 2 == 0:
                        v = nc.gpsimd.snap(ge * 4 + (j // 2 + 1))
                        nc.gpsimd.wait_ge(z_done, v)
                        nc.gpsimd.sem_inc(settle_pool, 1)
                    nc.gpsimd.indirect_dma_start(G[:, j, :], None, P_d[:, :],
                                                 bass.IndirectOffsetOnAxis(ap=stage[s][:, j:j + 1], axis=0)).then_inc(g_in[j], 16)
            for i in range(2):
                nc.gpsimd.wait_ge(a_out[i], r * (EC // 2 * 16) + EC // 2 * 16 if isinstance(r, int)
                                  else nc.gpsimd.snap(r * (EC // 2 * 16) + EC // 2 * 16))
                nc.gpsimd.sem_inc(settle_pool, 1)
            with nc.gpsimd.Fori(0, NEG // 2) as i:
                for s in range(2):
                    group(i * 2 + s, i * 2 + s + r * NEG, s)
            group(NEG - 1, NEG - 1 + r * NEG, 0)

        def sp_attr(e, ge):
            nc.sync.wait_ge(at_T, ge + 1)
            nc.sync.dma_start(ATx[:, :, :].rearrange("p i r -> p (i r)"),
                              attr_flat[:, ds(e * PG * 32, PG * 32)]).then_inc(atx_in, 16)

        attr_flat = attr_d.rearrange("e p r -> e (p r)")


        def dve_tables_a(r):
            ts = [0]

            def step(ins):
                ts[0] += 1
                ins.then_inc(t_step, 1)
                nc.vector.wait_ge(t_step, r * (2 * EC + 2) + ts[0])

            if not isinstance(r, int):
                nc.vector.tensor_scalar(pid[:, :], pid[:, :], float(NPAIR), None, ALU.add).then_inc(pid_done, 1)
                nc.vector.wait_ge(pid_done, r)
            for c in range(EC):
                step(nc.vector.tensor_scalar(junk, cum[:, :], pid[:, c:c + 1], None, ALU.is_le, ALU.add, accum_out=tile_f[:, c:c + 1]))
                step(nc.vector.scalar_tensor_tensor(junk, cum[:, :], pid[:, c:c + 1], dg[:, :], ALU.is_le, ALU.mult,
                                                    accum_out=gsum[:, c:c + 1]))
            nc.vector.tensor_scalar(tile_i[:, :], tile_f[:, :], float(NET - 1), None, ALU.min).then_inc(t_idx, 1)
            step(nc.vector.scalar_tensor_tensor(blk[:, :], gsum[:, :], lo0[:, :], pid[:, :], ALU.add, ALU.add))
            nc.vector.tensor_scalar(blk125[:, :], blk[:, :], float(T), None, ALU.mult)
            step(nc.vector.tensor_scalar(blkc[:, :], blk[:, :], float(NT - 1), None, ALU.min))
            nc.vector.tensor_tensor(spread_b, ident[0:PQ, 0:PQ].unsqueeze(1).to_broadcast([PQ, EC, PQ]),
                                    blkc[:, :].unsqueeze(2).to_broadcast([PQ, EC, PQ]), ALU.mult).then_inc(t_cast, 1)

        def dve_tables_b(r):
            nc.vector.wait_ge(rows_in, r * (3 * EC * 16) + 3 * EC * 16)
            nc.vector.tensor_copy(src_rows, src_rows.bitcast(i32)).then_inc(t_cast, 1)
            nc.vector.tensor_tensor(dst_rows.rearrange("p (c e) -> p c e", e=ET),
                                    dst_rows.bitcast(i32).rearrange("p (c e) -> p c e", e=ET),
                                    blk125[:, :].unsqueeze(2).to_broadcast([PQ, EC, ET]), ALU.subtract).then_inc(t_cast, 1)
            for c in range(EC):
                ps = bank[1 + c % 2][0:ET, 0:EA * PQ].rearrange("p (a q) -> p q a", a=EA)
                ax, ar = ATS[c % 2], AR[c % 2]
                nc.vector.wait_ge(t_aT, r * EC + (c + 1))
                if c >= 2:
                    nc.vector.wait_ge(a_out[c % 2], r * (EC // 2 * 16) + 16 * (c // 2))
                nc.vector.tensor_copy(ax[:, :, 0:3], ps).then_inc(a_split, 1)
                nc.vector.wait_ge(a_split, r * (4 * EC) + 4 * c + 1)
                nc.vector.tensor_tensor(ar, ps, ax[:, :, 0:3], ALU.subtract).then_inc(a_split, 1)
                nc.vector.wait_ge(a_split, r * (4 * EC) + 4 * c + 2)
                nc.vector.tensor_copy(ax[:, :, 3:6], ar).then_inc(a_split, 1)
                nc.vector.wait_ge(a_split, r * (4 * EC) + 4 * c + 3)
                nc.vector.tensor_tensor(ax[:, :, 6:9], ar, ax[:, :, 3:6], ALU.subtract).then_inc(a_split, 1)

        def pool_tables_a(r):
            v = nc.gpsimd.snap(r + 1) if not isinstance(r, int) else r + 1
            nc.gpsimd.wait_ge(t_idx, v)
            nc.gpsimd.sem_inc(settle_pool, 1)
            for c in range(EC):
                for rows, table, w in ((src_rows.bitcast(i32), src.rearrange("(t e) -> t e", e=ET), ET),
                                       (dst_rows.bitcast(i32), dst.rearrange("(t e) -> t e", e=ET), ET),
                                       (attr_rows, edge_attr.rearrange("(t e) a -> t (e a)", e=ET), ET * EA)):
                    nc.gpsimd.indirect_dma_start(rows[:, c * w:(c + 1) * w], None, table,
                                                 bass.IndirectOffsetOnAxis(ap=tile_i[:, c:c + 1], axis=0)).then_inc(rows_in, 16)
        def pool_tables_b(r):
            for i in range(2):
                nc.gpsimd.memset(ATS[i][:, :, 27:30], 1.0).then_inc(a_dup, 1)
                nc.gpsimd.memset(ATS[i][:, :, 30:32], 0.0).then_inc(a_dup, 1)
            for c in range(EC):
                v = nc.gpsimd.snap(r * (4 * EC) + 4 * c + 4) if not isinstance(r, int) else 4 * c + 4
                nc.gpsimd.wait_ge(a_split, v)
                nc.gpsimd.sem_inc(settle_pool, 1)
                for i in (1, 2):
                    nc.gpsimd.tensor_copy(ATS[c % 2][:, :, 9 * i:9 * i + 9], ATS[c % 2][:, :, 0:9]).then_inc(a_dup, 1)

        def pe_tables(r):
            nc.tensor.wait_ge(t_cast, r * 3 + 1)
            flat = spread_b.rearrange("p c q -> p (c q)")
            for i in range(2):
                ins = nc.tensor.matmul(bank[6 + i][0:1, 0:4 * PQ], ones[0:PQ, 0:1], flat[:, 4 * PQ * i:4 * PQ * (i + 1)], start=True, stop=True)
            ins.then_inc(t_T, 1)
            for b, rows in ((1, src_rows), (3, dst_rows)):
                nc.tensor.wait_ge(t_cast, r * 3 + 2 + b // 2)
                for c in range(EC):
                    ins = nc.tensor.transpose(bank[b + c // 4][0:ET, PQ * (c % 4):PQ * (c % 4) + PQ], rows[:, c * ET:(c + 1) * ET],
                                              ident[0:PQ, 0:PQ])
                ins.then_inc(t_T, 1)
            nc.tensor.wait_ge(t_cp, r * 6 + 6)
            av = attr_rows.rearrange("p (c e a) -> p c a e", e=ET, a=EA)
            for c in range(EC):
                if c >= 2:
                    nc.tensor.wait_ge(a_split, r * (4 * EC) + 4 * (c - 2) + 2)
                for a in range(EA):
                    ins = nc.tensor.transpose(bank[1 + c % 2][0:ET, PQ * a:PQ * a + PQ], av[:, c, a, :], ident[0:PQ, 0:PQ])
                ins.then_inc(t_aT, 1)

        def act_tables(r):
            nc.scalar.wait_ge(t_T, r * 3 + 1)
            for i in range(2):
                nc.scalar.activation(blk_row[0:1, 4 * PQ * i:4 * PQ * (i + 1)], bank[6 + i][0:1, 0:4 * PQ], ACT.Copy).then_inc(t_cp, 1)
            for n, (b, to) in enumerate(((1, src_T), (3, dst_T))):
                nc.scalar.wait_ge(t_T, r * 3 + 2 + n)
                for i in range(2):
                    nc.scalar.activation(to[:, 4 * PQ * i:4 * PQ * (i + 1)], bank[b + i][0:ET, 0:4 * PQ], ACT.Copy).then_inc(t_cp, 1)

        def sp_tables(r):
            for c in range(EC):
                nc.sync.wait_ge(a_dup, r * (4 + 2 * EC) + 4 + 2 * (c + 1))
                nc.sync.dma_start(attr_flat[:, c * PQ * 32:(c + 1) * PQ * 32], ATS[c % 2].rearrange("p q r -> p (q r)")).then_inc(a_out[c % 2], 16)
            for i in range(2):
                nc.sync.wait_ge(a_out[i], r * (EC // 2 * 16) + EC // 2 * 16)


        def more_rounds(eng, tables, first, middle, last):
            eng.wait_ge(rounds_done, 1)
            rounds = eng.value_load(rounds_i[0:1, 0:1], min_val=1, max_val=ROUNDS)
            with eng.If(rounds > 1):
                with eng.Fori(1, rounds) as r:
                    tables(r)
                    first(r)
                    if middle is not None:
                        with eng.Fori(1, NEG - 1) as e:
                            middle(e, r * NEG + e)
                    last(r)

        block = ctx.enter_context(nc.Block())

        @block.sync
        def _(sp):
            sp.dma_start(gW1, gnn_W1.rearrange("(h p) f -> p h f", p=128)).then_inc(gw_in, 16)
            sp.dma_start(gW2, gnn_W2.rearrange("(h p) f -> p h f", p=128)).then_inc(gw_in, 16)
            with nc.allow_non_contiguous_dma(reason="short vectors to columns"):
                sp.dma_start(w4[:, :, 3:4].squeeze(2), gnn_b1.rearrange("(h p) -> p h", p=128)).then_inc(gw_in, 16)
            sp.dma_start(dst_tiles.rearrange("p (c e) -> p c e", e=ET), dst.rearrange("(c p e) -> p c e", p=EP, e=ET)).then_inc(dst_in, 16)
            for g in range(NG):
                sp.dma_start(X[:, g * GT * D:(g + 1) * GT * D].rearrange("p (t d) -> p t d", d=D),
                             x[g * GT * T:(g + 1) * GT * T, :].rearrange("(t p) d -> p t d", p=T)).then_inc(x_in[g], 16)
            sp.dma_start(browf[0:L, :], bo).then_inc(br_in, 16)
            sp.dma_start(browf[L:2 * L, :], b2).then_inc(br_in, 16)
            lnv = lnp[:, :].rearrange("p (l w k) -> p l w k", l=L, w=4)
            with nc.allow_non_contiguous_dma(reason="short vectors to columns"):
                for w, v in enumerate((ln1_g, ln1_b, ln2_g, ln2_b)):
                    for l in range(L):
                        sp.dma_start(lnv[:, l, w, :], v[l, :].rearrange("(k p) -> p k", p=128)).then_inc(par_in, 16)
                for l in range(L):
                    sp.dma_start(b1_s[:, l * NF:(l + 1) * NF], b1[l, :].rearrange("(f p) -> p f", p=128)).then_inc(par_in, 16)
            sp.wait_ge(brp_done, 4)
            sp.dma_start(brow_d, bparts[:, :, :]).then_inc(brow_out, 16)
            sp.wait_ge(brow_out, 16)
            sp.wait_ge(brow_z, 1)
            for l in range(L):
                for w in range(2):
                    sp.dma_start(brow[0:3, (2 * l + w) * D:(2 * l + w + 1) * D], brow_d[w * L + l]).then_inc(brow_out, 16)
            sp.dma_start(gw_s[:, :, :], gate_w.rearrange("(k p) e -> p k e", p=128)).then_inc(late_in, 16)
            sp.dma_start(gb_s[:, :], gate_b.unsqueeze(0).to_broadcast([T, NE])).then_inc(late_in, 16)
            sp.dma_start(gam_s[:, :], gamma.unsqueeze(0).to_broadcast([T, D])).then_inc(late_in, 16)
            sp.dma_start(bet_s[:, :], beta.unsqueeze(0).to_broadcast([T, D])).then_inc(late_in, 16)
            with sp.Fori(0, NG) as g:
                for j in range(GT):
                    sp.wait_ge(row_dve, g * GT + j + 2)
                    sp.dma_start(P_d[ds((g * GT + j) * T, T), :], es[:, j, :]).then_inc(p_out[j], 16)
            sp.wait_ge(xcopied, NT + GT)
            sp.dma_start(xn_d.rearrange("(t p) d -> p t d", p=T), X[:, :].rearrange("p (t d) -> p t d", d=D)).then_inc(xn_out, 16)
            sp_tables(0)
            sp.wait_ge(zmade, 1)
            for i in range(8):
                sp.dma_start(slot_in.rearrange("(a i p) d -> i p a d", i=8, p=128)[i],
                             zerob[:, :].unsqueeze(1).to_broadcast([128, MT // 8, D])).then_inc(slots_zero, 16)

            def load(dst_ap, src_ap, s):
                sp.dma_start(dst_ap, src_ap).then_inc(s, 16)

            def weights_A(l):
                load(Wk_s[:, :, :], Wk[ds(l, 1)].rearrange("o (k p) d -> p (o k) d", p=128), wA_in)
                load(Wv_s[:, :, :], Wv[ds(l, 1)].rearrange("o (k p) d -> p (o k) d", p=128), wA_in)

            def weights_B(l):
                load(Wq_s[:, :, :], Wq[ds(l, 1)].rearrange("o (k p) d -> p (o k) d", p=128), wQ_in)
                load(Wo_s[:, :, :], Wo[ds(l, 1)].rearrange("o (k p) d -> p (o k) d", p=128), wQ_in)
                load(W1_s[:, :, :], W1[ds(l, 1)].rearrange("o (k p) d -> p (o k) d", p=128), wF_in)
                load(W2_s[:, :, :], W2[ds(l, 1)].rearrange("o (k p) d -> p (o k) d", p=128), wF_in)

            sp.wait_ge(wT_cp, 3)
            sp.wait_ge(wparts_done, 1)
            for e in range(EG_FIRST + 1):
                if e:
                    sp_attr(e, e)
                else:
                    sp.dma_start(ATx[:, :, :].rearrange("p i r -> p (i r)"), attr_flat[:, 0:PG * 32]).then_inc(atx_in, 16)
            with sp.Fori(0, L) as l:
                sp.wait_ge(cn_done, l + 1)
                weights_A(l)
                sp.wait_ge(row_full, l * ROW_L + ROW_A)
                weights_B(l)
                with sp.Fori(0, NG) as g:
                    e = l * EG_L + g + (EG_FIRST + 1)
                    sp_attr(e, e)
                with sp.Fori(0, NG) as g:
                    for k in range(4):
                        e = l * EG_L + g * 4 + (EG_FIRST + 1 + NG + k)
                        sp_attr(e, e)
            more_rounds(sp, sp_tables, lambda r: (sp_attr(0, r * NEG), sp_attr(1, r * NEG + 1)),
                        lambda e, ge: sp_attr(e + 1, ge + 1), lambda r: None)
            with sp.Fori(0, NG) as g:
                sp.wait_ge(row_dve, g * (2 * GT) + ROW_C + 1)
                sp.dma_start(es[:, :, :], xn_d[ds(g * GT * T, GT * T), :].rearrange("(t p) d -> p t d", p=T)).then_inc(c_in, 16)
                sp.dma_start(qe[:, :, :], x[ds(g * GT * T, GT * T), :].rearrange("(t p) d -> p t d", p=T)).then_inc(c_in, 16)

            def store_tile(m, s):
                sp.dma_start(slot_out[ds(m * SL, SL), :], yo[s][:, :]).then_inc(yo_out[s], 16)

            def expert_tile(m, s, first=False):
                ex = sp.value_load(ej_row[0:1, ds(m, 1)], min_val=0, max_val=NE - 1)
                sp.wait_ge(ring_full, m * 2 + (RING_E - 3))
                load(xs[s][:, :], slot_in[ds(m * SL, SL), :], xs_in[s])
                sp.wait_ge(ring_act, m * 2 + (RING_E - 1))
                load(W1e[s], ew1[ds(ex, 1)].rearrange("o (k p) f -> p (o k) f", p=128), w1_in[s])
                load(b1e[s][:, :], eb1[ds(ex, 1), :].rearrange("o (p c) -> p (o c)", c=NFE), w1_in[s])
                sp.wait_ge(row_dve, m + ROW_E)
                if not first:
                    store_tile(m - 2, s)
                load(W2e[s], ew2[ds(ex, 1)].rearrange("o (p c) d -> p (o c) d", c=NFE), w2_in[s])
                load(b2e[s][:, :], eb2[ds(ex, 1), :].to_broadcast([128, D]), w2_in[s])
            sp.wait_ge(r_pos, 3)
            sp.wait_ge(sc_out, 2 * NT * 16)
            for s in range(2):
                expert_tile(s, s, first=True)
            with sp.Fori(1, MT // 2) as i:
                for s in range(2):
                    expert_tile(i * 2 + s, s)
            for s in range(2):
                sp.wait_ge(row_dve, MT + s + ROW_E)
                store_tile(MT - 2 + s, s)
            with sp.Fori(0, NG) as g:
                for j in range(GT):
                    sp.wait_ge(f_n, g * (4 * GT) + 4 * j + 4)
                    sp.dma_start(out[ds((g * GT + j) * T, T), :], u5[:, j, :]).then_inc(out_done, 16)
            sp.wait_ge(out_done, NT * 16 + 16)

        @block.gpsimd
        def _(pool):
            for t, v in ((ident, 0.0), (identb, 0.0), (headmask, 1.0), (tri, 1.0)):
                pool.memset(t[:, :], v).then_inc(cdep, 1)
            pool.memset(ones[:, :], 1.0).then_inc(consts, 1)
            pool.memset(onesb[:, :], 1.0).then_inc(consts, 1)
            pool.memset(epsc[:, :], EPS).then_inc(consts, 1)
            pool.memset(V5[:, :, :, 128:129], 1.0).then_inc(consts, 1)
            pool.memset(onee[:, :], 1.0).then_inc(consts, 1)
            pool.wait_ge(cdep, 4)
            for t in (ident, identb):
                pool.affine_select(out=t[:, :], in_=t[:, :], compare_op=ALU.not_equal, fill=1.0, base=0,
                                   pattern=[[-1, 128]], channel_multiplier=1).then_inc(consts, 1)
            pool.affine_select(out=tri[:, :], in_=tri[:, :], compare_op=ALU.is_gt, fill=0.0, base=0,
                               pattern=[[1, T]], channel_multiplier=-1).then_inc(consts, 1)
            hm = headmask[:, :].rearrange("p (c d) -> p c d", d=DH)
            pool.affine_select(out=hm, in_=hm, compare_op=ALU.is_ge, fill=0.0, base=0,
                               pattern=[[-DH, 128 // DH], [0, DH]], channel_multiplier=1).then_inc(cdep, 1)
            pool.wait_ge(cdep, 5)
            pool.affine_select(out=hm, in_=hm, compare_op=ALU.is_ge, fill=0.0, base=DH - 1,
                               pattern=[[DH, 128 // DH], [0, DH]], channel_multiplier=-1).then_inc(consts, 1)
            pool.iota(iota_n[:, :], [[1, T]], base=0, channel_multiplier=0, allow_small_or_imprecise_dtypes=True).then_inc(consts, 1)
            pool.iota(iota_e[:, :], [[1, NE]], base=-NE, channel_multiplier=0, allow_small_or_imprecise_dtypes=True).then_inc(consts, 1)
            pool.iota(thr[:, :], [[T, NT - 1]], base=T, channel_multiplier=0, allow_small_or_imprecise_dtypes=True).then_inc(consts, 1)
            pool.iota(thr2[:, :], [[NPAIR, ROUNDS]], base=0, channel_multiplier=0, allow_small_or_imprecise_dtypes=True).then_inc(consts, 1)
            pool.iota(thr3[:, :], [[SL, NT]], base=0, channel_multiplier=0, allow_small_or_imprecise_dtypes=True).then_inc(consts, 1)
            pool.iota(jt[:, :], [[1, MT]], base=0, channel_multiplier=0, allow_small_or_imprecise_dtypes=True).then_inc(consts, 1)
            pool.iota(pid[:, :], [[PQ, EC]], base=0, channel_multiplier=1, allow_small_or_imprecise_dtypes=True).then_inc(consts, 1)
            pool.memset(brow[:, :], 0.0).then_inc(brow_z, 1)
            pool.memset(zerob[:, :], 0.0).then_inc(zmade, 1)
            pool.memset(agg[:, :], 0.0).then_inc(consts, 1)
            pool_tables_a(0)
            pool.memset(WS[:, :, :, :], 0.0).then_inc(cdep, 1)
            pool.wait_ge(cdep, 6)
            pool.wait_ge(wparts_done, 5)
            for q in range(4):
                for j in range(3):
                    for h in range(KD):
                        o = 32 * q + 9 * j
                        pool.tensor_copy(WS[:, h, q, o:o + 9].rearrange("p (i c) -> p i c", c=EA),
                                         wparts[:, j, h, 0:EA].unsqueeze(1).to_broadcast([128, 3, EA])).then_inc(ws_done, 1)
                        pool.tensor_copy(WS[:, h, q, 32 * q + 27 + j:32 * q + 28 + j], wparts[:, j, h, EA:EA + 1]).then_inc(ws_done, 1)
            pool_tables_b(0)
            for j in range(GT):
                pool.wait_ge(p_out[j], 16 * NG + 16)
            pool.wait_ge(t_cp, 6)
            pool_edges(0)
            more_rounds(pool, lambda r: (pool_tables_a(r), pool_tables_b(r)), pool_edges, None, lambda r: None)
            pool.wait_ge(r_pos, 2)
            pool.wait_ge(slots_zero, 8 * 16)
            pool.sem_inc(zs_free, 1)
            with pool.Fori(0, NG) as g:
                pool.tensor_copy(ps1[:, :], pos1[:, ds(g * GT, GT)]).then_inc(ps_cp, 1)
                pool.tensor_copy(ps2[:, :], pos2[:, ds(g * GT, GT)]).then_inc(ps_cp, 1)
                v = pool.snap(g * 2 + 2)
                pool.wait_ge(ps_cp, v)
                pool.sem_inc(settle_pool, 1)
                v = pool.snap(g + 1)
                pool.wait_ge(zs_cp, v)
                pool.sem_inc(settle_pool, 1)
                for j in range(GT):
                    for p in (ps1, ps2):
                        pool.indirect_dma_start(slot_in[:, :], bass.IndirectOffsetOnAxis(ap=p[:, j:j + 1], axis=0),
                                                hn[:, j, :], None).then_inc(sc_out, 16)
                v = pool.snap(g * (2 * GT * 16) + 2 * GT * 16)
                pool.wait_ge(sc_out, v)
                pool.sem_inc(zs_free, 1)
            for s in range(2):
                pool.wait_ge(yo_out[s], MT // 2 * 16 + 16)
            with pool.Fori(0, NG) as g:
                v = pool.snap(g + 1)
                pool.wait_ge(f_rstd, v)
                pool.sem_inc(settle_pool, 1)
                pool.tensor_copy(ps1[:, :], pos1[:, ds(g * GT, GT)]).then_inc(fp_cp, 1)
                pool.tensor_copy(ps2[:, :], pos2[:, ds(g * GT, GT)]).then_inc(fp_cp, 1)
                v = pool.snap(g * 2 + 2)
                pool.wait_ge(fp_cp, v)
                pool.sem_inc(settle_pool, 1)
                for j in range(GT):
                    for p, rows in ((ps1, es), (ps2, qe)):
                        pool.indirect_dma_start(rows[:, j, :], None, slot_out[:, :],
                                                bass.IndirectOffsetOnAxis(ap=p[:, j:j + 1], axis=0)).then_inc(fi_in, 16)

        @block.scalar
        def _(act):
            act.sem_inc(ring_act, 1)
            act.sem_inc(at_c, 1)
            act.sem_inc(xcopied, GT)
            act.wait_ge(wT_T, 1)
            act.activation(W1T[:, :, :].rearrange("p k d -> p (k d)"), bank[6][:, :], ACT.Copy).then_inc(wT_cp, 1)
            for i in range(2):
                act.wait_ge(wT_T, 2 + i)
                act.activation(W2T[:, 2 * i:2 * i + 2, :].rearrange("p k d -> p (k d)"), bank[7 if i == 0 else 5][:, :], ACT.Copy).then_inc(wT_cp, 1)

            def std(to, var, s):
                act.activation(to, var, ACT.Sqrt, bias=epsc[0:T, :]).then_inc(s, 1)

            def features(u, loc, j, gain, shift):
                act.wait_ge(ring_full, u + 1)
                for k in range(KD):
                    ins = act.activation(TT[:, k, j * T:(j + 1) * T], RING[loc % 3][:, 128 * k:128 * k + T], ACT.Identity,
                                         bias=shift(k), scale=gain(k))
                ins.then_inc(ring_act, 1)

            def copy_tile(u, loc, to, w, parts=128):
                act.wait_ge(ring_full, u + 1)
                act.activation(to, RING[loc % 3][0:parts, 0:256].rearrange("p (k n) -> p k n", k=KD)[:, :, 0:w], ACT.Copy).then_inc(ring_act, 1)

            act.wait_ge(consts, 16)
            with act.Fori(0, NG) as g:
                act.wait_ge(paggr, g * GT + GT)
                std(std5[:, :], mv5[:, :, 1], pstd)
                for j in range(GT):
                    act.wait_ge(hn_done, g * GT + j + 1)
                    act.sem_inc(settle_act, 1)
                    act.activation(tile(X, g * GT + j), hn[:, j, :], ACT.Copy).then_inc(xcopied, 1)
                    copy_tile(g * GT + j, j, TT[:, :, j * T:(j + 1) * T], T)
            act.wait_ge(ws_done, 49)
            act.activation(Wst[:, :], bank[5][:, :].bitcast(bf16), ACT.Copy).then_inc(wT_cp, 1)
            act_tables(0)
            act.wait_ge(par_in, (4 * L + L) * 16)
            act.wait_ge(at_T, 2)
            act_attr(0, 0)
            for e in range(EG_FIRST):
                for half in range(2):
                    act_edges(e, e, half)

            with act.Fori(0, L) as l:
                act.wait_ge(ring_act, l * RING_L + (RING_A + 1))
                act.sem_inc(settle_act, 1)
                act.activation(lnc[:, :], lnp[:, ds(l * 8, 8)], ACT.Copy).then_inc(lnc_done, 1)
                act.activation(b1c[:, :], b1_s[:, ds(l * NF, NF)], ACT.Copy).then_inc(lnc_done, 1)
                act.wait_ge(lnc_done, l * 2 + 2)
                act.sem_inc(settle_act, 1)

                def ln_col(w, k):
                    return lnc[:, 2 * w + k:2 * w + k + 1]
                with act.Fori(0, NG) as g:
                    e = l * EG_L + g + EG_FIRST
                    n0, u0, q0 = l * NT + g * GT, l * RING_L + g * RING_GA + RING_A, l * (2 * NG) + g * 2
                    act.wait_ge(a_aggr, n0 + GT)
                    std(std5[:, :], mv5[:, :, 1], a_std)
                    act_edges(e, e, 0)
                    for j in range(GT):
                        features(u0 + j, j, j, lambda k: ln_col(0, k), lambda k: ln_col(1, k))
                    for pc, (a, b) in enumerate(PC):
                        act.wait_ge(cd_done, q0 + pc + 1)
                        act.activation(corr[:, pc, :], cdiff[:, pc, :], ACT.Exp).then_inc(corr_done, 1)
                        for h in range(KD):
                            act.activation(eT[:, h, a * T:b * T], RING[(GT + 2 * pc + h) % 3][:, 0:(b - a) * T], ACT.Exp,
                                           bias=nb[:, pc, h:h + 1], scale=SCALE).then_inc(ring_act, 1)
                        if pc == 0:
                            act_edges(e, e, 1)
                    for j in range(GT):
                        copy_tile(u0 + GT + 4 + j, GT + 4 + j, es[:, j, :].rearrange("p (k n) -> p k n", k=KD), 128, T)
                copy_tile(l * RING_L + (RING_A + NG * RING_GA), 0, ctxT[:, :, :], 128)
                with act.Fori(0, NG) as g:
                    n0, u0 = l * NT + g * GT, l * RING_L + g * RING_GB + (RING_A + NG * RING_GA + 1)
                    r0 = l * ROW_L + g * ROW_GB + (ROW_A + NG * ROW_GA + KD)
                    eg = lambda i: l * EG_L + g * 4 + (EG_FIRST + NG + i // 2)
                    edges = lambda i: act_edges(eg(i), eg(i), i % 2)
                    edges(0)
                    for j in range(GT):
                        features(u0 + j, j, j, lambda k: ln_col(0, k), lambda k: ln_col(1, k))
                    edges(1)
                    for j in range(GT):
                        act.wait_ge(row_dve, r0 + j + 2)
                        act.activation(qe[:, j, :], qe[:, j, :], ACT.Exp, scale=SCALE).then_inc(q_exp, 1)
                    edges(2)
                    for j in range(GT):
                        copy_tile(u0 + GT + j, GT + j, QT[:, :, j * T:(j + 1) * T], T)
                    edges(3)
                    act.wait_ge(b_aggr, n0 + GT)
                    std(std5b[:, :], mv5b[:, :, 1], b_std)
                    edges(4)
                    for j in range(GT):
                        features(u0 + 2 * GT + j, 2 * GT + j, j, lambda k: ln_col(2, k), lambda k: ln_col(3, k))
                    edges(5)
                    for f in range(NF):
                        for pc, (a, b) in enumerate(PC):
                            loc = 3 * GT + 2 * f + pc
                            act.wait_ge(ring_full, u0 + loc + 1)
                            act.activation(hid[:, f, a * T:b * T], RING[loc % 3][:, 0:(b - a) * T], ACT.Gelu,
                                           bias=b1c[:, f:f + 1]).then_inc(ring_act, 1)
                        if f == NF // 2 - 1:
                            edges(6)
                    edges(7)
            for half in range(2):
                act_edges(NEG - 1, NEG - 1, half, attr=False)

            def act_first(r):
                act_attr(0, r * NEG)
                for half in range(2):
                    act_edges(0, r * NEG, half)

            def act_middle(e, ge):
                for half in range(2):
                    act_edges(e, ge, half)

            def act_last(r):
                for half in range(2):
                    act_edges(NEG - 1, r * NEG + (NEG - 1), half, attr=False)
            more_rounds(act, act_tables, act_first, act_middle, act_last)

            with act.Fori(0, NG) as g:
                pt0 = g * (3 * GT) + RING_C
                for j in range(GT):
                    copy_tile(pt0 + 2 * j, 2 * j, TT[:, :, j * T:(j + 1) * T], T)
                    copy_tile(pt0 + 2 * j + 1, 2 * j + 1, QT[:, :, j * T:(j + 1) * T], T)
                for j in range(GT):
                    act.wait_ge(row_dve, g * (2 * GT) + j + (ROW_C + 2))
                    act.activation(sqj[:, j, :], HL[:, j, :], ACT.Square, accum_out=ss[:, j:j + 1]).then_inc(c_ss, 1)
                act.wait_ge(c_ss, g * GT + GT)
                act.activation(nrm[:, :], ss[:, :], ACT.Sqrt).then_inc(c_nrm, 1)
                act.wait_ge(c_aggr, g * GT + GT)
                std(std5[:, :], mv5[:, :, 1], c_std)
                for j in range(GT):
                    act.wait_ge(hn_done, g * GT + (HN_C + j + 1))
                    copy_tile(pt0 + 2 * GT + j, 2 * GT + j, TT[:, :, j * T:(j + 1) * T], T)
                act.activation(tile(agg, g * GT, GT), hn[:, :, :].rearrange("p j d -> p (j d)"), ACT.Copy).then_inc(c_zcp, 1)
            act.wait_ge(r_mask, 1)
            act.activation(e21[:, :], e21[:, :], ACT.Exp).then_inc(r_exp, 1)
            act.wait_ge(c_zcp, NG)
            with act.Fori(0, NG) as g:
                act.wait_ge(zs_free, g + 1)
                act.sem_inc(settle_act, 1)
                act.activation(hn[:, :, :].rearrange("p j d -> p (j d)"), tile(agg, g * GT, GT), ACT.Copy).then_inc(zs_cp, 1)

            def slots_T(m, s, loc):
                copy_tile(m * 2 + RING_E, loc, xT[s][:, :, :], SL)

            def hidden(m, s, loc):
                act.wait_ge(ring_full, m * 2 + (RING_E + 2))
                for c in range(NFE):
                    ins = act.activation(hT[s][:, c, :], RING[loc % 3][:, c * SL:(c + 1) * SL], ACT.Relu, bias=b1e[s][:, c:c + 1])
                ins.then_inc(ring_act, 1)
            slots_T(0, 0, 0)
            hidden(0, 0, 1)
            slots_T(1, 1, 2)
            with act.Fori(0, MT // 2 - 1) as i:
                hidden(i * 2 + 1, 1, 0)
                slots_T(i * 2 + 2, 0, 1)
                hidden(i * 2 + 2, 0, 2)
                slots_T(i * 2 + 3, 1, 3)
            hidden(MT - 1, 1, 0)
            with act.Fori(0, NG) as g:
                act.wait_ge(f_aggr, g * GT + GT)
                std(std5b[:, :], mv5b[:, :, 1], f_std)

        @block.tensor
        def _(pe):
            pe.sem_inc(s_done, 5)
            pe.sem_inc(at_T, 1)
            pe.sem_inc(cn_done, 1)
            pe.wait_ge(consts, 16)
            pe.wait_ge(gw_in, 48)
            for k in range(KD):
                for h in range(KD):
                    ins = pe.transpose(bank[6][:, 256 * k + 128 * h:256 * k + 128 * h + 128], gW1[:, h, 128 * k:128 * k + 128], ident[:, :])
            ins.then_inc(wT_T, 1)
            for i in range(2):
                for k in range(2):
                    for h in range(KD):
                        ins = pe.transpose(bank[7 if i == 0 else 5][:, 256 * k + 128 * h:256 * k + 128 * h + 128],
                                           gW2[:, h, 128 * (2 * i + k):128 * (2 * i + k) + 128], ident[:, :])
                ins.then_inc(wT_T, 1)
            pe.wait_ge(bc_ready, 1)
            flat = spread.rearrange("p c q -> p (c q)")
            for i in range(4):
                pe.matmul(bank[1 + i][0:PQ, 0:4 * EP], ones[0:EP, 0:PQ], flat[:, 4 * EP * i:4 * EP * (i + 1)], start=True, stop=True).then_inc(bc_ready, 1)

            def slot(u, loc):
                if loc == 0:
                    pe.wait_ge(ring_act, u + 1)
                elif loc >= 3:
                    pe.wait_ge(ring_act, u - 1)
                return RING[loc % 3]

            def row_slot(u, loc):
                pe.wait_ge(row_dve, u + 1 if loc == 0 else u)
                return ROW[loc % 2]

            def tile_T(u, loc, rows, parts=T):
                to = slot(u, loc)
                for k in range(KD):
                    ins = pe.transpose(to[:, 128 * k:128 * k + parts], rows[:, 128 * k:128 * k + 128], ident[0:parts, 0:parts])
                ins.then_inc(ring_full, 1)

            def row(u, loc, products, cols=D, parts=T):
                to = row_slot(u, loc)
                for i, (a, b) in enumerate(products):
                    ins = pe.matmul(to[0:parts, 0:cols], a, b, start=i == 0, stop=i == len(products) - 1)
                ins.then_inc(row_full, 1)

            pe.wait_ge(wT_cp, 3)
            with pe.Fori(0, NG) as g:
                for j in range(GT):
                    pe.wait_ge(hn_done, g * GT + j + 1)
                    tile_T(g * GT + j, j, hn[:, j, :])
                for j in range(GT):
                    pe.wait_ge(ring_act, g * GT + j + 2)
                    row(g * GT + j, j, [(TT[:, k, j * T:(j + 1) * T], W1T[:, k, :]) for k in range(KD)])
            pe.wait_ge(ws_done, 48)
            pe.wait_ge(row_dve, NT + 1)
            for q in range(4):
                for h in range(KD):
                    ins = pe.transpose(bank[5][:, :].bitcast(bf16)[:, q * D + 128 * h:q * D + 128 * h + 128], WS[:, h, q, :], identb[:, :])
            ins.then_inc(ws_done, 1)
            pe_tables(0)
            pe.wait_ge(wT_cp, 4)
            pe_attr(0, 0)
            for e in range(EG_FIRST):
                for half in range(2):
                    pe_edges(e, e, half, first=e == 0 and half == 0, second=e == 0 and half == 1)
            pe.wait_ge(brow_out, 16 + 2 * L * 16)

            with pe.Fori(0, L) as l:
                pe.wait_ge(wA_in, l * 32 + 32)
                pe.sem_inc(settle_pe, 1)
                with pe.Fori(0, NG) as g:
                    e = l * EG_L + g + EG_FIRST
                    h0, q0 = l * HN_L + g * GT + NT, l * (2 * NG) + g * 2
                    u0, r0 = l * RING_L + g * RING_GA + RING_A, l * ROW_L + g * ROW_GA + ROW_A
                    pe_edges(e, e, 0)
                    for j in range(GT):
                        pe.wait_ge(hn_done, h0 + j + 1)
                        tile_T(u0 + j, j, hn[:, j, :])
                    for pc, (a, b) in enumerate(PC):
                        for j in range(a, b):
                            pe.wait_ge(ring_act, u0 + j + 2)
                            row(r0 + j, j, [(TT[:, k, j * T:(j + 1) * T], Wv_s[:, k, :]) for k in range(KD)])
                        for h in range(KD):
                            loc = GT + 2 * pc + h
                            to = slot(u0 + loc, loc)
                            for k in range(KD):
                                ins = pe.matmul(to[:, 0:(b - a) * T], Wk_s[:, k, 128 * h:128 * h + 128], TT[:, k, a * T:b * T],
                                                start=k == 0, stop=k == KD - 1)
                            ins.then_inc(ring_full, 1)
                        if pc == 0:
                            pe_edges(e, e, 1)
                    for pc, (a, b) in enumerate(PC):
                        for j in range(a, b):
                            loc = GT + 4 + j
                            pe.wait_ge(ring_act, u0 + (GT + 2 * pc + 3))
                            to = slot(u0 + loc, loc)
                            for h in range(KD):
                                ins = pe.transpose(to[0:T, 128 * h:128 * h + 128], eT[:, h, j * T:(j + 1) * T], ident[:, :])
                            ins.then_inc(ring_full, 1)
                    for pc, (a, b) in enumerate(PC):
                        to = row_slot(r0 + GT + pc, GT + pc)
                        for h in range(KD):
                            for j in range(a, b):
                                if h == 0:
                                    pe.wait_ge(ring_act, u0 + (GT + 4 + j + 2))
                                    pe.wait_ge(row_dve, r0 + j + 2)
                                ins = pe.matmul(to[:, 129 * h:129 * h + 129], es[:, j, 128 * h:128 * h + 128], V5[:, j, h, :],
                                                start=j == a, stop=j == b - 1)
                        ins.then_inc(row_full, 1)
                pe.wait_ge(cn_done, l + 2)
                u0, r0 = l * RING_L + (RING_A + NG * RING_GA), l * ROW_L + (ROW_A + NG * ROW_GA)
                to = slot(u0, 0)
                for h in range(KD):
                    ins = pe.transpose(to[:, 128 * h:128 * h + 128], ctxN[:, h, :], ident[:, :])
                ins.then_inc(ring_full, 1)
                pe.wait_ge(wQ_in, l * 32 + 32)
                pe.wait_ge(ring_act, u0 + 2)
                for h in range(KD):
                    row(r0 + h, h, [(ctxT[:, h, :], Wo_s[:, h, :])], parts=128)
                pe.wait_ge(wF_in, l * 32 + 32)
                pe.sem_inc(settle_pe, 1)
                with pe.Fori(0, NG) as g:
                    n0, h0 = l * NT + g * GT, l * HN_L + g * (2 * GT) + 2 * NT
                    u0 = l * RING_L + g * RING_GB + (RING_A + NG * RING_GA + 1)
                    r0 = l * ROW_L + g * ROW_GB + (ROW_A + NG * ROW_GA + KD)
                    eg = lambda i: l * EG_L + g * 4 + (EG_FIRST + NG + i // 2)
                    edges = lambda i: pe_edges(eg(i), eg(i), i % 2)
                    bias_row = lambda w: (onesb[:, 0:T], brow[:, ds(l * (2 * D) + w * D, D)])
                    edges(0)
                    for j in range(GT):
                        pe.wait_ge(hn_done, h0 + j + 1)
                        tile_T(u0 + j, j, hn[:, j, :])
                    edges(1)
                    for j in range(GT):
                        pe.wait_ge(ring_act, u0 + j + 2)
                        row(r0 + j, j, [(TT[:, k, j * T:(j + 1) * T], Wq_s[:, k, :]) for k in range(KD)])
                    edges(2)
                    for j in range(GT):
                        pe.wait_ge(q_norm, n0 + j + 1)
                        tile_T(u0 + GT + j, GT + j, qe[:, j, :])
                    edges(3)
                    for j in range(GT):
                        pe.wait_ge(ring_act, u0 + GT + j + 2)
                        row(r0 + GT + j, GT + j, [(QT[:, k, j * T:(j + 1) * T], M_s[:, k, :]) for k in range(KD)] + [bias_row(0)])
                    edges(4)
                    for j in range(GT):
                        pe.wait_ge(hn_done, h0 + GT + j + 1)
                        tile_T(u0 + 2 * GT + j, 2 * GT + j, hn[:, j, :])
                    edges(5)
                    pe.wait_ge(ring_act, u0 + 3 * GT + 1)
                    for f in range(NF):
                        for pc, (a, b) in enumerate(PC):
                            loc = 3 * GT + 2 * f + pc
                            to = slot(u0 + loc, loc)
                            for k in range(KD):
                                ins = pe.matmul(to[:, 0:(b - a) * T], W1_s[:, k, 128 * f:128 * f + 128], TT[:, k, a * T:b * T],
                                                start=k == 0, stop=k == KD - 1)
                            ins.then_inc(ring_full, 1)
                        if f == NF // 2 - 1:
                            edges(6)
                    edges(7)
                    pe.wait_ge(ring_act, u0 + RING_GB + 1)
                    for j in range(GT):
                        row(r0 + 2 * GT + j, 2 * GT + j, [(hid[:, f, j * T:(j + 1) * T], W2_s[:, f, :]) for f in range(NF)] + [bias_row(1)])
            pe_edges(NEG - 1, NEG - 1, 0)
            pe_edges(NEG - 1, NEG - 1, 1, attr=False)
            pe_sums(NEG - 1, NEG - 1, 1, last=True)

            def pe_first(r):
                pe_attr(0, r * NEG)
                pe_edges(0, r * NEG, 0, first=True)
                pe_edges(0, r * NEG, 1, second=True)

            def pe_middle(e, ge):
                pe_edges(e, ge, 0)
                pe_edges(e, ge, 1)

            def pe_last(r):
                ge = r * NEG + (NEG - 1)
                pe_edges(NEG - 1, ge, 0)
                pe_edges(NEG - 1, ge, 1, attr=False)
                pe_sums(NEG - 1, ge, 1, last=True)
            more_rounds(pe, pe_tables, pe_first, pe_middle, pe_last)

            pe.wait_ge(late_in, 64)
            with pe.Fori(0, NG) as g:
                pt0, r0 = g * (3 * GT) + RING_C, g * (2 * GT) + ROW_C
                pe.wait_ge(c_in, g * 32 + 32)
                pe.wait_ge(c_agg, g + 1)
                for j in range(GT):
                    tile_T(pt0 + 2 * j, 2 * j, es[:, j, :])
                    tile_T(pt0 + 2 * j + 1, 2 * j + 1, hn[:, j, :])
                for j in range(GT):
                    pe.wait_ge(ring_act, pt0 + 2 * j + 3)
                    row(r0 + j, j, [(TT[:, k, j * T:(j + 1) * T], W2T[:, k, :]) for k in range(KD)]
                        + [(QT[:, k, j * T:(j + 1) * T], W2T[:, KD + k, :]) for k in range(KD)])
                for j in range(GT):
                    pe.wait_ge(hn_done, g * GT + (HN_C + j + 1))
                    tile_T(pt0 + 2 * GT + j, 2 * GT + j, hn[:, j, :])
                for j in range(GT):
                    pe.wait_ge(ring_act, pt0 + 2 * GT + j + 2)
                    row(r0 + GT + j, GT + j, [(TT[:, k, j * T:(j + 1) * T], gw_s[:, k, :]) for k in range(KD)], cols=NE)
            pe.wait_ge(r_mask, 2)
            flat = mask.rearrange("p t e -> p (t e)")
            pe.matmul(RING[0][0:T, 0:NT * NE], tri[:, :], flat, start=True, stop=True).then_inc(r_rank, 1)
            pe.matmul(RING[1][0:T, 0:NT * NE], ones[0:T, 0:T], flat, start=True, stop=True).then_inc(r_rank, 1)

            def slots_T(m, mi, s, loc):
                pe.wait_ge(xs_in[s], mi * 16 + 16)
                tile_T(m * 2 + RING_E, loc, xs[s][:, :], parts=128)

            def up(m, mi, s, loc):
                pe.wait_ge(w1_in[s], mi * 32 + 32)
                pe.wait_ge(ring_act, m * 2 + (RING_E + 2))
                to = slot(m * 2 + (RING_E + 1), loc)
                for c in range(NFE):
                    for k in range(KD):
                        ins = pe.matmul(to[:, c * SL:(c + 1) * SL], W1e[s][:, k, c::NFE], xT[s][:, k, :], start=k == 0, stop=k == KD - 1)
                ins.then_inc(ring_full, 1)

            def down(m, mi, s):
                pe.wait_ge(w2_in[s], mi * 32 + 32)
                pe.wait_ge(ring_act, m * 2 + (RING_E + 3))
                row(m + ROW_E, s, [(hT[s][:, c, :], W2e[s][:, c, :]) for c in range(NFE)], parts=128)
            pe.wait_ge(r_pos, 1)
            slots_T(0, 0, 0, 0)
            up(0, 0, 0, 1)
            slots_T(1, 0, 1, 2)
            with pe.Fori(0, MT // 2 - 1) as i:
                up(i * 2 + 1, i, 1, 0)
                slots_T(i * 2 + 2, i + 1, 0, 1)
                down(i * 2, i, 0)
                up(i * 2 + 2, i + 1, 0, 2)
                slots_T(i * 2 + 3, i + 1, 1, 3)
                down(i * 2 + 1, i, 1)
            up(MT - 1, MT // 2 - 1, 1, 0)
            down(MT - 2, MT // 2 - 1, 0)
            down(MT - 1, MT // 2 - 1, 1)

        @block.vector
        def _(dve):
            dve.sem_inc(z_done, 4)
            dve.sem_inc(acc_done, 5)
            dve.sem_inc(row_dve, 1)
            dve.sem_inc(f_rstd, 1)
            dve.sem_inc(out_done, 16)
            for i in range(2):
                dve.sem_inc(yo_out[i], 16)
            for j in range(GT):
                dve.sem_inc(p_out[j], 16)
            chain = [0]

            def link(ins):
                chain[0] += 1
                ins.then_inc(base_step, 1)
                dve.wait_ge(base_step, chain[0])

            dve.wait_ge(consts, 16)
            dve.wait_ge(dst_in, 16)
            dt = dst_tiles.rearrange("p (c e) -> p c e", e=ET)
            dve.tensor_reduce(hl[:, 0:EC], dt, AX.X, ALU.max)
            link(dve.tensor_reduce(hl[:, EC:2 * EC], dt, AX.X, ALU.min))
            link(dve.tensor_tensor(above, hl[:, :].unsqueeze(2).to_broadcast([EP, 2 * EC, NT - 1]),
                                   thr[:, :].unsqueeze(1).to_broadcast([EP, 2 * EC, NT - 1]), ALU.is_ge))
            link(dve.tensor_reduce(hlb[:, :], above, AX.X, ALU.add))
            link(dve.scalar_tensor_tensor(hlb[:, 0:EC], hlb[:, 0:EC], 1.0, hlb[:, EC:2 * EC], ALU.add, ALU.subtract))
            dve.tensor_tensor(spread, ident[0:EP, 0:EP].unsqueeze(1).to_broadcast([EP, 2 * EC, EP]),
                              hlb[:, :].unsqueeze(2).to_broadcast([EP, 2 * EC, EP]), ALU.mult).then_inc(bc_ready, 1)
            dve.wait_ge(gw_in, 48)
            dve.tensor_copy(w4[:, :, 0:EA], gW1[:, :, D:D + EA]).then_inc(wparts_done, 1)
            dve.wait_ge(wparts_done, 1)
            dve.tensor_copy(wparts[:, 0, :, :], w4[:, :, :]).then_inc(wparts_done, 1)
            dve.wait_ge(wparts_done, 2)
            dve.tensor_tensor(w4r[:, :, :], w4[:, :, :], wparts[:, 0, :, :], ALU.subtract).then_inc(wparts_done, 1)
            dve.wait_ge(wparts_done, 3)
            dve.tensor_copy(wparts[:, 1, :, :], w4r[:, :, :]).then_inc(wparts_done, 1)
            dve.wait_ge(wparts_done, 4)
            dve.tensor_tensor(wparts[:, 2, :, :], w4r[:, :, :], wparts[:, 1, :, :], ALU.subtract).then_inc(wparts_done, 1)
            dve.wait_ge(br_in, 32)
            dve.tensor_copy(bparts[:, 0, :], browf[:, :]).then_inc(brp_done, 1)
            dve.wait_ge(brp_done, 1)
            dve.tensor_tensor(browr[:, :], browf[:, :], bparts[:, 0, :], ALU.subtract).then_inc(brp_done, 1)
            dve.wait_ge(brp_done, 2)
            dve.tensor_copy(bparts[:, 1, :], browr[:, :]).then_inc(brp_done, 1)
            dve.wait_ge(brp_done, 3)
            dve.tensor_tensor(bparts[:, 2, :], browr[:, :], bparts[:, 1, :], ALU.subtract).then_inc(brp_done, 1)
            for i in range(4):
                dve.wait_ge(bc_ready, i + 2)
                to = (n_bc, lo_bc)[i // 2][:, 4 * EP * (i % 2):4 * EP * (i % 2 + 1)]
                ins = dve.tensor_copy(to, bank[1 + i][0:PQ, 0:4 * EP])
            link(ins)
            dve.tensor_copy(lo0[:, :], lo_bc[:, 0:1])
            link(dve.tensor_tensor_scan(cum[:, :], n_bc, n_bc, 0.0, ALU.add, ALU.max))
            dve.tensor_scalar(rjunk[:, :], thr2[:, :], cum[0:1, NET - 1:NET], None, ALU.is_lt, ALU.add, accum_out=rcnt[:, :])
            link(dve.tensor_tensor(junk, n_bc, cum[:, :], ALU.subtract))
            dve.tensor_copy(rounds_i[:, :], rcnt[:, :]).then_inc(rounds_done, 1)
            link(dve.tensor_tensor(junk, junk, lo_bc, ALU.add))
            dve.memset(dg[:, NET - 1:NET], 0.0)
            link(dve.tensor_tensor(dg[:, 0:NET - 1], junk[:, 1:NET], junk[:, 0:NET - 1], ALU.subtract))
            dve_tables_a(0)

            def stats(rows, s_stat, s_aggr, n, st, mv):
                dve.sem_inc(settle_dve, 1)
                for j in range(GT):
                    dve.bn_stats(st[:, j, :], rows(j)).then_inc(s_stat, 1)
                for j in range(GT):
                    dve.wait_ge(s_stat, n + j + 1)
                    dve.sem_inc(settle_dve, 1)
                    dve.bn_aggr(mv[:, j, :], st[:, j, :]).then_inc(s_aggr, 1)

            for g in range(NG):
                dve.wait_ge(x_in[g], 16)
            with dve.Fori(0, NG) as g:
                stats(lambda j: tile(X, g * GT + j), pstat, paggr, g * GT, st5, mv5)
                dve.wait_ge(pstd, g + 1)
                dve.reciprocal(rs5b[:, :], std5[:, :]).then_inc(prstd, 1)
                dve.wait_ge(prstd, g + 1)
                for j in range(GT):
                    dve.wait_ge(xcopied, g * GT + j + 1)
                    dve.tensor_scalar(hn[:, j, :], tile(X, g * GT + j), mv5[:, j, 0:1], rs5b[:, j:j + 1],
                                      ALU.subtract, ALU.mult).then_inc(hn_done, 1)
                for j in range(GT):
                    dve.wait_ge(row_full, g * GT + j + 1)
                    dve.wait_ge(p_out[j], g * 16 + 16)
                    dve.tensor_copy(es[:, j, :], ROW[j % 2][0:T, 0:D]).then_inc(row_dve, 1)
            dve_tables_b(0)
            dve.wait_ge(t_cp, 6)
            for e in range(EG_FIRST):
                for half in range(2):
                    dve_edges(e, e, half, first=e == 0 and half == 0)
            dve.wait_ge(xcopied, NT + GT)
            dve.wait_ge(xn_out, 16)

            with dve.Fori(0, L) as l:
                dve.memset(ctxS[:, :, :], 0.0).then_inc(l_init, 1)
                dve.memset(mO[:, :], LOW).then_inc(l_init, 1)
                with dve.Fori(0, NG) as g:
                    e = l * EG_L + g + EG_FIRST
                    n0, h0, lg = l * NT + g * GT, l * HN_L + g * GT + NT, l * NG + g
                    u0, r0, q0 = l * RING_L + g * RING_GA + RING_A, l * ROW_L + g * ROW_GA + ROW_A, l * (2 * NG) + g * 2
                    dve.wait_ge(row_dve, l * ROW_L + ROW_A + 1)
                    stats(lambda j: tile(X, g * GT + j), a_stat, a_aggr, n0, st5, mv5)
                    dve.wait_ge(a_aggr, n0 + GT)
                    dve.tensor_copy(mean_t[:, ds(g * GT, GT)], mv5[:, :, 0])
                    dve.wait_ge(a_std, lg + 1)
                    dve.reciprocal(rstd_t[:, ds(g * GT, GT)], std5[:, :]).then_inc(a_rstd, 1)
                    dve.wait_ge(a_rstd, lg + 1)
                    for j in range(GT):
                        dve.tensor_scalar(hn[:, j, :], tile(X, g * GT + j), mean_t[:, ds(g * GT + j, 1)], rstd_t[:, ds(g * GT + j, 1)],
                                          ALU.subtract, ALU.mult).then_inc(hn_done, 1)
                    dve_edges(e, e, 0)
                    dve.wait_ge(l_init, l * 2 + 2)
                    for pc, (a, b) in enumerate(PC):
                        for j in range(a, b):
                            dve.wait_ge(row_full, r0 + j + 1)
                            dve.tensor_copy(V5[:, j, :, 0:128], ROW[j % 2][0:T, 0:D].rearrange("p (k n) -> p k n", k=KD)).then_inc(row_dve, 1)
                        for h in range(KD):
                            loc = GT + 2 * pc + h
                            dve.wait_ge(ring_full, u0 + loc + 1)
                            dve.reduce_max(pm[:, h:h + 1], RING[loc % 3][:, 0:(b - a) * T], axis=AX.X).then_inc(k_max, 1)
                        dve.wait_ge(k_max, q0 * 2 + 2 * pc + 2)
                        if pc:
                            dve.wait_ge(m_cp, q0 + pc)
                        dve.tensor_tensor(mN[:, :], mO[:, :], pm[:, :], ALU.max).then_inc(m_new, 1)
                        dve.wait_ge(m_new, q0 + pc + 1)
                        dve.tensor_scalar(nb[:, pc, :], mN[:, :], -SCALE, None, ALU.mult).then_inc(nb_done, 1)
                        dve.wait_ge(nb_done, q0 + pc + 1)
                        dve.scalar_tensor_tensor(cdiff[:, pc, :], mO[:, :], SCALE, nb[:, pc, :], ALU.mult, ALU.add).then_inc(cd_done, 1)
                        dve.wait_ge(cd_done, q0 + pc + 1)
                        dve.tensor_copy(mO[:, :], mN[:, :]).then_inc(m_cp, 1)
                        if pc == 0:
                            dve_edges(e, e, 1)
                    for pc in range(2):
                        dve.wait_ge(corr_done, q0 + pc + 1)
                        dve.wait_ge(row_full, r0 + (GT + pc + 1))
                        dve.wait_ge(row_dve, r0 + (GT + pc + 1))
                        for h in range(KD):
                            ins = dve.scalar_tensor_tensor(ctxS[:, h, :], ctxS[:, h, :], corr[:, pc, h:h + 1],
                                                           ROW[(GT + pc) % 2][:, 129 * h:129 * h + 129], ALU.mult, ALU.add)
                        ins.then_inc(row_dve, 1)
                dve.wait_ge(row_dve, l * ROW_L + (ROW_A + NG * ROW_GA + 1))
                dve.reciprocal(rk[:, :], ctxS[:, :, 128]).then_inc(rk_done, 1)
                dve.tensor_tensor(ctxN[:, :, :], ctxS[:, :, 0:128], headmask[:, :].unsqueeze(1).to_broadcast([128, KD, 128]),
                                  ALU.mult).then_inc(cn_done, 1)
                dve.wait_ge(rk_done, l + 1)
                for h in range(KD):
                    dve.wait_ge(row_full, l * ROW_L + (ROW_A + NG * ROW_GA + h + 1))
                    dve.tensor_scalar(M_s[:, h, :], ROW[h][:, 0:D], rk[:, h:h + 1], None, ALU.mult).then_inc(row_dve, 1)
                with dve.Fori(0, NG) as g:
                    n0, lg = l * NT + g * GT, l * NG + g
                    r0 = l * ROW_L + g * ROW_GB + (ROW_A + NG * ROW_GA + KD)
                    eg = lambda i: l * EG_L + g * 4 + (EG_FIRST + NG + i // 2)
                    edges = lambda i: dve_edges(eg(i), eg(i), i % 2)
                    heads = lambda ap: ap.rearrange("p (h d) -> p h d", d=DH)
                    per_head = lambda ap: ap.unsqueeze(2).to_broadcast([T, H, DH])
                    for j in range(GT):
                        dve.tensor_scalar(hn[:, j, :], tile(X, g * GT + j), mean_t[:, ds(g * GT + j, 1)], rstd_t[:, ds(g * GT + j, 1)],
                                          ALU.subtract, ALU.mult).then_inc(hn_done, 1)
                    edges(0)
                    edges(1)
                    for j in range(GT):
                        q_ps = heads(ROW[j % 2][0:T, 0:D])
                        dve.wait_ge(row_full, r0 + j + 1)
                        dve.reduce_max(qm[:, j, :], q_ps, axis=AX.X).then_inc(q_max, 1)
                        dve.wait_ge(q_max, n0 + j + 1)
                        dve.tensor_tensor(heads(qe[:, j, :]), q_ps, per_head(qm[:, j, :]), ALU.subtract).then_inc(row_dve, 1)
                    edges(2)
                    for j in range(GT):
                        dve.wait_ge(q_exp, n0 + j + 1)
                        dve.reduce_sum(qs[:, j, :], heads(qe[:, j, :]), axis=AX.X).then_inc(q_sum, 1)
                    for j in range(GT):
                        dve.wait_ge(q_sum, n0 + j + 1)
                        dve.reciprocal(qr[:, j, :], qs[:, j, :]).then_inc(q_rec, 1)
                    for j in range(GT):
                        dve.wait_ge(q_rec, n0 + j + 1)
                        dve.tensor_tensor(heads(qe[:, j, :]), heads(qe[:, j, :]), per_head(qr[:, j, :]), ALU.mult).then_inc(q_norm, 1)
                    edges(3)
                    for j in range(GT):
                        dve.wait_ge(row_full, r0 + GT + j + 1)
                        dve.tensor_tensor(tile(X, g * GT + j), ROW[(GT + j) % 2][0:T, 0:D], tile(X, g * GT + j), ALU.add).then_inc(row_dve, 1)
                    dve.wait_ge(row_dve, r0 + 2 * GT + 1)
                    stats(lambda j: tile(X, g * GT + j), b_stat, b_aggr, n0, st5b, mv5b)
                    dve.wait_ge(b_std, lg + 1)
                    dve.reciprocal(rs5b[:, :], std5b[:, :]).then_inc(b_rstd, 1)
                    dve.wait_ge(b_rstd, lg + 1)
                    dve.wait_ge(b_aggr, n0 + GT)
                    for j in range(GT):
                        dve.tensor_scalar(hn[:, j, :], tile(X, g * GT + j), mv5b[:, j, 0:1], rs5b[:, j:j + 1],
                                          ALU.subtract, ALU.mult).then_inc(hn_done, 1)
                    edges(4)
                    edges(5)
                    edges(6)
                    edges(7)
                    for j in range(GT):
                        dve.wait_ge(row_full, r0 + 2 * GT + j + 1)
                        dve.tensor_tensor(tile(X, g * GT + j), ROW[(2 * GT + j) % 2][0:T, 0:D], tile(X, g * GT + j), ALU.add).then_inc(row_dve, 1)

            def last_group(ge):
                for half in range(2):
                    dve_edges(NEG - 1, ge, half)
                regs = blocks_of(NEG - 1, 1)
                for i in range(4):
                    dve_acc(NEG - 1, ge, 1, i, regs[i])
            last_group(NEG - 1)

            def dve_first(r):
                dve_edges(0, r * NEG, 0, first=True)
                dve_edges(0, r * NEG, 1)

            def dve_middle(e, ge):
                for half in range(2):
                    dve_edges(e, ge, half)

            def tables(r):
                dve_tables_a(r)
                dve_tables_b(r)
                dve.wait_ge(t_cp, r * 6 + 6)
            more_rounds(dve, tables, dve_first, dve_middle, lambda r: last_group(r * NEG + (NEG - 1)))

            dve.wait_ge(late_in, 64)
            with dve.Fori(0, NG) as g:
                r0 = g * (2 * GT) + ROW_C
                dve.tensor_copy(hn[:, :, :].rearrange("p j d -> p (j d)"), tile(agg, g * GT, GT)).then_inc(c_agg, 1)
                for j in range(GT):
                    dve.wait_ge(row_full, r0 + j + 1)
                    dve.tensor_scalar(HL[:, j, :], ROW[j % 2][0:T, 0:D], 0.0, None, ALU.max).then_inc(row_dve, 1)
                dve.wait_ge(c_nrm, g + 1)
                dve.tensor_scalar(nrm[:, :], nrm[:, :], 1e-12, None, ALU.max).then_inc(c_rn, 1)
                dve.wait_ge(c_rn, g * 2 + 1)
                dve.reciprocal(rn[:, :], nrm[:, :]).then_inc(c_rn, 1)
                dve.wait_ge(c_rn, g * 2 + 2)
                dve.wait_ge(c_in, g * 32 + 32)
                for j in range(GT):
                    dve.scalar_tensor_tensor(HL[:, j, :], HL[:, j, :], rn[:, j:j + 1], qe[:, j, :], ALU.mult, ALU.add).then_inc(c_y, 1)
                for j in range(GT):
                    dve.wait_ge(c_y, g * (2 * GT) + j + 1)
                    dve.tensor_tensor(tile(X, g * GT + j), HL[:, j, :], tile(X, g * GT + j), ALU.add).then_inc(c_y, 1)
                dve.wait_ge(c_y, g * (2 * GT) + 2 * GT)
                stats(lambda j: tile(X, g * GT + j), c_stat, c_aggr, g * GT, st5, mv5)
                dve.wait_ge(c_std, g + 1)
                dve.reciprocal(rs5b[:, :], std5[:, :]).then_inc(c_rstd, 1)
                dve.wait_ge(c_rstd, g + 1)
                for j in range(GT):
                    dve.tensor_scalar(hn[:, j, :], tile(X, g * GT + j), mv5[:, j, 0:1], rs5b[:, j:j + 1],
                                      ALU.subtract, ALU.mult).then_inc(hn_done, 1)
                for j in range(GT):
                    dve.wait_ge(row_full, r0 + GT + j + 1)
                    dve.tensor_tensor(LG[:, ds((g * GT + j) * NE, NE)], ROW[(GT + j) % 2][0:T, 0:NE], gb_s[:, :], ALU.add).then_inc(row_dve, 1)
                dve.wait_ge(c_zcp, g + 1)
            steps = [0]

            def then(ins):
                steps[0] += 1
                ins.then_inc(r_step, 1)
                dve.wait_ge(r_step, steps[0])

            dve.wait_ge(row_dve, ROW_E + 1)
            lg = LG[:, :].rearrange("p (t e) -> p t e", e=NE)
            per_tile = lambda ap: ap.unsqueeze(2).to_broadcast([T, NT, NE])
            per_expert = lambda ap: ap.unsqueeze(1).to_broadcast([T, NT, NE])
            flat = lambda ap: ap.rearrange("p t e -> p (t e)")
            for logits, most, sel in ((lg, m1, sel1), (lg2, m2, sel2)):
                then(dve.reduce_max(most[:, :], logits, axis=AX.X))
                then(dve.tensor_tensor(sel, logits, per_tile(most[:, :]), ALU.is_equal))
                then(dve.tensor_tensor(rtmp, sel, per_expert(iota_e[:, :]), ALU.mult))
                then(dve.tensor_reduce(i1[:, :], rtmp, AX.X, ALU.min))
                then(dve.tensor_tensor(sel, per_expert(iota_e[:, :]), per_tile(i1[:, :]), ALU.is_equal))
                if sel is sel1:
                    then(dve.scalar_tensor_tensor(flat(lg2), flat(sel1), LOW, LG[:, :], ALU.mult, ALU.add))
            dve.tensor_tensor(e21[:, :], m2[:, :], m1[:, :], ALU.subtract).then_inc(r_mask, 1)
            dve.tensor_tensor(mask, sel1, sel2, ALU.add).then_inc(r_mask, 1)
            dve.wait_ge(r_exp, 1)
            then(dve.tensor_scalar(w1t[:, :], e21[:, :], 1.0, None, ALU.add))
            then(dve.reciprocal(w1t[:, :], w1t[:, :]))
            then(dve.tensor_tensor(w2t[:, :], w1t[:, :], e21[:, :], ALU.mult))
            dve.wait_ge(r_rank, 2)
            tiles3 = lambda b: b[0:T, 0:NT * NE].rearrange("p (t e) -> p t e", e=NE)
            then(dve.tensor_copy(tot, tiles3(RING[1])))
            for x_ in range(NE):
                ins = dve.tensor_tensor_scan(cumt[:, :, x_], onee[:, :], tot[:, :, x_], 0.0, ALU.mult, ALU.add)
            then(ins)
            then(dve.tensor_tensor(nge, cumt[:, NT - 1, :].unsqueeze(2).to_broadcast([T, NE, NT]),
                                   thr3[:, :].unsqueeze(1).to_broadcast([T, NE, NT]), ALU.is_gt))
            then(dve.tensor_reduce(te[:, :], nge, AX.X, ALU.add))
            then(dve.tensor_tensor_scan(ce[:, :], onee[:, 0:NE], te[:, :], 0.0, ALU.mult, ALU.add))
            then(dve.tensor_tensor(ste[:, :], ce[:, :], te[:, :], ALU.subtract))
            then(dve.tensor_scalar(ste[:, :], ste[:, :], float(SL), None, ALU.mult))
            then(dve.tensor_tensor(slotp, tiles3(RING[0]), cumt, ALU.add))
            then(dve.tensor_tensor(slotp, slotp, tot, ALU.subtract))
            then(dve.tensor_tensor(slotp, slotp, per_expert(ste[:, :]), ALU.add))
            for sel, posf, pos in ((sel1, pos1f, pos1), (sel2, pos2f, pos2)):
                then(dve.tensor_tensor(rtmp, sel, slotp, ALU.mult))
                then(dve.tensor_reduce(posf[:, :], rtmp, AX.X, ALU.add))
                dve.tensor_copy(pos[:, :], posf[:, :]).then_inc(r_pos, 1)
            then(dve.tensor_tensor(ejc, ce[0:1, :].unsqueeze(1).to_broadcast([1, MT, NE]),
                                   jt[0:1, :].unsqueeze(2).to_broadcast([1, MT, NE]), ALU.is_le))
            then(dve.tensor_reduce(ejf[:, :], ejc, AX.X, ALU.add))
            dve.tensor_scalar(ej_row[:, :], ejf[:, :], float(NE - 1), None, ALU.min).then_inc(r_pos, 1)

            with dve.Fori(0, MT // 2) as i:
                for s in range(2):
                    dve.wait_ge(row_full, i * 2 + (s + ROW_E + 1))
                    dve.wait_ge(w2_in[s], i * 32 + 32)
                    dve.wait_ge(yo_out[s], i * 16 + 16)
                    dve.tensor_tensor(yo[s][:, :], ROW[s][:, 0:D], b2e[s][:, :], ALU.add).then_inc(row_dve, 1)
            with dve.Fori(0, NG) as g:
                dve.wait_ge(fi_in, g * (2 * GT * 16) + 2 * GT * 16)
                dve.wait_ge(out_done, g * (GT * 16) + 16)
                for j in range(GT):
                    dve.scalar_tensor_tensor(u5[:, j, :], es[:, j, :], w1t[:, ds(g * GT + j, 1)], tile(agg, g * GT + j), ALU.mult, ALU.add).then_inc(f_u, 1)
                for j in range(GT):
                    dve.wait_ge(f_u, g * (2 * GT) + j + 1)
                    dve.scalar_tensor_tensor(u5[:, j, :], qe[:, j, :], w2t[:, ds(g * GT + j, 1)], u5[:, j, :], ALU.mult, ALU.add).then_inc(f_u, 1)
                dve.wait_ge(f_u, g * (2 * GT) + 2 * GT)
                stats(lambda j: u5[:, j, :], f_stat, f_aggr, g * GT, st5b, mv5b)
                dve.wait_ge(f_std, g + 1)
                dve.reciprocal(rs5b[:, :], std5b[:, :]).then_inc(f_rstd, 1)
                dve.wait_ge(f_rstd, g + 2)
                dve.wait_ge(f_aggr, g * GT + GT)
                for j in range(GT):
                    dve.tensor_scalar(u5[:, j, :], u5[:, j, :], mv5b[:, j, 0:1], rs5b[:, j:j + 1], ALU.subtract, ALU.mult).then_inc(f_n, 1)
                    dve.wait_ge(f_n, g * (4 * GT) + 4 * j + 1)
                    dve.tensor_tensor(u5[:, j, :], u5[:, j, :], gam_s[:, :], ALU.mult).then_inc(f_n, 1)
                    dve.wait_ge(f_n, g * (4 * GT) + 4 * j + 2)
                    dve.tensor_tensor(u5[:, j, :], u5[:, j, :], bet_s[:, :], ALU.add).then_inc(f_n, 1)
                    dve.wait_ge(f_n, g * (4 * GT) + 4 * j + 3)
                    dve.tensor_tensor(u5[:, j, :], u5[:, j, :], tile(X, g * GT + j), ALU.add).then_inc(f_n, 1)


def kernel(**inputs):
    import numpy as np
    import concourse.bacc as bacc
    from concourse.bass_utils import run_bass_kernel_spmd
    nc = bacc.Bacc("TRN2", target_bir_lowering=False, num_devices=1)
    arrays, args = {}, []
    for name in INPUTS:
        a = np.ascontiguousarray(inputs[name])
        arrays[f"in_{name}"] = a
        args.append(nc.dram_tensor(f"in_{name}", a.shape, mybir.dt.from_np(a.dtype), kind="ExternalInput").ap())
    out = nc.dram_tensor("out_0", inputs["x"].shape, mybir.dt.float32, kind="ExternalOutput").ap()
    build(nc, *args, out)
    result = run_bass_kernel_spmd(nc, [arrays], core_ids=[0])
    return result.results[0]["out_0"]
```

```python
import concourse.bass as bass
from concourse import mybir
from contextlib import ExitStack

INPUTS = ['x', 'src', 'dst', 'edge_attr_3', 'L0_gnn_W1', 'L0_gnn_b1', 'L0_gnn_W2',
          'L0_mix_Wq', 'L0_mix_Wk', 'L0_mix_Wv', 'L0_mix_Wo', 'L0_mix_bo', 'L0_mix_ln1_g', 'L0_mix_ln1_b',
          'L0_mix_W1', 'L0_mix_b1', 'L0_mix_W2', 'L0_mix_b2', 'L0_mix_ln2_g', 'L0_mix_ln2_b',
          'L0_ffn_gate_w', 'L0_ffn_gate_b', 'L0_ffn_w1', 'L0_ffn_b1', 'L0_ffn_w2', 'L0_ffn_b2',
          'L0_ffn_gamma', 'L0_ffn_beta']


def build(nc, x, src, dst, edge_attr, gnn_W1, gnn_b1, gnn_W2,
          Wq, Wk, Wv, Wo, bo, ln1_g, ln1_b, W1, b1, W2, b2, ln2_g, ln2_b,
          gate_w, gate_b, ew1, eb1, ew2, eb2, gamma, beta, out):
    f32, f32r, bf16, i32 = mybir.dt.float32, mybir.dt.float32r, mybir.dt.bfloat16, mybir.dt.int32
    ALU, ACT, AX = mybir.AluOpType, mybir.ActivationFunctionType, mybir.AxisListType
    ds = bass.ds

    N, D = x.shape
    T = 125
    NT = N // T
    GT = 5
    NG = NT // GT
    KD = D // 128
    L = Wq.shape[0]
    H, DH = 8, D // 8
    FF = W1.shape[2]
    NF = FF // 128
    SCALE = DH ** -0.25
    EPS = 1e-5
    LOW = -3.0e38
    PC = ((0, 3), (3, 5))
    E = src.shape[0]
    ET = 125
    ST = 4
    SE = ST * ET
    NS = E // SE
    EP = 100
    EC = NS // EP
    NPAIR = NS + NT - 1
    PG = 2
    NEG = NPAIR // PG
    PQ = NPAIR // EC
    AC = EC * ST
    ROUNDS = -(-NS * NT // NPAIR)
    EA = 3
    NE, F = ew1.shape[0], ew1.shape[2]
    NFE = F // 128
    SL = 128
    MT = (2 * N + NE * (SL - 1)) // SL
    assert N == T * NT and E == SE * NS and NPAIR == PG * NEG == PQ * EC and MT % 4 == 0

    def dram(name, shape, dt):
        return nc.dram_tensor(name, shape, dt, kind="Internal").ap()
    xn_d = dram("xn_d", (N, D), f32)
    P_d = dram("P_d", (N, D), f32)
    attr_d = dram("attr_d", (NPAIR, ST, 32, ET), bf16)
    brow_d = dram("brow_d", (2 * L, 3, D), bf16)
    slot_in = dram("slot_in", (MT * SL, D), f32)
    slot_out = dram("slot_out", (MT * SL, D), f32)

    with ExitStack() as ctx:
        def sb(name, shape, dt=f32):
            return ctx.enter_context(nc.sbuf_tensor(name, shape, dt))

        def pb(name, shape, dt=f32):
            return ctx.enter_context(nc.psum_tensor(name, shape, dt))

        def sem(name):
            return ctx.enter_context(nc.semaphore(name))

        X = sb("X", [T, NT * D])
        agg = sb("agg", [T, NT * D])
        ident = sb("ident", [128, 128])
        identb = sb("identb", [128, 128], bf16)
        ones = sb("ones", [128, 128])
        onesb = sb("onesb", [128, 128], bf16)
        iota_n = sb("iota_n", [128, T])
        headmask = sb("headmask", [128, 128])
        epsc = sb("epsc", [128, 1])
        Wkv_s = [sb(f"W{n}_s", [128, KD, D]) for n in "qkvo"]
        Wq_s, Wk_s, Wv_s, Wo_s = Wkv_s
        W1_s = sb("W1_s", [128, KD, FF])
        W2_s = sb("W2_s", [128, NF, D])
        lnp = sb("lnp", [128, L * 8])
        b1_s = sb("b1_s", [128, L * NF])
        lnc = sb("lnc", [128, 8])
        b1c = sb("b1c", [128, NF])
        brow = sb("brow", [128, L * 2 * D], bf16)
        W1T = sb("W1T", [128, KD, D])
        W2T = sb("W2T", [128, 2 * KD, D])
        Wst = sb("Wst", [128, 4 * D], bf16)
        hn = sb("hn", [T, GT, D])
        es = sb("es", [T, GT, D])
        qe = sb("qe", [T, GT, D])
        TT = sb("TT", [128, KD, GT * T])
        QT = sb("QT", [128, KD, GT * T])
        V5 = sb("V5", [T, GT, KD, 129])
        eT = sb("eT", [128, KD, GT * T])
        hid = sb("hid", [128, NF, GT * T])
        M_s = sb("M_s", [128, KD, D])
        st5 = sb("st5", [T, GT, 6])
        mv5 = sb("mv5", [T, GT, 2])
        std5 = sb("std5", [T, GT])
        mvA = sb("mvA", [T, NT, 2])
        stdA = sb("stdA", [T, NT])
        rstd_t = sb("rstd_t", [T, NT])
        st5b = sb("st5b", [T, GT, 6])
        mv5b = sb("mv5b", [T, GT, 2])
        std5b = sb("std5b", [T, GT])
        rs5b = sb("rs5b", [T, GT])
        ctxS = sb("ctxS", [128, KD, 129])
        ctxN = sb("ctxN", [128, KD, 128])
        ctxT = sb("ctxT", [128, KD, 128])
        mO = sb("mO", [128, KD])
        mN = sb("mN", [128, KD])
        pm = sb("pm", [128, KD])
        nb = sb("nb", [128, 2, KD])
        cdiff = sb("cdiff", [128, 2, KD])
        corr = sb("corr", [128, 2, KD])
        rk = sb("rk", [128, KD])
        qm = sb("qm", [T, GT, H])
        qs = sb("qs", [T, GT, H])
        qr = sb("qr", [T, GT, H])
        src_T = sb("src_T", [ET, NPAIR * ST], i32)
        dst_T = sb("dst_T", [ET, NPAIR * ST])
        blk_row = sb("blk_row", [1, NPAIR], i32)
        stage = [sb(f"stage{i}", [ET, PG * ST], i32) for i in range(2)]
        G = sb("G", [ET, PG * ST, D])
        z = sb("z", [ET, 2, 2 * D])
        zr = sb("zr", [ET, PG, 2, 2 * D], f32r)
        zl = sb("zl", [ET, 2, 2 * D], f32r)
        onehot = sb("onehot", [ET, PG, ST, T], f32r)
        aT = sb("aT", [128, PG, ET], bf16)
        cum = sb("cum", [PQ, NS])
        dg = sb("dg", [PQ, NS])
        lo0 = sb("lo0", [PQ, 1])
        pid = sb("pid", [PQ, EC])
        tile_f = sb("tile_f", [PQ, EC])
        tile_i = sb("tile_i", [PQ, EC], i32)
        gsum = sb("gsum", [PQ, EC])
        blk = sb("blk", [PQ, EC])
        blk125 = sb("blk125", [PQ, EC])
        blkc = sb("blkc", [PQ, EC])
        rounds_i = sb("rounds_i", [1, 1], i32)

        bank = [pb(f"bank{i}", [128, 512]) for i in range(8)]
        edge_bank, sum_bank = (bank[1], bank[2]), bank[3]
        RING = [bank[4], bank[6], bank[7]]
        ROW = [bank[5], bank[0]]

        SC = hid[:, :, :].rearrange("p f n -> p (f n)")
        LG = sb("LG", [T, NT * NE])
        V5x = eT[:, :, :].rearrange("p k n -> p (k n)")
        dst_tiles = eT[0:EP, :, :].rearrange("p k n -> p (k n)")[:, 0:EC * SE].bitcast(i32)
        n_bc, lo_bc, junk = SC[0:PQ, 0:NS], SC[0:PQ, NS:2 * NS], SC[0:PQ, 2 * NS:3 * NS]
        spread = SC[0:EP, 3 * NS:3 * NS + 2 * EC * EP].rearrange("p (c q) -> p c q", q=EP)
        above = SC[0:EP, 4000:4000 + 2 * EC * (NT - 1)].rearrange("p (c b) -> p c b", b=NT - 1)
        src_rows = SC[0:PQ, 0:EC * SE]
        dst_rows = SC[0:PQ, EC * SE:2 * EC * SE]
        attr_rows = SC[0:PQ, 2 * EC * SE:5 * EC * SE]
        spread_b = V5x[0:PQ, 0:EC * PQ].rearrange("p (c q) -> p c q", q=PQ)
        ATS = [G[0:PQ, 3 * i:3 * i + 3, :].rearrange("p j d -> p (j d)").bitcast(bf16)[:, 0:9 * ET].rearrange("p (r e) -> p r e", e=ET)
               for i in range(2)]
        AR = [qe[0:PQ, 2 * i:2 * i + 2, :].rearrange("p j d -> p (j d)")[:, 0:EA * ET].rearrange("p (a e) -> p a e", e=ET)
              for i in range(2)]
        arest = M_s[0:PQ, :, :].rearrange("p k d -> p (k d)").bitcast(bf16)[:, 0:5 * ET].rearrange("p (r e) -> p r e", e=ET)
        thr = sb("thr", [EP, NT - 1])
        thr2 = sb("thr2", [1, ROUNDS])
        hl = sb("hl", [EP, 2 * EC])
        hlb = sb("hlb", [EP, 2 * EC])
        rcnt = sb("rcnt", [1, 1])
        rjunk = sb("rjunk", [1, ROUNDS])
        gW1 = W1_s[:, :, 0:D + EA]
        gW2 = W2_s[:, 0:4, :].rearrange("p (k a) d -> p k (a d)", k=KD)
        w4 = sb("w4", [128, KD, 4])
        w4r = sb("w4r", [128, KD, 4])
        wparts = sb("wparts", [128, 3, KD, 4], bf16)
        WS = QT[:, :, :].rearrange("p k n -> p (k n)").bitcast(bf16)[:, 0:KD * 512].rearrange("p (h q r) -> p h q r", h=KD, q=4)
        bparts = sb("bparts", [2 * L, 3, D], bf16)
        HL = SC[0:T, 0:GT * D].rearrange("p (j d) -> p j d", d=D)
        sqj = SC[0:T, GT * D:2 * GT * D].rearrange("p (j d) -> p j d", d=D)
        ss = sb("ss", [T, GT])
        nrm = sb("nrm", [T, GT])
        rn = sb("rn", [T, GT])
        gw_s = sb("gw_s", [128, KD, NE])
        gb_s = sb("gb_s", [T, NE])
        gam_s = sb("gam_s", [T, D])
        bet_s = sb("bet_s", [T, D])
        iota_e = sb("iota_e", [T, NE])
        tri = sb("tri", [T, T])
        m1 = sb("m1", [T, NT])
        m2 = sb("m2", [T, NT])
        i1 = sb("i1", [T, NT])
        w1t = sb("w1t", [T, NT])
        w2t = sb("w2t", [T, NT])
        e21 = sb("e21", [T, NT])
        ts3 = lambda k: SC[0:T, 400 * k:400 * k + 400].rearrange("p (t e) -> p t e", e=NE)
        sel1, sel2, rtmp, lg2, mask, tot, cumt, slotp = (ts3(k) for k in range(8))
        nge = SC[0:T, 3200:3200 + NE * NT].rearrange("p (e k) -> p e k", k=NT)
        thr3 = sb("thr3", [T, NT])
        jt = sb("jt", [T, MT])
        ejc = SC[0:1, 3720:3720 + MT * NE].rearrange("p (m e) -> p m e", e=NE)
        te = sb("te", [T, NE])
        ce = sb("ce", [T, NE])
        ste = sb("ste", [T, NE])
        onee = sb("onee", [T, NT])
        ejf = sb("ejf", [1, MT])
        ej_row = sb("ej_row", [1, MT], i32)
        pos1f = sb("pos1f", [T, NT])
        pos2f = sb("pos2f", [T, NT])
        pos1 = sb("pos1", [T, NT], i32)
        pos2 = sb("pos2", [T, NT], i32)
        ps1 = sb("ps1", [T, GT], i32)
        ps2 = sb("ps2", [T, GT], i32)
        XB = 4
        W1e = [W1_s[:, :, F * i:F * i + F] for i in range(2)] + [
            SC[:, KD * F * i:KD * F * (i + 1)].rearrange("p (k f) -> p k f", f=F) for i in range(2)]
        W2e = [W2_s[:, NFE * i:NFE * i + NFE, :] for i in range(2)] + [
            SC[:, 2 * KD * F + NFE * D * i:2 * KD * F + NFE * D * (i + 1)].rearrange("p (c d) -> p c d", d=D) for i in range(2)]
        b1e = [sb(f"b1e{i}", [128, NFE]) for i in range(XB)]
        b2e = [sb(f"b2e{i}", [128, D])[:, :] for i in range(2)] + [eT[:, i, 0:D] for i in range(2)]
        xs = [sb(f"xs{i}", [128, D])[:, :] for i in range(2)] + [TT[:, i, 0:D] for i in range(2)]
        xT = [sb(f"xT{i}", [128, KD, SL]) for i in range(2)]
        hT = [QT[:, i, 0:NFE * SL].rearrange("p (c n) -> p c n", n=SL) for i in range(2)]
        yo = [sb(f"yo{i}", [128, D]) for i in range(2)]
        u5 = SC[0:T, 0:GT * D].rearrange("p (j d) -> p j d", d=D)
        zerob = yo[0]
        browf, browr = (xT[i][0:2 * L, :, :].rearrange("p k n -> p (k n)") for i in range(2))

        x_in = [sem(f"x_in{i}") for i in range(NG)]
        gw_in, par_in, dst_in, br_in, late_in = sem("gw_in"), sem("par_in"), sem("dst_in"), sem("br_in"), sem("late_in")
        consts, cdep, wparts_done, ws_done, wT_T, wT_cp = (sem(n) for n in ("consts", "cdep", "wparts_done", "ws_done", "wT_T", "wT_cp"))
        brp_done, brow_out, brow_z = sem("brp_done"), sem("brow_out"), sem("brow_z")
        pid_done, r_mask = sem("pid_done"), sem("r_mask")
        pstat, paggr, pstd, prstd, xcopied = (sem(n) for n in ("pstat", "paggr", "pstd", "prstd", "xcopied"))
        p_out = [sem(f"p_out{i}") for i in range(GT)]
        xn_out, arest_out, slots_zero = sem("xn_out"), sem("arest_out"), sem("slots_zero")
        zmade = sem("zmade")
        base_step, bc_ready, bc_cp = sem("base_step"), sem("bc_ready"), sem("bc_cp")
        t_step, t_idx, rows_in, t_cast, t_T, t_cp, a_split, rounds_done = (sem(n) for n in (
            "t_step", "t_idx", "rows_in", "t_cast", "t_T", "t_cp", "a_split", "rounds_done"))
        a_out = [sem(f"a_out{i}") for i in range(2)]
        st_ready, e_done, z_done, r_done, lo_done, oh_done, s_done, acc_done = (sem(n) for n in (
            "st_ready", "e_done", "z_done", "r_done", "lo_done", "oh_done", "s_done", "acc_done"))
        g_in = [sem(f"g_in{i}") for i in range(PG * ST)]
        at_in = [sem(f"at_in{i}") for i in range(PG)]
        settle_pool, settle_dve, settle_act, settle_pe = (sem(f"settle_{n}") for n in ("pool", "dve", "act", "pe"))
        lnc_done = sem("lnc_done")
        ring_full, ring_act, row_full, row_dve = (sem(n) for n in ("ring_full", "ring_act", "row_full", "row_dve"))
        hn_done = sem("hn_done")
        wA_in, wQ_in, wF_in = sem("wA_in"), sem("wQ_in"), sem("wF_in")
        a_stat, a_aggr, a_mv, a_std, a_rstd = (sem(n) for n in ("a_stat", "a_aggr", "a_mv", "a_std", "a_rstd"))
        b_stat, b_aggr, b_std, b_rstd = (sem(n) for n in ("b_stat", "b_aggr", "b_std", "b_rstd"))
        l_init, k_max, m_new, nb_done, cd_done, m_cp, corr_done = (sem(n) for n in (
            "l_init", "k_max", "m_new", "nb_done", "cd_done", "m_cp", "corr_done"))
        cn_done, rk_done = sem("cn_done"), sem("rk_done")
        q_max, q_exp, q_sum, q_rec, q_norm = (sem(n) for n in ("q_max", "q_exp", "q_sum", "q_rec", "q_norm"))
        c_in, c_agg, c_ss, c_nrm, c_rn, c_y, c_stat, c_aggr, c_std, c_rstd, c_zcp = (sem(n) for n in (
            "c_in", "c_agg", "c_ss", "c_nrm", "c_rn", "c_y", "c_stat", "c_aggr", "c_std", "c_rstd", "c_zcp"))
        r_step, r_exp, r_rank, r_pos, r_thr = (sem(n) for n in ("r_step", "r_exp", "r_rank", "r_pos", "r_thr"))
        zs_cp, zs_free, ps_cp, sc_out = sem("zs_cp"), sem("zs_free"), sem("ps_cp"), sem("sc_out")
        xs_in, w1_in, w2_in = ([sem(f"{n}_in{i}") for i in range(XB)] for n in ("xs", "w1", "w2"))
        yo_out = [sem(f"yo_out{i}") for i in range(2)]
        fi_in, f_u, f_stat, f_aggr, f_std, f_rstd, f_n, out_done, fp_cp = (sem(n) for n in (
            "fi_in", "f_u", "f_stat", "f_aggr", "f_std", "f_rstd", "f_n", "out_done", "fp_cp"))

        def tile(buf, t, n=1):
            return buf[:, ds(t * D, n * D)]

        RING_GA, RING_GB = 2 * GT + 4, 3 * GT + 2 * NF
        ROW_GA, ROW_GB = GT + 2, 3 * GT
        RING_A, RING_L = NT, NG * RING_GA + 1 + NG * RING_GB
        ROW_A, ROW_L = NT, NG * ROW_GA + KD + NG * ROW_GB
        RING_C, ROW_C = RING_A + L * RING_L, ROW_A + L * ROW_L
        RING_E, ROW_E = RING_C + 3 * NT, ROW_C + 2 * NT
        HN_L = 3 * NT
        HN_C = NT + L * HN_L
        EG_FIRST = 2
        EG_A, EG_M = 1, 1 + NG
        EG_B = EG_M + 1
        RING_M, ROW_M = GT + NG * RING_GA, NG * ROW_GA
        RING_B, ROW_B = RING_M + 1, ROW_M + GT + KD
        EG_L = EG_B + 4 * NG
        EG_LAST = EG_FIRST + L * EG_L


        def pe_sums(ge, s):
            nc.tensor.wait_ge(oh_done, ge + 1)
            nc.tensor.wait_ge(acc_done, ge + 1)
            for i in range(ST):
                cols = slice(D * (i % 2), D * (i % 2) + D)
                if i % 2 == 0:
                    nc.tensor.wait_ge(lo_done, ge * 2 + (i // 2 + 3))
                nc.tensor.matmul(sum_bank[0:T, 0:D], onehot[:, s, i, :], zr[:, s, i // 2, cols], start=i == 0, stop=False)
                ins = nc.tensor.matmul(sum_bank[0:T, 0:D], onehot[:, s, i, :], zl[:, i // 2, cols], start=False, stop=i == ST - 1)
            ins.then_inc(s_done, 1)

        def pe_edges(ge, group, s, first=False):
            nc.tensor.wait_ge(at_in[s], group * 16 + 16)
            for k in range(2):
                nc.tensor.wait_ge(z_done, ge * 2 + (k + 3))
                nc.tensor.matmul(edge_bank[k][0:ET, :], aT[:, s, :], Wst[:, 2 * k * D:2 * (k + 1) * D],
                                 start=True, stop=True).then_inc(e_done, 1)
            if not first:
                pe_sums(ge - 1, 1 - s)

        def act_edges(ge, s):
            for k in range(2):
                nc.scalar.wait_ge(z_done, ge * 2 + (k + 5))
                nc.scalar.activation(zr[:, s, k, :], z[:, k, :], ACT.Relu).then_inc(r_done, 1)

        def dve_low(ge, s):
            for k in range(2):
                nc.vector.wait_ge(r_done, ge * 2 + (k + 1))
                nc.vector.scalar_tensor_tensor(zl[:, k, :], z[:, k, :], 0.0, zr[:, s, k, :].bitcast(f32), ALU.max, ALU.subtract).then_inc(lo_done, 1)

        def dve_acc(ge, reg):
            nc.vector.wait_ge(s_done, ge + 3)
            nc.vector.wait_ge(acc_done, ge + 1)
            part = agg[:, ds(reg * D, D)]
            nc.vector.tensor_tensor(part, sum_bank[0:T, 0:D], part, ALU.add).then_inc(acc_done, 1)

        def block_of(e):
            return nc.vector.value_load(blk_row[0:1, ds(e, 1)], min_val=0, max_val=NT - 1)

        def dve_onehot(e, ge, s):
            nc.vector.wait_ge(s_done, ge + 1)
            nc.vector.tensor_tensor(onehot[:, s, :, :], iota_n[0:ET, :].unsqueeze(1).to_broadcast([ET, ST, T]),
                                    dst_T[:, ds(e * ST, ST)].unsqueeze(2).to_broadcast([ET, ST, T]),
                                    ALU.is_equal).then_inc(oh_done, 1)

        def dve_edges(e, ge, group, s, first=False, last=False):
            reg = None if first else block_of(e - 1)
            if first:
                dve_onehot(e, ge, s)
            nc.vector.wait_ge(lo_done, ge * 2 + 2)
            for k in range(2):
                nc.vector.wait_ge(e_done, ge * 2 + (k + 1))
                for j in (ST * s + 2 * k, ST * s + 2 * k + 1):
                    nc.vector.wait_ge(g_in[j], group * 16 + 16)
                nc.vector.tensor_tensor(z[:, k, :], edge_bank[k][0:ET, :],
                                        G[:, ST * s + 2 * k:ST * s + 2 * k + 2, :].rearrange("p j d -> p (j d)"),
                                        ALU.add).then_inc(z_done, 1)
            if not first:
                dve_acc(ge - 1, reg)
            dve_low(ge, s)
            if not last:
                dve_onehot(e + 1, ge + 1, 1 - s)

        def pool_edges(r):
            def group(e, ge, s):
                nc.gpsimd.tensor_copy(stage[s][:, :], src_T[:, ds(e * (PG * ST), PG * ST)]).then_inc(st_ready, 1)
                v = nc.gpsimd.snap(ge + 1)
                nc.gpsimd.wait_ge(st_ready, v)
                nc.gpsimd.sem_inc(settle_pool, 1)
                for j in range(PG * ST):
                    if j % 2 == 0:
                        v = nc.gpsimd.snap(ge * (2 * PG) + (j // 2 + 1))
                        nc.gpsimd.wait_ge(z_done, v)
                        nc.gpsimd.sem_inc(settle_pool, 1)
                    nc.gpsimd.indirect_dma_start(G[:, j, :], None, P_d[:, :],
                                                 bass.IndirectOffsetOnAxis(ap=stage[s][:, j:j + 1], axis=0)).then_inc(g_in[j], 16)
            for i in range(2):
                nc.gpsimd.wait_ge(a_out[i], r * (AC // 2 * 48) + AC // 2 * 48 if isinstance(r, int)
                                  else nc.gpsimd.snap(r * (AC // 2 * 48) + AC // 2 * 48))
                nc.gpsimd.sem_inc(settle_pool, 1)
            with nc.gpsimd.Fori(0, NEG // 2) as i:
                for s in range(2):
                    group(i * 2 + s, i * 2 + s + r * NEG, s)

        def sp_attr(ge, e, s, first=False):
            if not first:
                nc.sync.wait_ge(e_done, ge * 2 - 2)
            nc.sync.dma_start(aT[:, s, :], attr_flat[ds(e * 128, 128), :]).then_inc(at_in[s], 16)

        attr_flat = attr_d.rearrange("q i r e -> (q i r) e")


        def dve_tables_a(r):
            ts = [0]

            def step(ins):
                ts[0] += 1
                ins.then_inc(t_step, 1)
                nc.vector.wait_ge(t_step, r * (2 * EC + 2) + ts[0])

            if not isinstance(r, int):
                nc.vector.tensor_scalar(pid[:, :], pid[:, :], float(NPAIR), None, ALU.add).then_inc(pid_done, 1)
                nc.vector.wait_ge(pid_done, r)
            for c in range(EC):
                step(nc.vector.tensor_scalar(junk, cum[:, :], pid[:, c:c + 1], None, ALU.is_le, ALU.add, accum_out=tile_f[:, c:c + 1]))
                step(nc.vector.scalar_tensor_tensor(junk, cum[:, :], pid[:, c:c + 1], dg[:, :], ALU.is_le, ALU.mult,
                                                    accum_out=gsum[:, c:c + 1]))
            nc.vector.tensor_scalar(tile_i[:, :], tile_f[:, :], float(NS - 1), None, ALU.min).then_inc(t_idx, 1)
            step(nc.vector.scalar_tensor_tensor(blk[:, :], gsum[:, :], lo0[:, :], pid[:, :], ALU.add, ALU.add))
            nc.vector.tensor_scalar(blk125[:, :], blk[:, :], float(T), None, ALU.mult)
            step(nc.vector.tensor_scalar(blkc[:, :], blk[:, :], float(NT - 1), None, ALU.min))
            nc.vector.tensor_tensor(spread_b, ident[0:PQ, 0:PQ].unsqueeze(1).to_broadcast([PQ, EC, PQ]),
                                    blkc[:, :].unsqueeze(2).to_broadcast([PQ, EC, PQ]), ALU.mult).then_inc(t_cast, 1)

        def dve_tables_b(r):
            nc.vector.wait_ge(rows_in, r * (3 * EC * 16) + 3 * EC * 16)
            nc.vector.tensor_copy(src_rows, src_rows.bitcast(i32)).then_inc(t_cast, 1)
            nc.vector.tensor_tensor(dst_rows.rearrange("p (c e) -> p c e", e=SE),
                                    dst_rows.bitcast(i32).rearrange("p (c e) -> p c e", e=SE),
                                    blk125[:, :].unsqueeze(2).to_broadcast([PQ, EC, SE]), ALU.subtract).then_inc(t_cast, 1)
            rows = attr_rows.rearrange("p (c e a) -> p c a e", e=ET, a=EA)
            for c in range(AC):
                at, ax, ar = rows[:, c], ATS[c % 2], AR[c % 2]
                if c >= 2:
                    nc.vector.wait_ge(a_out[c % 2], r * (AC // 2 * 48) + 48 * (c // 2))
                nc.vector.tensor_copy(ax[:, 0:3, :], at).then_inc(a_split, 1)
                nc.vector.wait_ge(a_split, r * (4 * AC) + 4 * c + 1)
                nc.vector.tensor_tensor(ar, at, ax[:, 0:3, :], ALU.subtract).then_inc(a_split, 1)
                nc.vector.wait_ge(a_split, r * (4 * AC) + 4 * c + 2)
                nc.vector.tensor_copy(ax[:, 3:6, :], ar).then_inc(a_split, 1)
                nc.vector.wait_ge(a_split, r * (4 * AC) + 4 * c + 3)
                nc.vector.tensor_tensor(ax[:, 6:9, :], ar, ax[:, 3:6, :], ALU.subtract).then_inc(a_split, 1)

        def pool_tables_a(r):
            v = nc.gpsimd.snap(r + 1) if not isinstance(r, int) else r + 1
            nc.gpsimd.wait_ge(t_idx, v)
            nc.gpsimd.sem_inc(settle_pool, 1)
            for c in range(EC):
                for rows, table, w in ((src_rows.bitcast(i32), src.rearrange("(t e) -> t e", e=SE), SE),
                                       (dst_rows.bitcast(i32), dst.rearrange("(t e) -> t e", e=SE), SE),
                                       (attr_rows, edge_attr.rearrange("(t e) a -> t (e a)", e=SE), SE * EA)):
                    nc.gpsimd.indirect_dma_start(rows[:, c * w:(c + 1) * w], None, table,
                                                 bass.IndirectOffsetOnAxis(ap=tile_i[:, c:c + 1], axis=0)).then_inc(rows_in, 16)
        def pe_tables(r):
            nc.tensor.wait_ge(t_cast, r * 3 + 1)
            flat = spread_b.rearrange("p c q -> p (c q)")
            nc.tensor.matmul(bank[6][0:1, 0:NPAIR], ones[0:PQ, 0:1], flat, start=True, stop=True).then_inc(t_T, 1)
            for b, rows in ((1, src_rows), (3, dst_rows)):
                nc.tensor.wait_ge(t_cast, r * 3 + 2 + b // 2)
                for c in range(AC):
                    ins = nc.tensor.transpose(bank[b + c // ST][0:ET, PQ * (c % ST):PQ * (c % ST) + PQ], rows[:, c * ET:(c + 1) * ET],
                                              ident[0:PQ, 0:PQ])
                ins.then_inc(t_T, 1)

        def act_tables(r):
            nc.scalar.wait_ge(t_T, r * 3 + 1)
            nc.scalar.activation(blk_row[0:1, :], bank[6][0:1, 0:NPAIR], ACT.Copy).then_inc(t_cp, 1)
            for n, (b, to) in enumerate(((1, src_T), (3, dst_T))):
                nc.scalar.wait_ge(t_T, r * 3 + 2 + n)
                for c in range(EC):
                    nc.scalar.activation(to[:, ST * PQ * c:ST * PQ * (c + 1)].rearrange("p (q i) -> p i q", i=ST),
                                         bank[b + c][0:ET, 0:ST * PQ].rearrange("p (i q) -> p i q", i=ST), ACT.Copy).then_inc(t_cp, 1)

        def sp_tables(r):
            by_tile = attr_d.rearrange("(c q) i r e -> c i q (r e)", q=PQ)
            for c in range(AC):
                nc.sync.wait_ge(a_split, r * (4 * AC) + 4 * c + 4)
                for i in range(3):
                    nc.sync.dma_start(by_tile[c // ST, c % ST][:, 9 * i * ET:9 * (i + 1) * ET],
                                      ATS[c % 2].rearrange("p r e -> p (r e)")).then_inc(a_out[c % 2], 16)
            for i in range(2):
                nc.sync.wait_ge(a_out[i], r * (AC // 2 * 48) + AC // 2 * 48)


        def more_rounds(eng, tables, first, middle, last):
            eng.wait_ge(rounds_done, 1)
            rounds = eng.value_load(rounds_i[0:1, 0:1], min_val=1, max_val=ROUNDS)
            with eng.If(rounds > 1):
                with eng.Fori(1, rounds) as r:
                    tables(r)
                    first(r)
                    if middle is not None:
                        with eng.Fori(1, NEG - 1) as e:
                            middle(e, r * NEG + e)
                    last(r)

        block = ctx.enter_context(nc.Block())

        @block.sync
        def _(sp):
            sp.dma_start(gW1, gnn_W1.rearrange("(h p) f -> p h f", p=128)).then_inc(gw_in, 16)
            sp.dma_start(gW2, gnn_W2.rearrange("(h p) f -> p h f", p=128)).then_inc(gw_in, 16)
            with nc.allow_non_contiguous_dma(reason="short vectors to columns"):
                sp.dma_start(w4[:, :, 3:4].squeeze(2), gnn_b1.rearrange("(h p) -> p h", p=128)).then_inc(gw_in, 16)
            sp.dma_start(dst_tiles.rearrange("p (c e) -> p c e", e=SE), dst.rearrange("(c p e) -> p c e", p=EP, e=SE)).then_inc(dst_in, 16)
            for g in range(NG):
                sp.dma_start(X[:, g * GT * D:(g + 1) * GT * D].rearrange("p (t d) -> p t d", d=D),
                             x[g * GT * T:(g + 1) * GT * T, :].rearrange("(t p) d -> p t d", p=T)).then_inc(x_in[g], 16)
            sp.dma_start(browf[0:L, :], bo).then_inc(br_in, 16)
            sp.dma_start(browf[L:2 * L, :], b2).then_inc(br_in, 16)
            lnv = lnp[:, :].rearrange("p (l w k) -> p l w k", l=L, w=4)
            with nc.allow_non_contiguous_dma(reason="short vectors to columns"):
                for w, v in enumerate((ln1_g, ln1_b, ln2_g, ln2_b)):
                    for l in range(L):
                        sp.dma_start(lnv[:, l, w, :], v[l, :].rearrange("(k p) -> p k", p=128)).then_inc(par_in, 16)
                for l in range(L):
                    sp.dma_start(b1_s[:, l * NF:(l + 1) * NF], b1[l, :].rearrange("(f p) -> p f", p=128)).then_inc(par_in, 16)
            sp.wait_ge(brp_done, 4)
            sp.dma_start(brow_d, bparts[:, :, :]).then_inc(brow_out, 16)
            sp.wait_ge(brow_out, 16)
            sp.wait_ge(brow_z, 1)
            for l in range(L):
                for w in range(2):
                    sp.dma_start(brow[0:3, (2 * l + w) * D:(2 * l + w + 1) * D], brow_d[w * L + l]).then_inc(brow_out, 16)
            sp.dma_start(gw_s[:, :, :], gate_w.rearrange("(k p) e -> p k e", p=128)).then_inc(late_in, 16)
            sp.dma_start(gb_s[:, :], gate_b.unsqueeze(0).to_broadcast([T, NE])).then_inc(late_in, 16)
            sp.dma_start(gam_s[:, :], gamma.unsqueeze(0).to_broadcast([T, D])).then_inc(late_in, 16)
            sp.dma_start(bet_s[:, :], beta.unsqueeze(0).to_broadcast([T, D])).then_inc(late_in, 16)
            with sp.Fori(0, NG) as g:
                for j in range(GT):
                    sp.wait_ge(row_dve, g * GT + j + 2)
                    sp.dma_start(P_d[ds((g * GT + j) * T, T), :], es[:, j, :]).then_inc(p_out[j], 16)
            sp.wait_ge(xcopied, NT + GT)
            sp.dma_start(xn_d.rearrange("(t p) d -> p t d", p=T), X[:, :].rearrange("p (t d) -> p t d", d=D)).then_inc(xn_out, 16)
            sp.wait_ge(zmade, 2)
            for c in range(AC):
                sp.dma_start(attr_d.rearrange("(c q) i r e -> c i q (r e)", q=PQ)[c // ST, c % ST][:, 27 * ET:32 * ET],
                             arest[:, :, :].rearrange("p r e -> p (r e)")).then_inc(arest_out, 16)
            sp_tables(0)
            sp.wait_ge(arest_out, AC * 16)
            sp.wait_ge(zmade, 3)
            for i in range(8):
                sp.dma_start(slot_in.rearrange("(a i p) d -> i p a d", i=8, p=128)[i],
                             zerob[:, :].unsqueeze(1).to_broadcast([128, MT // 8, D])).then_inc(slots_zero, 16)

            def load(dst_ap, src_ap, s):
                sp.dma_start(dst_ap, src_ap).then_inc(s, 16)

            def attr_group(group, e):
                for s in range(PG):
                    sp_attr(group * PG + s, e * PG + s, s)

            def weights_A(l):
                load(Wk_s[:, :, :], Wk[ds(l, 1)].rearrange("o (k p) d -> p (o k) d", p=128), wA_in)
                load(Wv_s[:, :, :], Wv[ds(l, 1)].rearrange("o (k p) d -> p (o k) d", p=128), wA_in)

            def weights_B(l):
                load(Wq_s[:, :, :], Wq[ds(l, 1)].rearrange("o (k p) d -> p (o k) d", p=128), wQ_in)
                load(Wo_s[:, :, :], Wo[ds(l, 1)].rearrange("o (k p) d -> p (o k) d", p=128), wQ_in)
                load(W1_s[:, :, :], W1[ds(l, 1)].rearrange("o (k p) d -> p (o k) d", p=128), wF_in)
                load(W2_s[:, :, :], W2[ds(l, 1)].rearrange("o (k p) d -> p (o k) d", p=128), wF_in)

            sp.wait_ge(wT_cp, 3)
            sp.wait_ge(wparts_done, 1)
            for e in range(PG):
                sp_attr(e, e, e, first=True)
            with sp.Fori(1, EG_FIRST) as g:
                attr_group(g, g)
            with sp.Fori(0, L) as l:
                sp.wait_ge(cn_done, l + 1)
                weights_A(l)
                sp.wait_ge(row_full, l * ROW_L + ROW_A)
                weights_B(l)
                with sp.Fori(0, EG_L) as g:
                    e = l * EG_L + g + EG_FIRST
                    attr_group(e, e)
            with sp.Fori(EG_LAST, NEG) as g:
                attr_group(g, g)
            more_rounds(sp, sp_tables, lambda r: attr_group(r * NEG, 0), lambda e, ge: attr_group(ge, e),
                        lambda r: attr_group(r * NEG + (NEG - 1), NEG - 1))
            with sp.Fori(0, NG) as g:
                sp.wait_ge(row_dve, g * (2 * GT) + ROW_C + 1)
                sp.dma_start(es[:, :, :], xn_d[ds(g * GT * T, GT * T), :].rearrange("(t p) d -> p t d", p=T)).then_inc(c_in, 16)
                sp.dma_start(qe[:, :, :], x[ds(g * GT * T, GT * T), :].rearrange("(t p) d -> p t d", p=T)).then_inc(c_in, 16)

            def store_tile(m, s):
                sp.dma_start(slot_out[ds(m * SL, SL), :], yo[s][:, :]).then_inc(yo_out[s], 16)

            def expert_tile(m, s, first=False):
                ex = sp.value_load(ej_row[0:1, ds(m, 1)], min_val=0, max_val=NE - 1)
                if not first:
                    sp.wait_ge(row_dve, m + (ROW_E + 2 - XB))
                    store_tile(m - XB, s % 2)
                load(xs[s], slot_in[ds(m * SL, SL), :], xs_in[s])
                load(W1e[s], ew1[ds(ex, 1)].rearrange("o (k p) f -> p (o k) f", p=128), w1_in[s])
                load(b1e[s][:, :], eb1[ds(ex, 1), :].rearrange("o (p c) -> p (o c)", c=NFE), w1_in[s])
                load(W2e[s], ew2[ds(ex, 1)].rearrange("o (p c) d -> p (o c) d", c=NFE), w2_in[s])
                load(b2e[s], eb2[ds(ex, 1), :].to_broadcast([128, D]), w2_in[s])
            sp.wait_ge(r_pos, 3)
            sp.wait_ge(sc_out, 2 * NT * 16)
            for s in range(XB):
                expert_tile(s, s, first=True)
            with sp.Fori(1, MT // XB) as i:
                for s in range(XB):
                    expert_tile(i * XB + s, s)
            for s in range(XB):
                sp.wait_ge(row_dve, MT + (ROW_E + 2 - XB + s))
                store_tile(MT - XB + s, s % 2)
            with sp.Fori(0, NG) as g:
                for j in range(GT):
                    sp.wait_ge(f_n, g * (4 * GT) + 4 * j + 4)
                    sp.dma_start(out[ds((g * GT + j) * T, T), :], u5[:, j, :]).then_inc(out_done, 16)
            sp.wait_ge(out_done, NT * 16 + 16)

        @block.gpsimd
        def _(pool):
            for t, v in ((ident, 0.0), (identb, 0.0), (headmask, 1.0), (tri, 1.0)):
                pool.memset(t[:, :], v).then_inc(cdep, 1)
            pool.memset(ones[:, :], 1.0).then_inc(consts, 1)
            pool.memset(onesb[:, :], 1.0).then_inc(consts, 1)
            pool.memset(epsc[:, :], EPS).then_inc(consts, 1)
            pool.memset(V5[:, :, :, 128:129], 1.0).then_inc(consts, 1)
            pool.memset(onee[:, :], 1.0).then_inc(consts, 1)
            pool.wait_ge(cdep, 4)
            for t in (ident, identb):
                pool.affine_select(out=t[:, :], in_=t[:, :], compare_op=ALU.not_equal, fill=1.0, base=0,
                                   pattern=[[-1, 128]], channel_multiplier=1).then_inc(consts, 1)
            pool.affine_select(out=tri[:, :], in_=tri[:, :], compare_op=ALU.is_gt, fill=0.0, base=0,
                               pattern=[[1, T]], channel_multiplier=-1).then_inc(consts, 1)
            hm = headmask[:, :].rearrange("p (c d) -> p c d", d=DH)
            pool.affine_select(out=hm, in_=hm, compare_op=ALU.is_ge, fill=0.0, base=0,
                               pattern=[[-DH, 128 // DH], [0, DH]], channel_multiplier=1).then_inc(cdep, 1)
            pool.wait_ge(cdep, 5)
            pool.affine_select(out=hm, in_=hm, compare_op=ALU.is_ge, fill=0.0, base=DH - 1,
                               pattern=[[DH, 128 // DH], [0, DH]], channel_multiplier=-1).then_inc(consts, 1)
            pool.iota(iota_n[:, :], [[1, T]], base=0, channel_multiplier=0, allow_small_or_imprecise_dtypes=True).then_inc(consts, 1)
            pool.iota(iota_e[:, :], [[1, NE]], base=-NE, channel_multiplier=0, allow_small_or_imprecise_dtypes=True).then_inc(consts, 1)
            pool.iota(thr[:, :], [[T, NT - 1]], base=T, channel_multiplier=0, allow_small_or_imprecise_dtypes=True).then_inc(consts, 1)
            pool.iota(thr2[:, :], [[NPAIR, ROUNDS]], base=0, channel_multiplier=0, allow_small_or_imprecise_dtypes=True).then_inc(consts, 1)
            pool.iota(thr3[:, :], [[SL, NT]], base=0, channel_multiplier=0, allow_small_or_imprecise_dtypes=True).then_inc(consts, 1)
            pool.iota(jt[:, :], [[1, MT]], base=0, channel_multiplier=0, allow_small_or_imprecise_dtypes=True).then_inc(consts, 1)
            pool.iota(pid[:, :], [[PQ, EC]], base=0, channel_multiplier=1, allow_small_or_imprecise_dtypes=True).then_inc(consts, 1)
            pool.memset(brow[:, :], 0.0).then_inc(brow_z, 1)
            pool.memset(arest[:, 0:3, :], 1.0).then_inc(zmade, 1)
            pool.memset(arest[:, 3:5, :], 0.0).then_inc(zmade, 1)
            pool.memset(zerob[:, :], 0.0).then_inc(zmade, 1)
            pool.memset(agg[:, :], 0.0).then_inc(consts, 1)
            pool_tables_a(0)
            pool.memset(WS[:, :, :, :], 0.0).then_inc(cdep, 1)
            pool.wait_ge(cdep, 6)
            pool.wait_ge(wparts_done, 5)
            for q in range(4):
                for j in range(3):
                    for h in range(KD):
                        o = 32 * q + 9 * j
                        pool.tensor_copy(WS[:, h, q, o:o + 9].rearrange("p (i c) -> p i c", c=EA),
                                         wparts[:, j, h, 0:EA].unsqueeze(1).to_broadcast([128, 3, EA])).then_inc(ws_done, 1)
                        pool.tensor_copy(WS[:, h, q, 32 * q + 27 + j:32 * q + 28 + j], wparts[:, j, h, EA:EA + 1]).then_inc(ws_done, 1)
            for j in range(GT):
                pool.wait_ge(p_out[j], 16 * NG + 16)
            pool.wait_ge(t_cp, 5)
            pool_edges(0)
            more_rounds(pool, pool_tables_a, pool_edges, None, lambda r: None)
            pool.wait_ge(r_pos, 2)
            pool.wait_ge(slots_zero, 8 * 16)
            pool.sem_inc(zs_free, 1)
            with pool.Fori(0, NG) as g:
                pool.tensor_copy(ps1[:, :], pos1[:, ds(g * GT, GT)]).then_inc(ps_cp, 1)
                pool.tensor_copy(ps2[:, :], pos2[:, ds(g * GT, GT)]).then_inc(ps_cp, 1)
                v = pool.snap(g * 2 + 2)
                pool.wait_ge(ps_cp, v)
                pool.sem_inc(settle_pool, 1)
                v = pool.snap(g + 1)
                pool.wait_ge(zs_cp, v)
                pool.sem_inc(settle_pool, 1)
                for j in range(GT):
                    for p in (ps1, ps2):
                        pool.indirect_dma_start(slot_in[:, :], bass.IndirectOffsetOnAxis(ap=p[:, j:j + 1], axis=0),
                                                hn[:, j, :], None).then_inc(sc_out, 16)
                v = pool.snap(g * (2 * GT * 16) + 2 * GT * 16)
                pool.wait_ge(sc_out, v)
                pool.sem_inc(zs_free, 1)
            for s in range(2):
                pool.wait_ge(yo_out[s], MT // 2 * 16 + 16)
            with pool.Fori(0, NG) as g:
                v = pool.snap(g + 1)
                pool.wait_ge(f_rstd, v)
                pool.sem_inc(settle_pool, 1)
                pool.tensor_copy(ps1[:, :], pos1[:, ds(g * GT, GT)]).then_inc(fp_cp, 1)
                pool.tensor_copy(ps2[:, :], pos2[:, ds(g * GT, GT)]).then_inc(fp_cp, 1)
                v = pool.snap(g * 2 + 2)
                pool.wait_ge(fp_cp, v)
                pool.sem_inc(settle_pool, 1)
                for j in range(GT):
                    for p, rows in ((ps1, es), (ps2, qe)):
                        pool.indirect_dma_start(rows[:, j, :], None, slot_out[:, :],
                                                bass.IndirectOffsetOnAxis(ap=p[:, j:j + 1], axis=0)).then_inc(fi_in, 16)

        @block.scalar
        def _(act):
            act.sem_inc(ring_act, 1)
            act.sem_inc(xcopied, GT)
            act.wait_ge(wT_T, 1)
            act.activation(W1T[:, :, :].rearrange("p k d -> p (k d)"), bank[6][:, :], ACT.Copy).then_inc(wT_cp, 1)
            for i in range(2):
                act.wait_ge(wT_T, 2 + i)
                act.activation(W2T[:, 2 * i:2 * i + 2, :].rearrange("p k d -> p (k d)"), bank[7 if i == 0 else 5][:, :], ACT.Copy).then_inc(wT_cp, 1)

            def std(to, var, s):
                act.activation(to, var, ACT.Sqrt, bias=epsc[0:T, :]).then_inc(s, 1)

            def features(u, loc, j, gain, shift):
                act.wait_ge(ring_full, u + 1)
                for k in range(KD):
                    ins = act.activation(TT[:, k, j * T:(j + 1) * T], RING[loc % 3][:, 128 * k:128 * k + T], ACT.Identity,
                                         bias=shift(k), scale=gain(k))
                ins.then_inc(ring_act, 1)

            def copy_tile(u, loc, to, w, parts=128):
                act.wait_ge(ring_full, u + 1)
                act.activation(to, RING[loc % 3][0:parts, 0:256].rearrange("p (k n) -> p k n", k=KD)[:, :, 0:w], ACT.Copy).then_inc(ring_act, 1)

            act.wait_ge(consts, 16)
            with act.Fori(0, NG) as g:
                act.wait_ge(paggr, g * GT + GT)
                std(std5[:, :], mv5[:, :, 1], pstd)
                for j in range(GT):
                    act.wait_ge(hn_done, g * GT + j + 1)
                    act.sem_inc(settle_act, 1)
                    act.activation(tile(X, g * GT + j), hn[:, j, :], ACT.Copy).then_inc(xcopied, 1)
                    copy_tile(g * GT + j, j, TT[:, :, j * T:(j + 1) * T], T)
            act.wait_ge(ws_done, 49)
            act.activation(Wst[:, :], bank[5][:, :].bitcast(bf16), ACT.Copy).then_inc(wT_cp, 1)
            act_tables(0)
            act.wait_ge(par_in, (4 * L + L) * 16)

            def edges(group, s):
                act_edges(group * PG + s, s)

            def both(group):
                for s in range(PG):
                    edges(group, s)
            for e in range(EG_FIRST):
                both(e)

            with act.Fori(0, L) as l:
                act.wait_ge(ring_act, l * RING_L + (RING_A + 1))
                act.sem_inc(settle_act, 1)
                act.activation(lnc[:, :], lnp[:, ds(l * 8, 8)], ACT.Copy).then_inc(lnc_done, 1)
                act.activation(b1c[:, :], b1_s[:, ds(l * NF, NF)], ACT.Copy).then_inc(lnc_done, 1)
                act.wait_ge(lnc_done, l * 2 + 2)
                act.sem_inc(settle_act, 1)

                def ln_col(w, k):
                    return lnc[:, 2 * w + k:2 * w + k + 1]
                act.wait_ge(a_mv, l * NG + NG)
                std(stdA[:, :], mvA[:, :, 1], a_std)
                both(l * EG_L + EG_FIRST)

                def normalised(u, loc):
                    for j in range(GT):
                        features(u + j, loc + j, j, lambda k: ln_col(0, k), lambda k: ln_col(1, k))
                normalised(l * RING_L + RING_A, 0)
                with act.Fori(0, NG) as g:
                    eg = l * EG_L + g + (EG_FIRST + EG_A)
                    u0, q0 = l * RING_L + g * RING_GA + (RING_A + GT), l * (2 * NG) + g * 2
                    for pc, (a, b) in enumerate(PC):
                        act.wait_ge(cd_done, q0 + pc + 1)
                        act.activation(corr[:, pc, :], cdiff[:, pc, :], ACT.Exp).then_inc(corr_done, 1)
                        for h in range(KD):
                            act.activation(eT[:, h, a * T:b * T], RING[(2 * pc + h) % 3][:, 0:(b - a) * T], ACT.Exp,
                                           bias=nb[:, pc, h:h + 1], scale=SCALE).then_inc(ring_act, 1)
                    edges(eg, 0)
                    for j in range(GT):
                        copy_tile(u0 + 4 + j, 4 + j, es[:, j, :].rearrange("p (k n) -> p k n", k=KD), 128, T)
                    normalised(u0 + GT + 4, GT + 4)
                    edges(eg, 1)

                def q_softmax(r, n):
                    act.wait_ge(row_dve, r + GT + 1)
                    act.sem_inc(settle_act, 1)
                    act.activation(qe[:, :, :], qe[:, :, :], ACT.Exp, scale=SCALE).then_inc(q_exp, 1)
                uM, rM = l * RING_L + (RING_A + RING_M), l * ROW_L + (ROW_A + ROW_M)
                edges(l * EG_L + (EG_FIRST + EG_M), 0)
                copy_tile(uM, 0, ctxT[:, :, :], 128)
                edges(l * EG_L + (EG_FIRST + EG_M), 1)
                q_softmax(rM, l * NG)

                def second(g, last=False):
                    n0, u0 = l * NT + g * GT, l * RING_L + g * RING_GB + (RING_A + RING_B)
                    r0 = l * ROW_L + g * ROW_GB + (ROW_A + ROW_B)
                    step = lambda i: edges(l * EG_L + g * 4 + (EG_FIRST + EG_B + i // PG), i % PG)
                    for j in range(GT):
                        copy_tile(u0 + j, j, QT[:, :, j * T:(j + 1) * T], T)
                    act.wait_ge(b_aggr, n0 + GT)
                    std(std5b[:, :], mv5b[:, :, 1], b_std)
                    for j in range(GT):
                        features(u0 + GT + j, GT + j, j, lambda k: ln_col(2, k), lambda k: ln_col(3, k))
                    step(0)
                    for f in range(NF):
                        for pc, (a, b) in enumerate(PC):
                            loc = 2 * GT + 2 * f + pc
                            act.wait_ge(ring_full, u0 + loc + 1)
                            act.activation(hid[:, f, a * T:b * T], RING[loc % 3][:, 0:(b - a) * T], ACT.Gelu,
                                           bias=b1c[:, f:f + 1]).then_inc(ring_act, 1)
                        if f % 2 == 0:
                            step(f // 2 + 1)
                    if not last:
                        normalised(u0 + 2 * GT + 2 * NF, 2 * GT + 2 * NF)
                    step(5)
                    if not last:
                        q_softmax(r0 + GT, l * NG + g + 1)
                    step(6)
                    step(7)
                with act.Fori(0, NG - 1) as g:
                    second(g)
                second(NG - 1, last=True)
            with act.Fori(EG_LAST, NEG) as e:
                both(e)
            more_rounds(act, act_tables, lambda r: both(r * NEG), lambda e, ge: both(ge), lambda r: both(r * NEG + (NEG - 1)))

            with act.Fori(0, NG) as g:
                pt0 = g * (3 * GT) + RING_C
                for j in range(GT):
                    copy_tile(pt0 + 2 * j, 2 * j, TT[:, :, j * T:(j + 1) * T], T)
                    copy_tile(pt0 + 2 * j + 1, 2 * j + 1, QT[:, :, j * T:(j + 1) * T], T)
                for j in range(GT):
                    act.wait_ge(row_dve, g * (2 * GT) + j + (ROW_C + 2))
                    act.activation(sqj[:, j, :], HL[:, j, :], ACT.Square, accum_out=ss[:, j:j + 1]).then_inc(c_ss, 1)
                act.wait_ge(c_ss, g * GT + GT)
                act.activation(nrm[:, :], ss[:, :], ACT.Sqrt).then_inc(c_nrm, 1)
                act.wait_ge(c_aggr, g * GT + GT)
                std(std5[:, :], mv5[:, :, 1], c_std)
                for j in range(GT):
                    act.wait_ge(hn_done, g * GT + (HN_C + j + 1))
                    copy_tile(pt0 + 2 * GT + j, 2 * GT + j, TT[:, :, j * T:(j + 1) * T], T)
                act.activation(tile(agg, g * GT, GT), hn[:, :, :].rearrange("p j d -> p (j d)"), ACT.Copy).then_inc(c_zcp, 1)
            act.wait_ge(r_mask, 1)
            act.activation(e21[:, :], e21[:, :], ACT.Exp).then_inc(r_exp, 1)
            act.wait_ge(c_zcp, NG)
            with act.Fori(0, NG) as g:
                act.wait_ge(zs_free, g + 1)
                act.sem_inc(settle_act, 1)
                act.activation(hn[:, :, :].rearrange("p j d -> p (j d)"), tile(agg, g * GT, GT), ACT.Copy).then_inc(zs_cp, 1)

            def slots_T(u, s):
                act.wait_ge(ring_full, u + 1)
                act.activation(xT[s][:, :, :], RING[0][:, 0:KD * SL].rearrange("p (k n) -> p k n", k=KD), ACT.Copy).then_inc(ring_act, 1)

            def hidden(u, s):
                act.wait_ge(ring_full, u + 1)
                for c in range(NFE):
                    ins = act.activation(hT[s % 2][:, c, :], RING[1 + s % 2][:, c * SL:(c + 1) * SL], ACT.Relu, bias=b1e[s][:, c:c + 1])
                ins.then_inc(ring_act, 1)

            def expert_tile(m, s, last=False):
                u = m * 2 + (RING_E + 1)
                if not last:
                    slots_T(u, (s + 1) % 2)
                hidden(u + (0 if last else 1), s)
            slots_T(RING_E, 0)
            expert_tile(0, 0)
            with act.Fori(0, MT // XB - 1) as i:
                for t in range(XB):
                    expert_tile(i * XB + (1 + t), (1 + t) % XB)
            for m in range(MT - XB + 1, MT):
                expert_tile(m, m % XB, last=m == MT - 1)
            with act.Fori(0, NG) as g:
                act.wait_ge(f_aggr, g * GT + GT)
                std(std5b[:, :], mv5b[:, :, 1], f_std)

        @block.tensor
        def _(pe):
            pe.sem_inc(s_done, 2)
            pe.sem_inc(cn_done, 1)
            pe.wait_ge(consts, 16)
            pe.wait_ge(gw_in, 48)
            for k in range(KD):
                for h in range(KD):
                    ins = pe.transpose(bank[6][:, 256 * k + 128 * h:256 * k + 128 * h + 128], gW1[:, h, 128 * k:128 * k + 128], ident[:, :])
            ins.then_inc(wT_T, 1)
            for i in range(2):
                for k in range(2):
                    for h in range(KD):
                        ins = pe.transpose(bank[7 if i == 0 else 5][:, 256 * k + 128 * h:256 * k + 128 * h + 128],
                                           gW2[:, h, 128 * (2 * i + k):128 * (2 * i + k) + 128], ident[:, :])
                ins.then_inc(wT_T, 1)
            pe.wait_ge(bc_ready, 1)
            flat = spread.rearrange("p c q -> p (c q)")
            pe.matmul(bank[1][0:PQ, 0:2 * NS], ones[0:EP, 0:PQ], flat, start=True, stop=True).then_inc(bc_ready, 1)

            def slot(u, loc):
                if loc == 0:
                    pe.wait_ge(ring_act, u + 1)
                elif loc >= 3:
                    pe.wait_ge(ring_act, u - 1)
                return RING[loc % 3]

            def row_slot(u, loc):
                pe.wait_ge(row_dve, u + 1 if loc == 0 else u)
                return ROW[loc % 2]

            def tile_T(u, loc, rows, parts=T):
                to = slot(u, loc)
                for k in range(KD):
                    ins = pe.transpose(to[:, 128 * k:128 * k + parts], rows[:, 128 * k:128 * k + 128], ident[0:parts, 0:parts])
                ins.then_inc(ring_full, 1)

            def row(u, loc, products, cols=D, parts=T):
                to = row_slot(u, loc)
                for i, (a, b) in enumerate(products):
                    ins = pe.matmul(to[0:parts, 0:cols], a, b, start=i == 0, stop=i == len(products) - 1)
                ins.then_inc(row_full, 1)

            pe.wait_ge(wT_cp, 3)
            with pe.Fori(0, NG) as g:
                for j in range(GT):
                    pe.wait_ge(hn_done, g * GT + j + 1)
                    tile_T(g * GT + j, j, hn[:, j, :])
                for j in range(GT):
                    pe.wait_ge(ring_act, g * GT + j + 2)
                    row(g * GT + j, j, [(TT[:, k, j * T:(j + 1) * T], W1T[:, k, :]) for k in range(KD)])
            pe.wait_ge(ws_done, 48)
            pe.wait_ge(row_dve, NT + 1)
            for q in range(4):
                for h in range(KD):
                    ins = pe.transpose(bank[5][:, :].bitcast(bf16)[:, q * D + 128 * h:q * D + 128 * h + 128], WS[:, h, q, :], identb[:, :])
            ins.then_inc(ws_done, 1)
            pe_tables(0)
            pe.wait_ge(wT_cp, 4)
            pe.wait_ge(t_cp, 5)

            def edges(group, s, first=False):
                pe_edges(group * PG + s, group, s, first=first)

            def both(group, first=False):
                for s in range(PG):
                    edges(group, s, first=first and s == 0)
            for e in range(EG_FIRST):
                both(e, first=e == 0)
            pe.wait_ge(brow_out, 16 + 2 * L * 16)

            with pe.Fori(0, L) as l:
                both(l * EG_L + EG_FIRST)
                pe.wait_ge(wA_in, l * 32 + 32)
                pe.sem_inc(settle_pe, 1)

                def normalised(h, u, loc):
                    for j in range(GT):
                        pe.wait_ge(hn_done, h + j + 1)
                        tile_T(u + j, loc + j, hn[:, j, :])
                normalised(l * HN_L + NT, l * RING_L + RING_A, 0)
                with pe.Fori(0, NG) as g:
                    eg = l * EG_L + g + (EG_FIRST + EG_A)
                    h0, q0 = l * HN_L + g * GT + (NT + GT), l * (2 * NG) + g * 2
                    u0, r0 = l * RING_L + g * RING_GA + (RING_A + GT), l * ROW_L + g * ROW_GA + ROW_A
                    for pc, (a, b) in enumerate(PC):
                        for h in range(KD):
                            loc = 2 * pc + h
                            pe.wait_ge(ring_act, u0 + 1)
                            to = slot(u0 + loc, loc)
                            for k in range(KD):
                                ins = pe.matmul(to[:, 0:(b - a) * T], Wk_s[:, k, 128 * h:128 * h + 128], TT[:, k, a * T:b * T],
                                                start=k == 0, stop=k == KD - 1)
                            ins.then_inc(ring_full, 1)
                        for j in range(a, b):
                            row(r0 + j, j, [(TT[:, k, j * T:(j + 1) * T], Wv_s[:, k, :]) for k in range(KD)])
                    edges(eg, 0)
                    for pc, (a, b) in enumerate(PC):
                        for j in range(a, b):
                            loc = 4 + j
                            pe.wait_ge(ring_act, u0 + (2 * pc + 3))
                            to = slot(u0 + loc, loc)
                            for h in range(KD):
                                ins = pe.transpose(to[0:T, 128 * h:128 * h + 128], eT[:, h, j * T:(j + 1) * T], ident[:, :])
                            ins.then_inc(ring_full, 1)
                    normalised(h0, u0 + GT + 4, GT + 4)
                    for pc, (a, b) in enumerate(PC):
                        to = row_slot(r0 + GT + pc, GT + pc)
                        for h in range(KD):
                            for j in range(a, b):
                                if h == 0:
                                    pe.wait_ge(ring_act, u0 + (4 + j + 2))
                                    pe.wait_ge(row_dve, r0 + j + 2)
                                ins = pe.matmul(to[:, 129 * h:129 * h + 129], es[:, j, 128 * h:128 * h + 128], V5[:, j, h, :],
                                                start=j == a, stop=j == b - 1)
                        ins.then_inc(row_full, 1)

                    edges(eg, 1)

                def queries(u, r, rloc):
                    for j in range(GT):
                        pe.wait_ge(ring_act, u + j + 2)
                        row(r + j, rloc + j, [(TT[:, k, j * T:(j + 1) * T], Wq_s[:, k, :]) for k in range(KD)])
                uM, rM = l * RING_L + (RING_A + RING_M), l * ROW_L + (ROW_A + ROW_M)
                edges(l * EG_L + (EG_FIRST + EG_M), 0)
                pe.wait_ge(cn_done, l + 2)
                to = slot(uM, 0)
                for h in range(KD):
                    ins = pe.transpose(to[:, 128 * h:128 * h + 128], ctxN[:, h, :], ident[:, :])
                ins.then_inc(ring_full, 1)
                pe.wait_ge(wQ_in, l * 32 + 32)
                queries(uM - GT, rM, 0)
                edges(l * EG_L + (EG_FIRST + EG_M), 1)
                pe.wait_ge(ring_act, uM + 2)
                for h in range(KD):
                    row(rM + GT + h, GT + h, [(ctxT[:, h, :], Wo_s[:, h, :])], parts=128)
                pe.wait_ge(wF_in, l * 32 + 32)
                pe.sem_inc(settle_pe, 1)

                def second(g, last=False):
                    n0, h0 = l * NG + g, l * HN_L + g * (2 * GT) + (2 * NT + GT)
                    u0 = l * RING_L + g * RING_GB + (RING_A + RING_B)
                    r0 = l * ROW_L + g * ROW_GB + (ROW_A + ROW_B)
                    rF = GT if last else 2 * GT
                    step = lambda i: edges(l * EG_L + g * 4 + (EG_FIRST + EG_B + i // PG), i % PG)
                    bias_row = lambda w: (onesb[:, 0:T], brow[:, ds(l * (2 * D) + w * D, D)])
                    pe.wait_ge(q_norm, n0 + 1)
                    for j in range(GT):
                        tile_T(u0 + j, j, qe[:, j, :])
                    for j in range(GT):
                        pe.wait_ge(ring_act, u0 + j + 2)
                        row(r0 + j, j, [(QT[:, k, j * T:(j + 1) * T], M_s[:, k, :]) for k in range(KD)] + [bias_row(0)])
                    step(0)
                    for j in range(GT):
                        pe.wait_ge(hn_done, h0 + j + 1)
                        tile_T(u0 + GT + j, GT + j, hn[:, j, :])
                    for f in range(NF):
                        for pc, (a, b) in enumerate(PC):
                            loc = 2 * GT + 2 * f + pc
                            pe.wait_ge(ring_act, u0 + GT + b + 1)
                            to = slot(u0 + loc, loc)
                            for k in range(KD):
                                ins = pe.matmul(to[:, 0:(b - a) * T], W1_s[:, k, 128 * f:128 * f + 128], TT[:, k, a * T:b * T],
                                                start=k == 0, stop=k == KD - 1)
                            ins.then_inc(ring_full, 1)
                        if f % 2 == 0:
                            step(f // 2 + 1)
                    if not last:
                        normalised(h0 + GT, u0 + 2 * GT + 2 * NF, 2 * GT + 2 * NF)
                        queries(u0 + 2 * GT + 2 * NF, r0 + GT, GT)
                    step(5)
                    pe.wait_ge(ring_act, u0 + (2 * GT + 2 * NF + 1))
                    for j in range(GT):
                        if j % 2:
                            step(6 + j // 2)
                        row(r0 + rF + j, rF + j, [(hid[:, f, j * T:(j + 1) * T], W2_s[:, f, :]) for f in range(NF)] + [bias_row(1)])
                with pe.Fori(0, NG - 1) as g:
                    second(g)
                second(NG - 1, last=True)
            with pe.Fori(EG_LAST, NEG) as e:
                both(e)
            pe_sums(NPAIR - 1, 1)

            def pe_first(r):
                pe.wait_ge(t_cp, r * 5 + 5)
                pe.sem_inc(settle_pe, 1)
                both(r * NEG, first=True)

            def pe_last(r):
                both(r * NEG + (NEG - 1))
                pe_sums(r * NPAIR + (NPAIR - 1), 1)
            more_rounds(pe, pe_tables, pe_first, lambda e, ge: both(ge), pe_last)

            pe.wait_ge(late_in, 64)
            with pe.Fori(0, NG) as g:
                pt0, r0 = g * (3 * GT) + RING_C, g * (2 * GT) + ROW_C
                pe.wait_ge(c_in, g * 32 + 32)
                pe.wait_ge(c_agg, g + 1)
                for j in range(GT):
                    tile_T(pt0 + 2 * j, 2 * j, es[:, j, :])
                    tile_T(pt0 + 2 * j + 1, 2 * j + 1, hn[:, j, :])
                for j in range(GT):
                    pe.wait_ge(ring_act, pt0 + 2 * j + 3)
                    row(r0 + j, j, [(TT[:, k, j * T:(j + 1) * T], W2T[:, k, :]) for k in range(KD)]
                        + [(QT[:, k, j * T:(j + 1) * T], W2T[:, KD + k, :]) for k in range(KD)])
                for j in range(GT):
                    pe.wait_ge(hn_done, g * GT + (HN_C + j + 1))
                    tile_T(pt0 + 2 * GT + j, 2 * GT + j, hn[:, j, :])
                for j in range(GT):
                    pe.wait_ge(ring_act, pt0 + 2 * GT + j + 2)
                    row(r0 + GT + j, GT + j, [(TT[:, k, j * T:(j + 1) * T], gw_s[:, k, :]) for k in range(KD)], cols=NE)
            pe.wait_ge(r_mask, 2)
            flat = mask.rearrange("p t e -> p (t e)")
            pe.matmul(RING[0][0:T, 0:NT * NE], tri[:, :], flat, start=True, stop=True).then_inc(r_rank, 1)
            pe.matmul(RING[1][0:T, 0:NT * NE], ones[0:T, 0:T], flat, start=True, stop=True).then_inc(r_rank, 1)

            def slots_T(mi, s):
                pe.wait_ge(xs_in[s], mi * 16 + 16)
                for k in range(KD):
                    ins = pe.transpose(RING[0][:, SL * k:SL * (k + 1)], xs[s][:, 128 * k:128 * k + 128], ident[:, :])
                ins.then_inc(ring_full, 1)

            def up(mi, s):
                pe.wait_ge(w1_in[s], mi * 32 + 32)
                for c in range(NFE):
                    for k in range(KD):
                        ins = pe.matmul(RING[1 + s % 2][:, c * SL:(c + 1) * SL], W1e[s][:, k, c::NFE], xT[s % 2][:, k, :],
                                        start=k == 0, stop=k == KD - 1)
                ins.then_inc(ring_full, 1)

            def down(m, mi, s):
                pe.wait_ge(w2_in[s], mi * 32 + 32)
                pe.wait_ge(row_dve, m + ROW_E)
                for c in range(NFE):
                    ins = pe.matmul(ROW[s % 2][:, 0:D], hT[s % 2][:, c, :], W2e[s][:, c, :], start=c == 0, stop=c == NFE - 1)
                ins.then_inc(row_full, 1)

            def expert_tile(m, mi, s, first=False, last=False):
                u = m * 2 + (RING_E + 1)
                pe.wait_ge(ring_act, u + 1 if first else u)
                if not last:
                    slots_T(mi + (s + 1) // XB, (s + 1) % XB)
                up(mi, s)
                if not first:
                    pe.wait_ge(ring_act, u + 1)
                    down(m - 1, mi - (s == 0), (s - 1) % XB)
            pe.wait_ge(r_pos, 1)
            pe.wait_ge(ring_act, RING_E + 1)
            slots_T(0, 0)
            expert_tile(0, 0, 0, first=True)
            with pe.Fori(0, MT // XB - 1) as i:
                for t in range(XB):
                    s = (1 + t) % XB
                    expert_tile(i * XB + (1 + t), i + (1 + t) // XB, s)
            for m in range(MT - XB + 1, MT):
                expert_tile(m, m // XB, m % XB, last=m == MT - 1)
            pe.wait_ge(ring_act, 2 * MT + RING_E + 1)
            down(MT - 1, (MT - 1) // XB, (MT - 1) % XB)

        @block.vector
        def _(dve):
            dve.sem_inc(z_done, 4)
            dve.sem_inc(acc_done, 1)
            dve.sem_inc(lo_done, 2)
            dve.sem_inc(row_dve, 1)
            dve.sem_inc(f_rstd, 1)
            dve.sem_inc(out_done, 16)
            for i in range(2):
                dve.sem_inc(yo_out[i], 16)
            for j in range(GT):
                dve.sem_inc(p_out[j], 16)
            chain = [0]

            def link(ins):
                chain[0] += 1
                ins.then_inc(base_step, 1)
                dve.wait_ge(base_step, chain[0])

            dve.wait_ge(consts, 16)
            dve.wait_ge(dst_in, 16)
            dt = dst_tiles.rearrange("p (c e) -> p c e", e=SE)
            dve.tensor_reduce(hl[:, 0:EC], dt, AX.X, ALU.max)
            link(dve.tensor_reduce(hl[:, EC:2 * EC], dt, AX.X, ALU.min))
            link(dve.tensor_tensor(above, hl[:, :].unsqueeze(2).to_broadcast([EP, 2 * EC, NT - 1]),
                                   thr[:, :].unsqueeze(1).to_broadcast([EP, 2 * EC, NT - 1]), ALU.is_ge))
            link(dve.tensor_reduce(hlb[:, :], above, AX.X, ALU.add))
            link(dve.scalar_tensor_tensor(hlb[:, 0:EC], hlb[:, 0:EC], 1.0, hlb[:, EC:2 * EC], ALU.add, ALU.subtract))
            dve.tensor_tensor(spread, ident[0:EP, 0:EP].unsqueeze(1).to_broadcast([EP, 2 * EC, EP]),
                              hlb[:, :].unsqueeze(2).to_broadcast([EP, 2 * EC, EP]), ALU.mult).then_inc(bc_ready, 1)
            dve.wait_ge(gw_in, 48)
            dve.tensor_copy(w4[:, :, 0:EA], gW1[:, :, D:D + EA]).then_inc(wparts_done, 1)
            dve.wait_ge(wparts_done, 1)
            dve.tensor_copy(wparts[:, 0, :, :], w4[:, :, :]).then_inc(wparts_done, 1)
            dve.wait_ge(wparts_done, 2)
            dve.tensor_tensor(w4r[:, :, :], w4[:, :, :], wparts[:, 0, :, :], ALU.subtract).then_inc(wparts_done, 1)
            dve.wait_ge(wparts_done, 3)
            dve.tensor_copy(wparts[:, 1, :, :], w4r[:, :, :]).then_inc(wparts_done, 1)
            dve.wait_ge(wparts_done, 4)
            dve.tensor_tensor(wparts[:, 2, :, :], w4r[:, :, :], wparts[:, 1, :, :], ALU.subtract).then_inc(wparts_done, 1)
            dve.wait_ge(br_in, 32)
            dve.tensor_copy(bparts[:, 0, :], browf[:, :]).then_inc(brp_done, 1)
            dve.wait_ge(brp_done, 1)
            dve.tensor_tensor(browr[:, :], browf[:, :], bparts[:, 0, :], ALU.subtract).then_inc(brp_done, 1)
            dve.wait_ge(brp_done, 2)
            dve.tensor_copy(bparts[:, 1, :], browr[:, :]).then_inc(brp_done, 1)
            dve.wait_ge(brp_done, 3)
            dve.tensor_tensor(bparts[:, 2, :], browr[:, :], bparts[:, 1, :], ALU.subtract).then_inc(brp_done, 1)
            dve.wait_ge(bc_ready, 2)
            dve.tensor_copy(n_bc, bank[1][0:PQ, 0:NS])
            ins = dve.tensor_copy(lo_bc, bank[1][0:PQ, NS:2 * NS])
            link(ins)
            dve.tensor_copy(lo0[:, :], lo_bc[:, 0:1])
            link(dve.tensor_tensor_scan(cum[:, :], n_bc, n_bc, 0.0, ALU.add, ALU.max))
            dve.tensor_scalar(rjunk[:, :], thr2[:, :], cum[0:1, NS - 1:NS], None, ALU.is_lt, ALU.add, accum_out=rcnt[:, :])
            link(dve.tensor_tensor(junk, n_bc, cum[:, :], ALU.subtract))
            dve.tensor_copy(rounds_i[:, :], rcnt[:, :]).then_inc(rounds_done, 1)
            link(dve.tensor_tensor(junk, junk, lo_bc, ALU.add))
            dve.memset(dg[:, NS - 1:NS], 0.0)
            link(dve.tensor_tensor(dg[:, 0:NS - 1], junk[:, 1:NS], junk[:, 0:NS - 1], ALU.subtract))
            dve_tables_a(0)

            def aggregate(s_stat, s_aggr, n, st, mv):
                for j in range(GT):
                    dve.wait_ge(s_stat, n + j + 1)
                    dve.sem_inc(settle_dve, 1)
                    dve.bn_aggr(mv[:, j, :], st[:, j, :]).then_inc(s_aggr, 1)

            def stats(rows, s_stat, s_aggr, n, st, mv):
                dve.sem_inc(settle_dve, 1)
                for j in range(GT):
                    dve.bn_stats(st[:, j, :], rows(j)).then_inc(s_stat, 1)
                aggregate(s_stat, s_aggr, n, st, mv)

            def keep_stats(g, l):
                dve.wait_ge(a_aggr, l * NT + g * GT + GT)
                dve.sem_inc(settle_dve, 1)
                dve.tensor_copy(mvA[:, ds(g * GT, GT), :], mv5[:, :, :]).then_inc(a_mv, 1)

            for g in range(NG):
                dve.wait_ge(x_in[g], 16)
            with dve.Fori(0, NG) as g:
                stats(lambda j: tile(X, g * GT + j), pstat, paggr, g * GT, st5, mv5)
                dve.wait_ge(pstd, g + 1)
                dve.reciprocal(rs5b[:, :], std5[:, :]).then_inc(prstd, 1)
                dve.wait_ge(prstd, g + 1)
                for j in range(GT):
                    dve.wait_ge(xcopied, g * GT + j + 1)
                    dve.tensor_scalar(hn[:, j, :], tile(X, g * GT + j), mv5[:, j, 0:1], rs5b[:, j:j + 1],
                                      ALU.subtract, ALU.mult).then_inc(hn_done, 1)
                for j in range(GT):
                    dve.wait_ge(row_full, g * GT + j + 1)
                    dve.wait_ge(p_out[j], g * 16 + 16)
                    dve.tensor_copy(es[:, j, :], ROW[j % 2][0:T, 0:D]).then_inc(row_dve, 1)
            dve_tables_b(0)
            dve.wait_ge(t_cp, 5)

            def edges(e, group, s, first=False, last=False):
                dve_edges(e * PG + s, group * PG + s, group, s, first=first, last=last)

            def both(e, group, first=False, last=False):
                for s in range(PG):
                    edges(e, group, s, first=first and s == 0, last=last and s == PG - 1)
            for e in range(EG_FIRST):
                both(e, e, first=e == 0)
            dve.wait_ge(xcopied, NT + GT)
            dve.wait_ge(xn_out, 16)
            with dve.Fori(0, NG) as g:
                stats(lambda j: tile(X, g * GT + j), a_stat, a_aggr, g * GT, st5, mv5)
                keep_stats(g, 0)

            with dve.Fori(0, L) as l:
                dve.wait_ge(a_std, l + 1)
                dve.reciprocal(rstd_t[:, :], stdA[:, :]).then_inc(a_rstd, 1)
                both(l * EG_L + EG_FIRST, l * EG_L + EG_FIRST)
                dve.memset(ctxS[:, :, :], 0.0).then_inc(l_init, 1)
                dve.memset(mO[:, :], LOW).then_inc(l_init, 1)
                dve.wait_ge(a_rstd, l + 1)
                dve.sem_inc(settle_dve, 1)

                def normalised(g):
                    for j in range(GT):
                        dve.tensor_scalar(hn[:, j, :], tile(X, g * GT + j), mvA[:, ds(g * GT + j, 1), 0], rstd_t[:, ds(g * GT + j, 1)],
                                          ALU.subtract, ALU.mult).then_inc(hn_done, 1)
                normalised(0)
                dve.wait_ge(l_init, l * 2 + 2)
                dve.sem_inc(settle_dve, 1)

                def first(g, after):
                    eg = l * EG_L + g + (EG_FIRST + EG_A)
                    u0, r0, q0 = l * RING_L + g * RING_GA + (RING_A + GT), l * ROW_L + g * ROW_GA + ROW_A, l * (2 * NG) + g * 2
                    for pc, (a, b) in enumerate(PC):
                        for h in range(KD):
                            loc = 2 * pc + h
                            dve.wait_ge(ring_full, u0 + loc + 1)
                            dve.reduce_max(pm[:, h:h + 1], RING[loc % 3][:, 0:(b - a) * T], axis=AX.X).then_inc(k_max, 1)
                        dve.wait_ge(k_max, q0 * 2 + 2 * pc + 2)
                        if pc:
                            dve.wait_ge(m_cp, q0 + pc)
                        dve.tensor_tensor(mN[:, :], mO[:, :], pm[:, :], ALU.max).then_inc(m_new, 1)
                        dve.wait_ge(m_new, q0 + pc + 1)
                        dve.tensor_scalar(nb[:, pc, :], mN[:, :], -SCALE, None, ALU.mult).then_inc(nb_done, 1)
                        dve.wait_ge(nb_done, q0 + pc + 1)
                        dve.scalar_tensor_tensor(cdiff[:, pc, :], mO[:, :], SCALE, nb[:, pc, :], ALU.mult, ALU.add).then_inc(cd_done, 1)
                        dve.wait_ge(cd_done, q0 + pc + 1)
                        dve.tensor_copy(mO[:, :], mN[:, :]).then_inc(m_cp, 1)
                        for j in range(a, b):
                            dve.wait_ge(row_full, r0 + j + 1)
                            dve.tensor_copy(V5[:, j, :, 0:128], ROW[j % 2][0:T, 0:D].rearrange("p (k n) -> p k n", k=KD)).then_inc(row_dve, 1)
                    edges(eg, eg, 0)
                    dve.wait_ge(row_full, r0 + GT)
                    dve.sem_inc(settle_dve, 1)
                    normalised(after)
                    for pc in range(2):
                        dve.wait_ge(corr_done, q0 + pc + 1)
                        dve.wait_ge(row_full, r0 + (GT + pc + 1))
                        dve.wait_ge(row_dve, r0 + (GT + pc + 1))
                        for h in range(KD):
                            ins = dve.scalar_tensor_tensor(ctxS[:, h, :], ctxS[:, h, :], corr[:, pc, h:h + 1],
                                                           ROW[(GT + pc) % 2][:, 129 * h:129 * h + 129], ALU.mult, ALU.add)
                        ins.then_inc(row_dve, 1)
                    edges(eg, eg, 1)
                with dve.Fori(0, NG - 1) as g:
                    first(g, g + 1)
                first(NG - 1, 0)

                heads = lambda ap: ap.rearrange("p (h d) -> p h d", d=DH)
                all_heads = qe[:, :, :].rearrange("p j (h d) -> p (j h) d", d=DH)
                per_head = lambda ap: ap.unsqueeze(2).to_broadcast([T, H, DH])

                def queries(r, rloc, n):
                    for j in range(GT):
                        q_ps = heads(ROW[(rloc + j) % 2][0:T, 0:D])
                        dve.wait_ge(row_full, r + j + 1)
                        dve.reduce_max(qm[:, j, :], q_ps, axis=AX.X).then_inc(q_max, 1)
                        dve.wait_ge(q_max, n * GT + j + 1)
                        dve.tensor_tensor(heads(qe[:, j, :]), q_ps, per_head(qm[:, j, :]), ALU.subtract).then_inc(row_dve, 1)

                def q_softmax(n):
                    dve.wait_ge(q_exp, n + 1)
                    dve.reduce_sum(qs[:, :, :].rearrange("p j h -> p (j h)"), all_heads, axis=AX.X).then_inc(q_sum, 1)
                    dve.wait_ge(q_sum, n + 1)
                    dve.reciprocal(qr[:, :, :], qs[:, :, :]).then_inc(q_rec, 1)
                    dve.wait_ge(q_rec, n + 1)
                    dve.tensor_tensor(all_heads, all_heads, qr[:, :, :].rearrange("p j h -> p (j h)").unsqueeze(2).to_broadcast([T, GT * H, DH]),
                                      ALU.mult).then_inc(q_norm, 1)
                rM, eM = l * ROW_L + (ROW_A + ROW_M), l * EG_L + (EG_FIRST + EG_M)
                dve.wait_ge(row_dve, rM + 1)
                dve.reciprocal(rk[:, :], ctxS[:, :, 128]).then_inc(rk_done, 1)
                dve.tensor_tensor(ctxN[:, :, :], ctxS[:, :, 0:128], headmask[:, :].unsqueeze(1).to_broadcast([128, KD, 128]),
                                  ALU.mult).then_inc(cn_done, 1)
                edges(eM, eM, 0)
                queries(rM, 0, l * NG)
                edges(eM, eM, 1)
                q_softmax(l * NG)
                dve.wait_ge(rk_done, l + 1)
                for h in range(KD):
                    dve.wait_ge(row_full, rM + (GT + h + 1))
                    dve.tensor_scalar(M_s[:, h, :], ROW[(GT + h) % 2][:, 0:D], rk[:, h:h + 1], None, ALU.mult).then_inc(row_dve, 1)

                def second(g, last=False):
                    n0, lg = l * NT + g * GT, l * NG + g
                    u0 = l * RING_L + g * RING_GB + (RING_A + RING_B)
                    r0 = l * ROW_L + g * ROW_GB + (ROW_A + ROW_B)
                    rF = GT if last else 2 * GT
                    eg = lambda i: l * EG_L + g * 4 + (EG_FIRST + EG_B + i // PG)
                    step = lambda i: edges(eg(i), eg(i), i % PG)

                    def with_stats(write, written, s_stat, s_aggr, n, st, mv):
                        def stat(j):
                            dve.wait_ge(row_dve, written(j))
                            dve.sem_inc(settle_dve, 1)
                            dve.bn_stats(st[:, j, :], tile(X, g * GT + j)).then_inc(s_stat, 1)
                        for j in range(GT):
                            write(j)
                            if j:
                                stat(j - 1)
                        stat(GT - 1)
                        aggregate(s_stat, s_aggr, n, st, mv)

                    def residual(j, loc):
                        dve.wait_ge(row_full, r0 + loc + 1)
                        dve.tensor_tensor(tile(X, g * GT + j), ROW[loc % 2][0:T, 0:D], tile(X, g * GT + j), ALU.add).then_inc(row_dve, 1)
                    with_stats(lambda j: residual(j, j), lambda j: r0 + j + 2, b_stat, b_aggr, n0, st5b, mv5b)
                    dve.wait_ge(b_std, lg + 1)
                    dve.reciprocal(rs5b[:, :], std5b[:, :]).then_inc(b_rstd, 1)
                    dve.wait_ge(b_rstd, lg + 1)
                    dve.wait_ge(b_aggr, n0 + GT)
                    for j in range(GT):
                        dve.tensor_scalar(hn[:, j, :], tile(X, g * GT + j), mv5b[:, j, 0:1], rs5b[:, j:j + 1],
                                          ALU.subtract, ALU.mult).then_inc(hn_done, 1)
                    step(0)
                    step(1)
                    if not last:
                        dve.wait_ge(ring_full, u0 + 2 * GT)
                        dve.sem_inc(settle_dve, 1)
                        normalised(g + 1)
                    step(2)
                    step(3)
                    step(4)
                    if not last:
                        queries(r0 + GT, GT, lg + 1)
                    step(5)

                    def output(j):
                        if j % 2:
                            step(6 + j // 2)
                        if j == 1 and not last:
                            q_softmax(lg + 1)
                        residual(j, rF + j)
                    with_stats(output, lambda j: r0 + rF + j + 2, a_stat, a_aggr, n0 + NT, st5, mv5)
                    keep_stats(g, l + 1)
                with dve.Fori(0, NG - 1) as g:
                    second(g)
                second(NG - 1, last=True)

            for e in range(EG_LAST, NEG):
                both(e, e, last=e == NEG - 1)
            dve_acc(NPAIR - 1, block_of(NPAIR - 1))

            def dve_last(r):
                both(NEG - 1, r * NEG + (NEG - 1), last=True)
                dve_acc(r * NPAIR + (NPAIR - 1), block_of(NPAIR - 1))

            def tables(r):
                dve_tables_a(r)
                dve_tables_b(r)
                dve.wait_ge(t_cp, r * 5 + 5)
            more_rounds(dve, tables, lambda r: both(0, r * NEG, first=True), lambda e, ge: both(e, ge), dve_last)

            dve.wait_ge(late_in, 64)
            with dve.Fori(0, NG) as g:
                r0 = g * (2 * GT) + ROW_C
                dve.tensor_copy(hn[:, :, :].rearrange("p j d -> p (j d)"), tile(agg, g * GT, GT)).then_inc(c_agg, 1)
                for j in range(GT):
                    dve.wait_ge(row_full, r0 + j + 1)
                    dve.tensor_scalar(HL[:, j, :], ROW[j % 2][0:T, 0:D], 0.0, None, ALU.max).then_inc(row_dve, 1)
                dve.wait_ge(c_nrm, g + 1)
                dve.tensor_scalar(nrm[:, :], nrm[:, :], 1e-12, None, ALU.max).then_inc(c_rn, 1)
                dve.wait_ge(c_rn, g * 2 + 1)
                dve.reciprocal(rn[:, :], nrm[:, :]).then_inc(c_rn, 1)
                dve.wait_ge(c_rn, g * 2 + 2)
                dve.wait_ge(c_in, g * 32 + 32)
                for j in range(GT):
                    dve.scalar_tensor_tensor(HL[:, j, :], HL[:, j, :], rn[:, j:j + 1], qe[:, j, :], ALU.mult, ALU.add).then_inc(c_y, 1)
                for j in range(GT):
                    dve.wait_ge(c_y, g * (2 * GT) + j + 1)
                    dve.tensor_tensor(tile(X, g * GT + j), HL[:, j, :], tile(X, g * GT + j), ALU.add).then_inc(c_y, 1)
                dve.wait_ge(c_y, g * (2 * GT) + 2 * GT)
                stats(lambda j: tile(X, g * GT + j), c_stat, c_aggr, g * GT, st5, mv5)
                dve.wait_ge(c_std, g + 1)
                dve.reciprocal(rs5b[:, :], std5[:, :]).then_inc(c_rstd, 1)
                dve.wait_ge(c_rstd, g + 1)
                for j in range(GT):
                    dve.tensor_scalar(hn[:, j, :], tile(X, g * GT + j), mv5[:, j, 0:1], rs5b[:, j:j + 1],
                                      ALU.subtract, ALU.mult).then_inc(hn_done, 1)
                for j in range(GT):
                    dve.wait_ge(row_full, r0 + GT + j + 1)
                    dve.tensor_tensor(LG[:, ds((g * GT + j) * NE, NE)], ROW[(GT + j) % 2][0:T, 0:NE], gb_s[:, :], ALU.add).then_inc(row_dve, 1)
                dve.wait_ge(c_zcp, g + 1)
            steps = [0]

            def then(ins):
                steps[0] += 1
                ins.then_inc(r_step, 1)
                dve.wait_ge(r_step, steps[0])

            dve.wait_ge(row_dve, ROW_E + 1)
            lg = LG[:, :].rearrange("p (t e) -> p t e", e=NE)
            per_tile = lambda ap: ap.unsqueeze(2).to_broadcast([T, NT, NE])
            per_expert = lambda ap: ap.unsqueeze(1).to_broadcast([T, NT, NE])
            flat = lambda ap: ap.rearrange("p t e -> p (t e)")
            for logits, most, sel in ((lg, m1, sel1), (lg2, m2, sel2)):
                then(dve.reduce_max(most[:, :], logits, axis=AX.X))
                then(dve.tensor_tensor(sel, logits, per_tile(most[:, :]), ALU.is_equal))
                then(dve.tensor_tensor(rtmp, sel, per_expert(iota_e[:, :]), ALU.mult))
                then(dve.tensor_reduce(i1[:, :], rtmp, AX.X, ALU.min))
                then(dve.tensor_tensor(sel, per_expert(iota_e[:, :]), per_tile(i1[:, :]), ALU.is_equal))
                if sel is sel1:
                    then(dve.scalar_tensor_tensor(flat(lg2), flat(sel1), LOW, LG[:, :], ALU.mult, ALU.add))
            dve.tensor_tensor(e21[:, :], m2[:, :], m1[:, :], ALU.subtract).then_inc(r_mask, 1)
            dve.tensor_tensor(mask, sel1, sel2, ALU.add).then_inc(r_mask, 1)
            dve.wait_ge(r_exp, 1)
            then(dve.tensor_scalar(w1t[:, :], e21[:, :], 1.0, None, ALU.add))
            then(dve.reciprocal(w1t[:, :], w1t[:, :]))
            then(dve.tensor_tensor(w2t[:, :], w1t[:, :], e21[:, :], ALU.mult))
            dve.wait_ge(r_rank, 2)
            tiles3 = lambda b: b[0:T, 0:NT * NE].rearrange("p (t e) -> p t e", e=NE)
            then(dve.tensor_copy(tot, tiles3(RING[1])))
            for x_ in range(NE):
                ins = dve.tensor_tensor_scan(cumt[:, :, x_], onee[:, :], tot[:, :, x_], 0.0, ALU.mult, ALU.add)
            then(ins)
            then(dve.tensor_tensor(nge, cumt[:, NT - 1, :].unsqueeze(2).to_broadcast([T, NE, NT]),
                                   thr3[:, :].unsqueeze(1).to_broadcast([T, NE, NT]), ALU.is_gt))
            then(dve.tensor_reduce(te[:, :], nge, AX.X, ALU.add))
            then(dve.tensor_tensor_scan(ce[:, :], onee[:, 0:NE], te[:, :], 0.0, ALU.mult, ALU.add))
            then(dve.tensor_tensor(ste[:, :], ce[:, :], te[:, :], ALU.subtract))
            then(dve.tensor_scalar(ste[:, :], ste[:, :], float(SL), None, ALU.mult))
            then(dve.tensor_tensor(slotp, tiles3(RING[0]), cumt, ALU.add))
            then(dve.tensor_tensor(slotp, slotp, tot, ALU.subtract))
            then(dve.tensor_tensor(slotp, slotp, per_expert(ste[:, :]), ALU.add))
            for sel, posf, pos in ((sel1, pos1f, pos1), (sel2, pos2f, pos2)):
                then(dve.tensor_tensor(rtmp, sel, slotp, ALU.mult))
                then(dve.tensor_reduce(posf[:, :], rtmp, AX.X, ALU.add))
                dve.tensor_copy(pos[:, :], posf[:, :]).then_inc(r_pos, 1)
            then(dve.tensor_tensor(ejc, ce[0:1, :].unsqueeze(1).to_broadcast([1, MT, NE]),
                                   jt[0:1, :].unsqueeze(2).to_broadcast([1, MT, NE]), ALU.is_le))
            then(dve.tensor_reduce(ejf[:, :], ejc, AX.X, ALU.add))
            dve.tensor_scalar(ej_row[:, :], ejf[:, :], float(NE - 1), None, ALU.min).then_inc(r_pos, 1)

            with dve.Fori(0, MT // XB) as i:
                for s in range(XB):
                    dve.wait_ge(row_full, i * XB + (s + ROW_E + 1))
                    dve.wait_ge(w2_in[s], i * 32 + 32)
                    dve.wait_ge(yo_out[s % 2], i * (XB // 2 * 16) + (s // 2 * 16 + 16))
                    dve.tensor_tensor(yo[s % 2][:, :], ROW[s % 2][:, 0:D], b2e[s], ALU.add).then_inc(row_dve, 1)
            with dve.Fori(0, NG) as g:
                dve.wait_ge(fi_in, g * (2 * GT * 16) + 2 * GT * 16)
                dve.wait_ge(out_done, g * (GT * 16) + 16)
                for j in range(GT):
                    dve.scalar_tensor_tensor(u5[:, j, :], es[:, j, :], w1t[:, ds(g * GT + j, 1)], tile(agg, g * GT + j), ALU.mult, ALU.add).then_inc(f_u, 1)
                for j in range(GT):
                    dve.wait_ge(f_u, g * (2 * GT) + j + 1)
                    dve.scalar_tensor_tensor(u5[:, j, :], qe[:, j, :], w2t[:, ds(g * GT + j, 1)], u5[:, j, :], ALU.mult, ALU.add).then_inc(f_u, 1)
                dve.wait_ge(f_u, g * (2 * GT) + 2 * GT)
                stats(lambda j: u5[:, j, :], f_stat, f_aggr, g * GT, st5b, mv5b)
                dve.wait_ge(f_std, g + 1)
                dve.reciprocal(rs5b[:, :], std5b[:, :]).then_inc(f_rstd, 1)
                dve.wait_ge(f_rstd, g + 2)
                dve.wait_ge(f_aggr, g * GT + GT)
                for j in range(GT):
                    dve.tensor_scalar(u5[:, j, :], u5[:, j, :], mv5b[:, j, 0:1], rs5b[:, j:j + 1], ALU.subtract, ALU.mult).then_inc(f_n, 1)
                    dve.wait_ge(f_n, g * (4 * GT) + 4 * j + 1)
                    dve.tensor_tensor(u5[:, j, :], u5[:, j, :], gam_s[:, :], ALU.mult).then_inc(f_n, 1)
                    dve.wait_ge(f_n, g * (4 * GT) + 4 * j + 2)
                    dve.tensor_tensor(u5[:, j, :], u5[:, j, :], bet_s[:, :], ALU.add).then_inc(f_n, 1)
                    dve.wait_ge(f_n, g * (4 * GT) + 4 * j + 3)
                    dve.tensor_tensor(u5[:, j, :], u5[:, j, :], tile(X, g * GT + j), ALU.add).then_inc(f_n, 1)


def kernel(**inputs):
    import numpy as np
    import concourse.bacc as bacc
    from concourse.bass_utils import run_bass_kernel_spmd
    nc = bacc.Bacc("TRN2", target_bir_lowering=False, num_devices=1)
    arrays, args = {}, []
    for name in INPUTS:
        a = np.ascontiguousarray(inputs[name])
        arrays[f"in_{name}"] = a
        args.append(nc.dram_tensor(f"in_{name}", a.shape, mybir.dt.from_np(a.dtype), kind="ExternalInput").ap())
    out = nc.dram_tensor("out_0", inputs["x"].shape, mybir.dt.float32, kind="ExternalOutput").ap()
    build(nc, *args, out)
    result = run_bass_kernel_spmd(nc, [arrays], core_ids=[0])
    return result.results[0]["out_0"]
```

```python
import concourse.bass as bass
from concourse import mybir
from contextlib import ExitStack

INPUTS = ['x', 'src', 'dst', 'edge_attr_3', 'L0_gnn_W1', 'L0_gnn_b1', 'L0_gnn_W2',
          'L0_mix_Wq', 'L0_mix_Wk', 'L0_mix_Wv', 'L0_mix_Wo', 'L0_mix_bo', 'L0_mix_ln1_g', 'L0_mix_ln1_b',
          'L0_mix_W1', 'L0_mix_b1', 'L0_mix_W2', 'L0_mix_b2', 'L0_mix_ln2_g', 'L0_mix_ln2_b',
          'L0_ffn_gate_w', 'L0_ffn_gate_b', 'L0_ffn_w1', 'L0_ffn_b1', 'L0_ffn_w2', 'L0_ffn_b2',
          'L0_ffn_gamma', 'L0_ffn_beta']


def build(nc, x, src, dst, edge_attr, gnn_W1, gnn_b1, gnn_W2,
          Wq, Wk, Wv, Wo, bo, ln1_g, ln1_b, W1, b1, W2, b2, ln2_g, ln2_b,
          gate_w, gate_b, ew1, eb1, ew2, eb2, gamma, beta, out):
    f32, f32r, bf16, i32 = mybir.dt.float32, mybir.dt.float32r, mybir.dt.bfloat16, mybir.dt.int32
    ALU, ACT, AX = mybir.AluOpType, mybir.ActivationFunctionType, mybir.AxisListType
    ds = bass.ds

    N, D = x.shape
    T = 125
    NT = N // T
    GT = 5
    NG = NT // GT
    KD = D // 128
    L = Wq.shape[0]
    H, DH = 8, D // 8
    FF = W1.shape[2]
    NF = FF // 128
    SCALE = DH ** -0.25
    EPS = 1e-5
    LOW = -3.0e38
    PC = ((0, 3), (3, 5))
    E = src.shape[0]
    ET = 125
    ST = 4
    SE = ST * ET
    NS = E // SE
    EP = 100
    EC = NS // EP
    NPAIR = NS + NT - 1
    PG = 2
    NEG = NPAIR // PG
    PQ = NPAIR // EC
    AC = EC * ST
    ROUNDS = -(-NS * NT // NPAIR)
    EA = 3
    NE, F = ew1.shape[0], ew1.shape[2]
    NFE = F // 128
    SL = 128
    MT = (2 * N + NE * (SL - 1)) // SL
    assert N == T * NT and E == SE * NS and NPAIR == PG * NEG == PQ * EC and MT % 4 == 0

    def dram(name, shape, dt):
        return nc.dram_tensor(name, shape, dt, kind="Internal").ap()
    xn_d = dram("xn_d", (N, D), f32)
    P_d = dram("P_d", (N, D), f32)
    attr_d = dram("attr_d", (NPAIR, ST, 32, ET), bf16)
    brow_d = dram("brow_d", (2 * L, 3, D), bf16)
    slot_in = dram("slot_in", (MT * SL, D), f32)
    slot_out = dram("slot_out", (MT * SL, D), f32)

    with ExitStack() as ctx:
        def sb(name, shape, dt=f32):
            return ctx.enter_context(nc.sbuf_tensor(name, shape, dt))

        def over(name, shape, dt):
            with nc.sbuf_tensor(name, shape, dt) as tensor:
                return tensor

        def pb(name, shape, dt=f32):
            return ctx.enter_context(nc.psum_tensor(name, shape, dt))

        def sem(name):
            return ctx.enter_context(nc.semaphore(name))

        X = sb("X", [T, NT * D])
        agg = sb("agg", [T, NT * D])
        ident = sb("ident", [128, 128])
        identb = sb("identb", [128, 128], bf16)
        ones = sb("ones", [128, 128])
        onesb = sb("onesb", [128, 128], bf16)
        iota_n = sb("iota_n", [128, T])
        headmask = sb("headmask", [128, 128])
        epsc = sb("epsc", [128, 1])
        Wq_s, Wk_s, Wv_s, Wo_s = (sb(f"W{n}_s", [128, KD, D]) for n in "qkvo")
        W1_l = over("W1_l", [128, KD, FF], f32r)
        W1_s = sb("W1_s", [128, KD, FF])
        W2_s = sb("W2_s", [128, NF, D])
        lnp = sb("lnp", [128, L * 8])
        b1_s = sb("b1_s", [128, L * NF])
        lnc = sb("lnc", [128, 8])
        b1c = sb("b1c", [128, NF])
        brow = sb("brow", [128, L * 2 * D], bf16)
        W1T = sb("W1T", [128, KD, D])
        W2T = sb("W2T", [128, 2 * KD, D])
        Wst = sb("Wst", [128, 4 * D], bf16)
        hn = sb("hn", [T, GT, D])
        W1_h1 = over("W1_h1", [128, FF], f32r)
        es = sb("es", [T, GT, D])
        qe = sb("qe", [T, GT, D])
        PAD = PC[0][1] * T
        TTW = GT * T + 1
        TTl = over("TTl", [128, KD, TTW], f32r)
        TT = sb("TT", [128, KD, TTW])
        xT_all = over("xT", [128, 2, KD, 128], f32)
        TTh = sb("TTh", [128, KD, TTW], f32r)
        QT = sb("QT", [128, KD, GT * T])
        V5 = sb("V5", [T, GT, KD, 129])
        W1_h0 = over("W1_h0", [128, FF], f32r)
        W1_h = [W1_h0, W1_h1]
        eT = sb("eT", [128, KD, GT * T])
        hid = sb("hid", [128, NF, GT * T])
        M_s = sb("M_s", [128, KD, D])
        st5 = sb("st5", [T, GT, 6])
        mv5 = sb("mv5", [T, GT, 2])
        std5 = sb("std5", [T, GT])
        mvA = sb("mvA", [T, NT, 2])
        stdA = sb("stdA", [T, NT])
        rstd_t = sb("rstd_t", [T, NT])
        st5b = sb("st5b", [T, GT, 6])
        mv5b = sb("mv5b", [T, GT, 2])
        std5b = sb("std5b", [T, GT])
        rs5b = sb("rs5b", [T, GT])
        ctxS = sb("ctxS", [128, KD, 129])
        ctxN = sb("ctxN", [128, KD, 128])
        ctxT = sb("ctxT", [128, KD, 128])
        mO = sb("mO", [128, KD])
        mN = sb("mN", [128, KD])
        pm = sb("pm", [128, KD])
        nb = sb("nb", [128, 2, KD])
        cdiff = sb("cdiff", [128, 2, KD])
        corr = sb("corr", [128, 2, KD])
        rk = sb("rk", [128, KD])
        qm = sb("qm", [T, GT, H])
        qs = sb("qs", [T, GT, H])
        qr = sb("qr", [T, GT, H])
        src_T = sb("src_T", [ET, NPAIR * ST], i32)
        dst_T = sb("dst_T", [ET, NPAIR * ST])
        blk_row = sb("blk_row", [1, NPAIR], i32)
        stage = [sb(f"stage{i}", [ET, PG * ST], i32) for i in range(2)]
        G = sb("G", [ET, PG * ST, D])
        z = sb("z", [ET, 2, 2 * D])
        zr = sb("zr", [ET, PG, 2, 2 * D], f32r)
        zl = sb("zl", [ET, 2, 2 * D], f32r)
        onehot = sb("onehot", [ET, PG, ST, T], f32r)
        aT = sb("aT", [128, PG, ET], bf16)
        cum = sb("cum", [PQ, NS])
        dg = sb("dg", [PQ, NS])
        lo0 = sb("lo0", [PQ, 1])
        pid = sb("pid", [PQ, EC])
        tile_f = sb("tile_f", [PQ, EC])
        tile_i = sb("tile_i", [PQ, EC], i32)
        gsum = sb("gsum", [PQ, EC])
        blk = sb("blk", [PQ, EC])
        blk125 = sb("blk125", [PQ, EC])
        blkc = sb("blkc", [PQ, EC])
        rounds_i = sb("rounds_i", [1, 1], i32)

        bank = [pb(f"bank{i}", [128, 512]) for i in range(8)]
        edge_bank, sum_bank = (bank[1], bank[2]), bank[3]
        RING = [bank[4], bank[6], bank[7]]
        ROW = [bank[5], bank[0]]

        SC = hid[:, :, :].rearrange("p f n -> p (f n)")
        LG = sb("LG", [T, NT * NE])
        dst_tiles = eT[0:EP, :, :].rearrange("p k n -> p (k n)")[:, 0:EC * SE].bitcast(i32)
        n_bc, lo_bc, junk = SC[0:PQ, 0:NS], SC[0:PQ, NS:2 * NS], SC[0:PQ, 2 * NS:3 * NS]
        spread = SC[0:EP, 3 * NS:3 * NS + 2 * EC * EP].rearrange("p (c q) -> p c q", q=EP)
        above = SC[0:EP, 4000:4000 + 2 * EC * (NT - 1)].rearrange("p (c b) -> p c b", b=NT - 1)
        src_rows = SC[0:PQ, 0:EC * SE]
        dst_rows = SC[0:PQ, EC * SE:2 * EC * SE]
        attr_rows = SC[0:PQ, 2 * EC * SE:5 * EC * SE]
        spread_b = eT[0:PQ, :, :].rearrange("p k n -> p (k n)")[:, 0:EC * PQ].rearrange("p (c q) -> p c q", q=PQ)
        part_rows = lambda buf, at: buf[0:PQ].rearrange("p a b -> p (a b)")[:, at:at + 600].bitcast(bf16)[:, 0:9 * ET].rearrange(
            "p (r e) -> p r e", e=ET)
        ATS = [part_rows(hn, 0), part_rows(hn, 600), part_rows(TT, 0), part_rows(TT, 600), part_rows(z, 0)]
        AB = len(ATS)
        AR = [qe[0:PQ, 2 * i:2 * i + 2, :].rearrange("p j d -> p (j d)")[:, 0:EA * ET].rearrange("p (a e) -> p a e", e=ET)
              for i in range(2)]
        arest = M_s[0:PQ, :, :].rearrange("p k d -> p (k d)").bitcast(bf16)[:, 0:5 * ET].rearrange("p (r e) -> p r e", e=ET)
        thr = sb("thr", [EP, NT - 1])
        thr2 = sb("thr2", [1, ROUNDS])
        hl = sb("hl", [EP, 2 * EC])
        hlb = sb("hlb", [EP, 2 * EC])
        rcnt = sb("rcnt", [1, 1])
        rjunk = sb("rjunk", [1, ROUNDS])
        gW1 = W1_s[:, :, 0:D + EA]
        gW2 = W2_s[:, 0:4, :].rearrange("p (k a) d -> p k (a d)", k=KD)
        w4 = sb("w4", [128, KD, 4])
        w4r = sb("w4r", [128, KD, 4])
        wparts = sb("wparts", [128, 3, KD, 4], bf16)
        WS = QT[:, :, :].rearrange("p k n -> p (k n)").bitcast(bf16)[:, 0:KD * 512].rearrange("p (h q r) -> p h q r", h=KD, q=4)
        bparts = sb("bparts", [2 * L, 3, D], bf16)
        HL = SC[0:T, 0:GT * D].rearrange("p (j d) -> p j d", d=D)
        sqj = SC[0:T, GT * D:2 * GT * D].rearrange("p (j d) -> p j d", d=D)
        staged_sums = V5[:, :, :, :].rearrange("p j k n -> p (j k n)")[:, 0:GT * D].rearrange("p (j d) -> p j d", d=D)
        ss = sb("ss", [T, GT])
        nrm = sb("nrm", [T, GT])
        rn = sb("rn", [T, GT])
        gw_s = sb("gw_s", [128, KD, NE])
        gb_s = sb("gb_s", [T, NE])
        gam_s = sb("gam_s", [T, D])
        bet_s = sb("bet_s", [T, D])
        iota_e = sb("iota_e", [T, NE])
        tri = sb("tri", [T, T])
        m1 = sb("m1", [T, NT])
        m2 = sb("m2", [T, NT])
        i1 = sb("i1", [T, NT])
        w1t = sb("w1t", [T, NT])
        w2t = sb("w2t", [T, NT])
        e21 = sb("e21", [T, NT])
        ts3 = lambda k: SC[0:T, 400 * k:400 * k + 400].rearrange("p (t e) -> p t e", e=NE)
        sel1, sel2, rtmp, lg2, mask, tot, cumt, slotp = (ts3(k) for k in range(8))
        nge = SC[0:T, 3200:3200 + NE * NT].rearrange("p (e k) -> p e k", k=NT)
        thr3 = sb("thr3", [T, NT])
        jt = sb("jt", [T, MT])
        ejc = SC[0:1, 3720:3720 + MT * NE].rearrange("p (m e) -> p m e", e=NE)
        te = sb("te", [T, NE])
        ce = sb("ce", [T, NE])
        ste = sb("ste", [T, NE])
        onee = sb("onee", [T, NT])
        ejf = sb("ejf", [1, MT])
        ej_row = sb("ej_row", [1, MT], i32)
        pos1f = sb("pos1f", [T, NT])
        pos2f = sb("pos2f", [T, NT])
        pos1 = sb("pos1", [T, NT], i32)
        pos2 = sb("pos2", [T, NT], i32)
        ps1, ps2 = ([sb(f"ps{k}_{i}", [T, GT], i32) for i in range(2)] for k in (1, 2))
        ZS = [hn, staged_sums]
        XB = 4
        W1e = [W1_s[:, :, F * i:F * i + F] for i in range(2)] + [
            SC[:, KD * F * i:KD * F * (i + 1)].rearrange("p (k f) -> p k f", f=F) for i in range(2)]
        W2e = [W2_s[:, NFE * i:NFE * i + NFE, :] for i in range(2)] + [
            SC[:, 2 * KD * F + NFE * D * i:2 * KD * F + NFE * D * (i + 1)].rearrange("p (c d) -> p c d", d=D) for i in range(2)]
        b1e = [sb(f"b1e{i}", [128, NFE]) for i in range(XB)]
        b2e = [sb(f"b2e{i}", [128, D])[:, :] for i in range(2)] + [eT[:, i, 0:D] for i in range(2)]
        xs = [sb(f"xs{i}", [128, D])[:, :] for i in range(2)] + [TT[:, i, 0:D] for i in range(2)]
        xT = [xT_all[:, i, :, :] for i in range(2)]
        hT = [QT[:, i, 0:NFE * SL].rearrange("p (c n) -> p c n", n=SL) for i in range(2)]
        yo = [sb("yo0", [128, D])[:, :], eT[:, 1, D:2 * D]]
        fo = ZS[1]
        RES = ((es, qe), (hn, G))
        u5 = SC[0:T, 0:GT * D].rearrange("p (j d) -> p j d", d=D)
        zerob = yo[0]
        browf, browr = (xT[i][0:2 * L, :, :].rearrange("p k n -> p (k n)") for i in range(2))

        x_in = [sem(f"x_in{i}") for i in range(NG)]
        gw_in, par_in, dst_in, br_in, late_in = sem("gw_in"), sem("par_in"), sem("dst_in"), sem("br_in"), sem("late_in")
        consts, cdep, wparts_done, ws_done, wT_T, wT_cp = (sem(n) for n in ("consts", "cdep", "wparts_done", "ws_done", "wT_T", "wT_cp"))
        brp_done, brow_out, brow_z = sem("brp_done"), sem("brow_out"), sem("brow_z")
        pid_done, r_mask = sem("pid_done"), sem("r_mask")
        pstat, paggr, p_mv, pstd, prstd, xcopied = (sem(n) for n in ("pstat", "paggr", "p_mv", "pstd", "prstd", "xcopied"))
        p_out = [sem(f"p_out{i}") for i in range(GT)]
        xn_out, arest_out, slots_zero = sem("xn_out"), sem("arest_out"), sem("slots_zero")
        zmade = sem("zmade")
        base_step, bc_ready = sem("base_step"), sem("bc_ready")
        t_step, t_idx, rows_in, t_cast, t_T, t_cp, a_split, rounds_done = (sem(n) for n in (
            "t_step", "t_idx", "rows_in", "t_cast", "t_T", "t_cp", "a_split", "rounds_done"))
        a_out = [sem(f"a_out{i}") for i in range(AB)]
        st_ready, e_done, z_done, r_done, lo_done, oh_done, s_done, acc_done = (sem(n) for n in (
            "st_ready", "e_done", "z_done", "r_done", "lo_done", "oh_done", "s_done", "acc_done"))
        g_in = [sem(f"g_in{i}") for i in range(PG * ST)]
        at_in = [sem(f"at_in{i}") for i in range(PG)]
        settle_pool, settle_dve, settle_act, settle_pe = (sem(f"settle_{n}") for n in ("pool", "dve", "act", "pe"))
        lnc_done = sem("lnc_done")
        ring_full, ring_act, row_full, row_dve = (sem(n) for n in ("ring_full", "ring_act", "row_full", "row_dve"))
        hn_done = sem("hn_done")
        wA_in, wQ_in, wF_in = sem("wA_in"), sem("wQ_in"), sem("wF_in")
        tt_hi, tt_lo, wF_hi, wF_lo = (sem(n) for n in ("tt_hi", "tt_lo", "wF_hi", "wF_lo"))
        a_stat, a_aggr, a_mv, a_std, a_rstd = (sem(n) for n in ("a_stat", "a_aggr", "a_mv", "a_std", "a_rstd"))
        b_stat, b_aggr, b_std, b_rstd = (sem(n) for n in ("b_stat", "b_aggr", "b_std", "b_rstd"))
        l_init, k_max, m_new, nb_done, cd_done, m_cp, corr_done = (sem(n) for n in (
            "l_init", "k_max", "m_new", "nb_done", "cd_done", "m_cp", "corr_done"))
        cn_done, rk_done = sem("cn_done"), sem("rk_done")
        q_max, q_exp, q_sum, q_rec, q_norm = (sem(n) for n in ("q_max", "q_exp", "q_sum", "q_rec", "q_norm"))
        q_in = sem("q_in")
        c_in, c_agg, c_ss, c_nrm, c_rn, c_y, c_stat, c_aggr, c_std, c_rstd, c_zcp = (sem(n) for n in (
            "c_in", "c_agg", "c_ss", "c_nrm", "c_rn", "c_y", "c_stat", "c_aggr", "c_std", "c_rstd", "c_zcp"))
        r_step, r_exp, r_rank, r_pos = (sem(n) for n in ("r_step", "r_exp", "r_rank", "r_pos"))
        xb_done, zs_cp, zs_free, ps_cp = sem("xb_done"), sem("zs_cp"), sem("zs_free"), sem("ps_cp")
        sc_out = [sem(f"sc_out{i}") for i in range(2)]
        xs_in, w1_in, w2_in = ([sem(f"{n}_in{i}") for i in range(XB)] for n in ("xs", "w1", "w2"))
        yo_out = [sem(f"yo_out{i}") for i in range(2)]
        fi_in = [sem(f"fi_in{i}") for i in range(2)]
        f_u, f_n, out_done, fp_cp = (sem(n) for n in ("f_u", "f_n", "out_done", "fp_cp"))

        def tt_cols(j):
            at = j * T + (j >= PC[0][1])
            return slice(at, at + T)

        TT_PIECES = (slice(0, PAD), slice(PAD + 1, TTW))

        def tile(buf, t, n=1):
            return buf[:, ds(t * D, n * D)]

        RING_GA, RING_GB = 2 * GT + 4, 3 * GT + 2 * NF
        ROW_GA, ROW_GB = GT + 2, 3 * GT
        RING_A, RING_L = NT, NG * RING_GA + 1 + NG * RING_GB
        ROW_A, ROW_L = NT, NG * ROW_GA + KD + NG * ROW_GB
        RING_C, ROW_C = RING_A + L * RING_L, ROW_A + L * ROW_L
        RING_E, ROW_E = RING_C + 3 * NT, ROW_C + 2 * NT
        HN_L = 3 * NT
        HN_C = NT + L * HN_L
        EG_FIRST = 2
        EG_A, EG_M = 1, 1 + NG
        EG_B = EG_M + 1
        RING_M, ROW_M = GT + NG * RING_GA, NG * ROW_GA
        RING_B, ROW_B = RING_M + 1, ROW_M + GT + KD
        EG_L = EG_B + 4 * NG
        EG_LAST = EG_FIRST + L * EG_L


        def pe_sums(ge, s):
            nc.tensor.wait_ge(oh_done, ge + 1)
            nc.tensor.wait_ge(acc_done, ge + 1)
            for i in range(ST):
                cols = slice(D * (i % 2), D * (i % 2) + D)
                if i % 2 == 0:
                    nc.tensor.wait_ge(lo_done, ge * 2 + (i // 2 + 3))
                nc.tensor.matmul(sum_bank[0:T, 0:D], onehot[:, s, i, :], zr[:, s, i // 2, cols], start=i == 0, stop=False)
                ins = nc.tensor.matmul(sum_bank[0:T, 0:D], onehot[:, s, i, :], zl[:, i // 2, cols], start=False, stop=i == ST - 1)
            ins.then_inc(s_done, 1)

        def pe_edges(ge, group, s, first=False):
            nc.tensor.wait_ge(at_in[s], group * 16 + 16)
            for k in range(2):
                nc.tensor.wait_ge(z_done, ge * 2 + (k + 3))
                nc.tensor.matmul(edge_bank[k][0:ET, :], aT[:, s, :], Wst[:, 2 * k * D:2 * (k + 1) * D],
                                 start=True, stop=True).then_inc(e_done, 1)
            if not first:
                pe_sums(ge - 1, 1 - s)

        def act_edges(ge, s):
            for k in range(2):
                nc.scalar.wait_ge(z_done, ge * 2 + (k + 5))
                nc.scalar.activation(zr[:, s, k, :], z[:, k, :], ACT.Relu).then_inc(r_done, 1)

        def dve_low(ge, s):
            for k in range(2):
                nc.vector.wait_ge(r_done, ge * 2 + (k + 1))
                nc.vector.scalar_tensor_tensor(zl[:, k, :], z[:, k, :], 0.0, zr[:, s, k, :].bitcast(f32), ALU.max, ALU.subtract).then_inc(lo_done, 1)

        def dve_acc(ge, reg):
            nc.vector.wait_ge(s_done, ge + 3)
            nc.vector.wait_ge(acc_done, ge + 1)
            part = agg[:, ds(reg * D, D)]
            nc.vector.tensor_tensor(part, sum_bank[0:T, 0:D], part, ALU.add).then_inc(acc_done, 1)

        def block_of(e):
            return nc.vector.value_load(blk_row[0:1, ds(e, 1)], min_val=0, max_val=NT - 1)

        def dve_onehot(e, ge, s):
            nc.vector.wait_ge(s_done, ge + 1)
            nc.vector.tensor_tensor(onehot[:, s, :, :], iota_n[0:ET, :].unsqueeze(1).to_broadcast([ET, ST, T]),
                                    dst_T[:, ds(e * ST, ST)].unsqueeze(2).to_broadcast([ET, ST, T]),
                                    ALU.is_equal).then_inc(oh_done, 1)

        def dve_edges(e, ge, group, s, first=False, last=False):
            reg = None if first else block_of(e - 1)
            if first:
                dve_onehot(e, ge, s)
            nc.vector.wait_ge(lo_done, ge * 2 + 2)
            for k in range(2):
                nc.vector.wait_ge(e_done, ge * 2 + (k + 1))
                for j in (ST * s + 2 * k, ST * s + 2 * k + 1):
                    nc.vector.wait_ge(g_in[j], group * 16 + 16)
                nc.vector.tensor_tensor(z[:, k, :], edge_bank[k][0:ET, :],
                                        G[:, ST * s + 2 * k:ST * s + 2 * k + 2, :].rearrange("p j d -> p (j d)"),
                                        ALU.add).then_inc(z_done, 1)
            if not first:
                dve_acc(ge - 1, reg)
            dve_low(ge, s)
            if not last:
                dve_onehot(e + 1, ge + 1, 1 - s)

        def pool_edges(r):
            def group(e, ge, s):
                nc.gpsimd.tensor_copy(stage[s][:, :], src_T[:, ds(e * (PG * ST), PG * ST)]).then_inc(st_ready, 1)
                v = nc.gpsimd.snap(ge + 1)
                nc.gpsimd.wait_ge(st_ready, v)
                nc.gpsimd.sem_inc(settle_pool, 1)
                for j in range(PG * ST):
                    if j % 2 == 0:
                        v = nc.gpsimd.snap(ge * (2 * PG) + (j // 2 + 1))
                        nc.gpsimd.wait_ge(z_done, v)
                        nc.gpsimd.sem_inc(settle_pool, 1)
                    nc.gpsimd.indirect_dma_start(G[:, j, :], None, P_d[:, :],
                                                 bass.IndirectOffsetOnAxis(ap=stage[s][:, j:j + 1], axis=0)).then_inc(g_in[j], 16)
            with nc.gpsimd.Fori(0, NEG // 2) as i:
                for s in range(2):
                    group(i * 2 + s, i * 2 + s + r * NEG, s)

        def sp_attr(ge, e, s, first=False):
            if not first:
                nc.sync.wait_ge(e_done, ge * 2 - 2)
            nc.sync.dma_start(aT[:, s, :], attr_flat[ds(e * 128, 128), :]).then_inc(at_in[s], 16)

        attr_flat = attr_d.rearrange("q i r e -> (q i r) e")


        def dve_tables_a(r):
            ts = [0]

            def step(ins):
                ts[0] += 1
                ins.then_inc(t_step, 1)
                nc.vector.wait_ge(t_step, r * (2 * EC + 2) + ts[0])

            if not isinstance(r, int):
                nc.vector.tensor_scalar(pid[:, :], pid[:, :], float(NPAIR), None, ALU.add).then_inc(pid_done, 1)
                nc.vector.wait_ge(pid_done, r)
            for c in range(EC):
                step(nc.vector.tensor_scalar(junk, cum[:, :], pid[:, c:c + 1], None, ALU.is_le, ALU.add, accum_out=tile_f[:, c:c + 1]))
                step(nc.vector.scalar_tensor_tensor(junk, cum[:, :], pid[:, c:c + 1], dg[:, :], ALU.is_le, ALU.mult,
                                                    accum_out=gsum[:, c:c + 1]))
            nc.vector.tensor_scalar(tile_i[:, :], tile_f[:, :], float(NS - 1), None, ALU.min).then_inc(t_idx, 1)
            step(nc.vector.scalar_tensor_tensor(blk[:, :], gsum[:, :], lo0[:, :], pid[:, :], ALU.add, ALU.add))
            nc.vector.tensor_scalar(blk125[:, :], blk[:, :], float(T), None, ALU.mult)
            step(nc.vector.tensor_scalar(blkc[:, :], blk[:, :], float(NT - 1), None, ALU.min))
            nc.vector.tensor_tensor(spread_b, ident[0:PQ, 0:PQ].unsqueeze(1).to_broadcast([PQ, EC, PQ]),
                                    blkc[:, :].unsqueeze(2).to_broadcast([PQ, EC, PQ]), ALU.mult).then_inc(t_cast, 1)

        def dve_tables_b(r):
            nc.vector.wait_ge(rows_in, r * (3 * EC * 16) + 3 * EC * 16)
            nc.vector.tensor_copy(src_rows, src_rows.bitcast(i32)).then_inc(t_cast, 1)
            nc.vector.tensor_tensor(dst_rows.rearrange("p (c e) -> p c e", e=SE),
                                    dst_rows.bitcast(i32).rearrange("p (c e) -> p c e", e=SE),
                                    blk125[:, :].unsqueeze(2).to_broadcast([PQ, EC, SE]), ALU.subtract).then_inc(t_cast, 1)
            rows = attr_rows.rearrange("p (c e a) -> p c a e", e=ET, a=EA)
            for c in range(AC):
                at, ax, ar = rows[:, c], ATS[c % AB], AR[c % 2]
                if c >= AB:
                    nc.vector.wait_ge(a_out[c % AB], r * (len(range(c % AB, AC, AB)) * 48) + 48)
                nc.vector.tensor_copy(ax[:, 0:3, :], at).then_inc(a_split, 1)
                nc.vector.wait_ge(a_split, r * (4 * AC) + 4 * c + 1)
                nc.vector.tensor_tensor(ar, at, ax[:, 0:3, :], ALU.subtract).then_inc(a_split, 1)
                nc.vector.wait_ge(a_split, r * (4 * AC) + 4 * c + 2)
                nc.vector.tensor_copy(ax[:, 3:6, :], ar).then_inc(a_split, 1)
                nc.vector.wait_ge(a_split, r * (4 * AC) + 4 * c + 3)
                nc.vector.tensor_tensor(ax[:, 6:9, :], ar, ax[:, 3:6, :], ALU.subtract).then_inc(a_split, 1)

        def pool_tables_a(r):
            v = nc.gpsimd.snap(r + 1) if not isinstance(r, int) else r + 1
            nc.gpsimd.wait_ge(t_idx, v)
            nc.gpsimd.sem_inc(settle_pool, 1)
            for c in range(EC):
                for rows, table, w in ((src_rows.bitcast(i32), src.rearrange("(t e) -> t e", e=SE), SE),
                                       (dst_rows.bitcast(i32), dst.rearrange("(t e) -> t e", e=SE), SE),
                                       (attr_rows, edge_attr.rearrange("(t e) a -> t (e a)", e=SE), SE * EA)):
                    nc.gpsimd.indirect_dma_start(rows[:, c * w:(c + 1) * w], None, table,
                                                 bass.IndirectOffsetOnAxis(ap=tile_i[:, c:c + 1], axis=0)).then_inc(rows_in, 16)
        def pe_tables(r):
            nc.tensor.wait_ge(t_cast, r * 3 + 1)
            flat = spread_b.rearrange("p c q -> p (c q)")
            nc.tensor.matmul(bank[6][0:1, 0:NPAIR], ones[0:PQ, 0:1], flat, start=True, stop=True).then_inc(t_T, 1)
            for b, rows in ((1, src_rows), (3, dst_rows)):
                nc.tensor.wait_ge(t_cast, r * 3 + 2 + b // 2)
                for c in range(AC):
                    ins = nc.tensor.transpose(bank[b + c // ST][0:ET, PQ * (c % ST):PQ * (c % ST) + PQ], rows[:, c * ET:(c + 1) * ET],
                                              ident[0:PQ, 0:PQ])
                ins.then_inc(t_T, 1)

        def act_tables(r):
            nc.scalar.wait_ge(t_T, r * 3 + 1)
            nc.scalar.activation(blk_row[0:1, :], bank[6][0:1, 0:NPAIR], ACT.Copy).then_inc(t_cp, 1)
            for n, (b, to) in enumerate(((1, src_T), (3, dst_T))):
                nc.scalar.wait_ge(t_T, r * 3 + 2 + n)
                for c in range(EC):
                    nc.scalar.activation(to[:, ST * PQ * c:ST * PQ * (c + 1)].rearrange("p (q i) -> p i q", i=ST),
                                         bank[b + c][0:ET, 0:ST * PQ].rearrange("p (i q) -> p i q", i=ST), ACT.Copy).then_inc(t_cp, 1)

        def sp_tables(r):
            by_tile = attr_d.rearrange("(c q) i r e -> c i q (r e)", q=PQ)
            for c in range(AC):
                nc.sync.wait_ge(a_split, r * (4 * AC) + 4 * c + 4)
                for i in range(3):
                    nc.sync.dma_start(by_tile[c // ST, c % ST][:, 9 * i * ET:9 * (i + 1) * ET],
                                      ATS[c % AB].rearrange("p r e -> p (r e)")).then_inc(a_out[c % AB], 16)
            for i in range(AB):
                nc.sync.wait_ge(a_out[i], r * (len(range(i, AC, AB)) * 48) + len(range(i, AC, AB)) * 48)


        def more_rounds(eng, tables, first, middle, last):
            eng.wait_ge(rounds_done, 1)
            rounds = eng.value_load(rounds_i[0:1, 0:1], min_val=1, max_val=ROUNDS)
            with eng.If(rounds > 1):
                with eng.Fori(1, rounds) as r:
                    tables(r)
                    first(r)
                    if middle is not None:
                        with eng.Fori(1, NEG - 1) as e:
                            middle(e, r * NEG + e)
                    last(r)

        block = ctx.enter_context(nc.Block())

        @block.sync
        def _(sp):
            sp.dma_start(gW1, gnn_W1.rearrange("(h p) f -> p h f", p=128)).then_inc(gw_in, 16)
            sp.dma_start(gW2, gnn_W2.rearrange("(h p) f -> p h f", p=128)).then_inc(gw_in, 16)
            with nc.allow_non_contiguous_dma(reason="short vectors to columns"):
                sp.dma_start(w4[:, :, 3:4].squeeze(2), gnn_b1.rearrange("(h p) -> p h", p=128)).then_inc(gw_in, 16)
            sp.dma_start(dst_tiles.rearrange("p (c e) -> p c e", e=SE), dst.rearrange("(c p e) -> p c e", p=EP, e=SE)).then_inc(dst_in, 16)
            for g in range(NG):
                sp.dma_start(X[:, g * GT * D:(g + 1) * GT * D].rearrange("p (t d) -> p t d", d=D),
                             x[g * GT * T:(g + 1) * GT * T, :].rearrange("(t p) d -> p t d", p=T)).then_inc(x_in[g], 16)
            sp.dma_start(browf[0:L, :], bo).then_inc(br_in, 16)
            sp.dma_start(browf[L:2 * L, :], b2).then_inc(br_in, 16)
            lnv = lnp[:, :].rearrange("p (l w k) -> p l w k", l=L, w=4)
            with nc.allow_non_contiguous_dma(reason="short vectors to columns"):
                for w, v in enumerate((ln1_g, ln1_b, ln2_g, ln2_b)):
                    for l in range(L):
                        sp.dma_start(lnv[:, l, w, :], v[l, :].rearrange("(k p) -> p k", p=128)).then_inc(par_in, 16)
                for l in range(L):
                    sp.dma_start(b1_s[:, l * NF:(l + 1) * NF], b1[l, :].rearrange("(f p) -> p f", p=128)).then_inc(par_in, 16)
            sp.wait_ge(brp_done, 4)
            sp.dma_start(brow_d, bparts[:, :, :]).then_inc(brow_out, 16)
            sp.wait_ge(brow_out, 16)
            sp.wait_ge(brow_z, 1)
            for l in range(L):
                for w in range(2):
                    sp.dma_start(brow[0:3, (2 * l + w) * D:(2 * l + w + 1) * D], brow_d[w * L + l]).then_inc(brow_out, 16)
            sp.dma_start(gw_s[:, :, :], gate_w.rearrange("(k p) e -> p k e", p=128)).then_inc(late_in, 16)
            sp.dma_start(gb_s[:, :], gate_b.unsqueeze(0).to_broadcast([T, NE])).then_inc(late_in, 16)
            sp.dma_start(gam_s[:, :], gamma.unsqueeze(0).to_broadcast([T, D])).then_inc(late_in, 16)
            sp.dma_start(bet_s[:, :], beta.unsqueeze(0).to_broadcast([T, D])).then_inc(late_in, 16)
            sp.wait_ge(zmade, 2)
            for c in range(AC):
                sp.dma_start(attr_d.rearrange("(c q) i r e -> c i q (r e)", q=PQ)[c // ST, c % ST][:, 27 * ET:32 * ET],
                             arest[:, :, :].rearrange("p r e -> p (r e)")).then_inc(arest_out, 16)
            sp.wait_ge(zmade, 3)
            for i in range(8):
                sp.dma_start(slot_in.rearrange("(a i p) d -> i p a d", i=8, p=128)[i],
                             zerob[:, :].unsqueeze(1).to_broadcast([128, MT // 8, D])).then_inc(slots_zero, 16)
            def load(dst_ap, src_ap, s):
                sp.dma_start(dst_ap, src_ap).then_inc(s, 16)

            def attr_group(group, e):
                for s in range(PG):
                    sp_attr(group * PG + s, e * PG + s, s)

            def weights_A(l):
                load(Wk_s[:, :, :], Wk[ds(l, 1)].rearrange("o (k p) d -> p (o k) d", p=128), wA_in)
                load(Wv_s[:, :, :], Wv[ds(l, 1)].rearrange("o (k p) d -> p (o k) d", p=128), wA_in)

            def weights_B(l):
                load(Wq_s[:, :, :], Wq[ds(l, 1)].rearrange("o (k p) d -> p (o k) d", p=128), wQ_in)
                load(Wo_s[:, :, :], Wo[ds(l, 1)].rearrange("o (k p) d -> p (o k) d", p=128), wQ_in)
                load(W1_s[:, :, :], W1[ds(l, 1)].rearrange("o (k p) d -> p (o k) d", p=128), wF_in)
                load(W2_s[:, :, :], W2[ds(l, 1)].rearrange("o (k p) d -> p (o k) d", p=128), wF_in)
            weights_A(0)
            sp.wait_ge(wT_cp, 3)
            sp.wait_ge(wparts_done, 1)
            weights_B(0)
            with sp.Fori(0, NG) as g:
                for j in range(GT):
                    sp.wait_ge(row_dve, g * GT + j + 2)
                    sp.dma_start(P_d[ds((g * GT + j) * T, T), :], es[:, j, :]).then_inc(p_out[j], 16)
            sp_tables(0)
            sp.wait_ge(xcopied, NT + GT)
            sp.dma_start(xn_d.rearrange("(t p) d -> p t d", p=T), X[:, :].rearrange("p (t d) -> p t d", d=D)).then_inc(xn_out, 16)
            sp.wait_ge(arest_out, AC * 16)

            for e in range(PG):
                sp_attr(e, e, e, first=True)
            with sp.Fori(1, EG_FIRST + 1) as g:
                attr_group(g, g)

            def layer(l, last=False):
                with sp.Fori(1, EG_B + 1) as g:
                    e = l * EG_L + g + EG_FIRST
                    attr_group(e, e)
                if not last:
                    sp.wait_ge(cn_done, l + 2)
                    weights_A(l + 1)
                with sp.Fori(EG_B + 1, EG_L + 1) as g:
                    e = l * EG_L + g + EG_FIRST
                    attr_group(e, e)
                if not last:
                    sp.wait_ge(row_full, l * ROW_L + (ROW_A + ROW_L))
                    weights_B(l + 1)
            with sp.Fori(0, L - 1) as l:
                layer(l)
            layer(L - 1, last=True)
            with sp.Fori(EG_LAST + 1, NEG) as g:
                attr_group(g, g)
            more_rounds(sp, sp_tables, lambda r: attr_group(r * NEG, 0), lambda e, ge: attr_group(ge, e),
                        lambda r: attr_group(r * NEG + (NEG - 1), NEG - 1))
            def load_rows(to, rows, g, done):
                sp.dma_start(to[:, :, :], rows[ds(g * GT * T, GT * T), :].rearrange("(t p) d -> p t d", p=T)).then_inc(done, 16)
            sp.wait_ge(row_dve, ROW_C + 1)
            load_rows(es, xn_d, 0, c_in)
            load_rows(qe, x, 0, q_in)
            with sp.Fori(0, NG - 1) as g:
                sp.wait_ge(ring_full, RING_C + 2 * GT + g * (3 * GT))
                load_rows(es, xn_d, g + 1, c_in)
                sp.wait_ge(c_y, g * (2 * GT) + GT)
                load_rows(qe, x, g + 1, q_in)

            def store_tile(m, s):
                sp.dma_start(slot_out[ds(m * SL, SL), :], yo[s][:, :]).then_inc(yo_out[s], 16)

            def expert_tile(m, s, first=False):
                ex = sp.value_load(ej_row[0:1, ds(m, 1)], min_val=0, max_val=NE - 1)
                if not first:
                    sp.wait_ge(row_dve, m + (ROW_E + 2 - XB))
                    store_tile(m - XB, s % 2)
                load(xs[s], slot_in[ds(m * SL, SL), :], xs_in[s])
                load(W1e[s], ew1[ds(ex, 1)].rearrange("o (k p) f -> p (o k) f", p=128), w1_in[s])
                load(b1e[s][:, :], eb1[ds(ex, 1), :].rearrange("o (p c) -> p (o c)", c=NFE), w1_in[s])
                load(W2e[s], ew2[ds(ex, 1)].rearrange("o (p c) d -> p (o c) d", c=NFE), w2_in[s])
                load(b2e[s], eb2[ds(ex, 1), :].to_broadcast([128, D]), w2_in[s])
            sp.wait_ge(r_pos, 3)
            for s in range(2):
                sp.wait_ge(sc_out[s], (NG + 1 - s) // 2 * (2 * GT * 16))
            for s in range(XB):
                expert_tile(s, s, first=True)
            with sp.Fori(1, MT // XB) as i:
                for s in range(XB):
                    expert_tile(i * XB + s, s)
            for s in range(XB):
                sp.wait_ge(row_dve, MT + (ROW_E + 2 - XB + s))
                store_tile(MT - XB + s, s % 2)
            with sp.Fori(0, NG) as g:
                for j in range(GT):
                    sp.wait_ge(f_n, g * (2 * GT) + (GT + j + 2))
                    sp.dma_start(out[ds((g * GT + j) * T, T), :], fo[:, j, :]).then_inc(out_done, 16)
            sp.wait_ge(out_done, NT * 16 + 16)

        @block.gpsimd
        def _(pool):
            for t, v in ((ident, 0.0), (identb, 0.0), (headmask, 1.0), (tri, 1.0)):
                pool.memset(t[:, :], v).then_inc(cdep, 1)
            pool.memset(ones[:, :], 1.0).then_inc(consts, 1)
            pool.memset(onesb[:, :], 1.0).then_inc(consts, 1)
            pool.memset(epsc[:, :], EPS).then_inc(consts, 1)
            pool.memset(V5[:, :, :, 128:129], 1.0).then_inc(consts, 1)
            pool.memset(onee[:, :], 1.0).then_inc(consts, 1)
            pool.wait_ge(cdep, 4)
            for t in (ident, identb):
                pool.affine_select(out=t[:, :], in_=t[:, :], compare_op=ALU.not_equal, fill=1.0, base=0,
                                   pattern=[[-1, 128]], channel_multiplier=1).then_inc(consts, 1)
            pool.affine_select(out=tri[:, :], in_=tri[:, :], compare_op=ALU.is_gt, fill=0.0, base=0,
                               pattern=[[1, T]], channel_multiplier=-1).then_inc(consts, 1)
            hm = headmask[:, :].rearrange("p (c d) -> p c d", d=DH)
            pool.affine_select(out=hm, in_=hm, compare_op=ALU.is_ge, fill=0.0, base=0,
                               pattern=[[-DH, 128 // DH], [0, DH]], channel_multiplier=1).then_inc(cdep, 1)
            pool.wait_ge(cdep, 5)
            pool.affine_select(out=hm, in_=hm, compare_op=ALU.is_ge, fill=0.0, base=DH - 1,
                               pattern=[[DH, 128 // DH], [0, DH]], channel_multiplier=-1).then_inc(consts, 1)
            pool.iota(iota_n[:, :], [[1, T]], base=0, channel_multiplier=0, allow_small_or_imprecise_dtypes=True).then_inc(consts, 1)
            pool.iota(iota_e[:, :], [[1, NE]], base=-NE, channel_multiplier=0, allow_small_or_imprecise_dtypes=True).then_inc(consts, 1)
            pool.iota(thr[:, :], [[T, NT - 1]], base=T, channel_multiplier=0, allow_small_or_imprecise_dtypes=True).then_inc(consts, 1)
            pool.iota(thr2[:, :], [[NPAIR, ROUNDS]], base=0, channel_multiplier=0, allow_small_or_imprecise_dtypes=True).then_inc(consts, 1)
            pool.iota(thr3[:, :], [[SL, NT]], base=0, channel_multiplier=0, allow_small_or_imprecise_dtypes=True).then_inc(consts, 1)
            pool.iota(jt[:, :], [[1, MT]], base=0, channel_multiplier=0, allow_small_or_imprecise_dtypes=True).then_inc(consts, 1)
            pool.iota(pid[:, :], [[PQ, EC]], base=0, channel_multiplier=1, allow_small_or_imprecise_dtypes=True).then_inc(consts, 1)
            pool.memset(brow[:, :], 0.0).then_inc(brow_z, 1)
            pool.memset(arest[:, 0:3, :], 1.0).then_inc(zmade, 1)
            pool.memset(arest[:, 3:5, :], 0.0).then_inc(zmade, 1)
            pool.memset(zerob[:, :], 0.0).then_inc(zmade, 1)
            pool.memset(agg[:, :], 0.0).then_inc(consts, 1)
            pool_tables_a(0)
            pool.memset(WS[:, :, :, :], 0.0).then_inc(cdep, 1)
            pool.wait_ge(cdep, 6)
            pool.wait_ge(wparts_done, 5)
            for q in range(4):
                for j in range(3):
                    for h in range(KD):
                        o = 32 * q + 9 * j
                        pool.tensor_copy(WS[:, h, q, o:o + 9].rearrange("p (i c) -> p i c", c=EA),
                                         wparts[:, j, h, 0:EA].unsqueeze(1).to_broadcast([128, 3, EA])).then_inc(ws_done, 1)
                        pool.tensor_copy(WS[:, h, q, 32 * q + 27 + j:32 * q + 28 + j], wparts[:, j, h, EA:EA + 1]).then_inc(ws_done, 1)
            for j in range(GT):
                pool.wait_ge(p_out[j], 16 * NG + 16)
            pool.wait_ge(t_cp, 5)
            pool_edges(0)
            more_rounds(pool, pool_tables_a, pool_edges, None, lambda r: None)
            pool.wait_ge(r_pos, 2)
            pool.wait_ge(slots_zero, 8 * 16)
            pool.sem_inc(zs_free, 2)

            def scatter(g, s, i=None, first=False):
                for pos, to in ((pos1, ps1[s]), (pos2, ps2[s])):
                    pool.tensor_copy(to[:, :], pos[:, ds(g * GT, GT)]).then_inc(ps_cp, 1)
                v = pool.snap(g * 2 + 2) if not first else 2
                pool.wait_ge(ps_cp, v)
                pool.sem_inc(settle_pool, 1)
                v = pool.snap(g + 1) if not first else 1
                pool.wait_ge(zs_cp, v)
                pool.sem_inc(settle_pool, 1)
                for j in range(GT):
                    for to in (ps1[s], ps2[s]):
                        pool.indirect_dma_start(slot_in[:, :], bass.IndirectOffsetOnAxis(ap=to[:, j:j + 1], axis=0),
                                                ZS[s][:, j, :], None).then_inc(sc_out[s], 16)
                if not first:
                    v = pool.snap((i + 1) * (2 * GT * 16))
                    pool.wait_ge(sc_out[1 - s], v)
                    pool.sem_inc(zs_free, 1)
            scatter(0, 0, first=True)
            with pool.Fori(0, NG // 2) as i:
                scatter(i * 2 + 1, 1, i)
                scatter(i * 2 + 2, 0, i)
            pool.wait_ge(late_in, 64)
            pool.tensor_tensor(X[:, :].rearrange("p (t d) -> p t d", d=D), X[:, :].rearrange("p (t d) -> p t d", d=D),
                               bet_s[:, :].unsqueeze(1).to_broadcast([T, NT, D]), ALU.add).then_inc(xb_done, 1)
            for s in range(2):
                pool.wait_ge(sc_out[s], (NG + 1 - s) // 2 * (2 * GT * 16))
            for s in range(2):
                pool.wait_ge(yo_out[s], MT // 2 * 16 + 16)

            def value(v):
                return v if isinstance(v, int) else pool.snap(v)

            def results(g, s):
                v = value(g * (2 * GT) + 2)
                pool.wait_ge(f_u, v)
                pool.sem_inc(settle_pool, 1)
                for pos, to in ((pos1, ps1[s]), (pos2, ps2[s])):
                    pool.tensor_copy(to[:, :], pos[:, ds(g * GT, GT)]).then_inc(fp_cp, 1)
                v = value(g * 2 + 2)
                pool.wait_ge(fp_cp, v)
                pool.sem_inc(settle_pool, 1)
                for j in range(GT):
                    v = value(g * (2 * GT) + 2 * j + 2)
                    pool.wait_ge(f_u, v)
                    pool.sem_inc(settle_pool, 1)
                    for to, rows in zip((ps1[s], ps2[s]), RES[s]):
                        pool.indirect_dma_start(rows[:, j, :], None, slot_out[:, :],
                                                bass.IndirectOffsetOnAxis(ap=to[:, j:j + 1], axis=0)).then_inc(fi_in[s], 16)
            with pool.Fori(0, NG // 2) as i:
                for s in range(2):
                    results(i * 2 + s, s)
            results(NG - 1, 0)

        @block.scalar
        def _(act):
            act.sem_inc(ring_act, 1)
            act.sem_inc(xcopied, GT)
            act.wait_ge(wT_T, 1)
            act.activation(W1T[:, :, :].rearrange("p k d -> p (k d)"), bank[6][:, :], ACT.Copy).then_inc(wT_cp, 1)
            for i in range(2):
                act.wait_ge(wT_T, 2 + i)
                act.activation(W2T[:, 2 * i:2 * i + 2, :].rearrange("p k d -> p (k d)"), bank[7 if i == 0 else 5][:, :], ACT.Copy).then_inc(wT_cp, 1)

            def std(to, var, s):
                act.activation(to, var, ACT.Sqrt, bias=epsc[0:T, :]).then_inc(s, 1)

            def features(u, loc, j, gain, shift):
                act.wait_ge(ring_full, u + 1)
                for k in range(KD):
                    ins = act.activation(TT[:, k, tt_cols(j)], RING[loc % 3][:, 128 * k:128 * k + T], ACT.Identity,
                                         bias=shift(k), scale=gain(k))
                ins.then_inc(ring_act, 1)

            def copy_tile(u, loc, to, w, parts=128):
                act.wait_ge(ring_full, u + 1)
                act.activation(to, RING[loc % 3][0:parts, 0:256].rearrange("p (k n) -> p k n", k=KD)[:, :, 0:w], ACT.Copy).then_inc(ring_act, 1)

            act.wait_ge(consts, 16)
            act.wait_ge(p_mv, NG)
            std(stdA[:, :], mvA[:, :, 1], pstd)
            with act.Fori(0, NG) as g:
                for j in range(GT):
                    act.wait_ge(hn_done, g * GT + j + 1)
                    act.sem_inc(settle_act, 1)
                    act.activation(tile(X, g * GT + j), hn[:, j, :], ACT.Copy).then_inc(xcopied, 1)
                    copy_tile(g * GT + j, j, TT[:, :, j * T:(j + 1) * T], T)
            act.wait_ge(ws_done, 49)
            act.activation(Wst[:, :], bank[5][:, :].bitcast(bf16), ACT.Copy).then_inc(wT_cp, 1)
            act_tables(0)
            act.wait_ge(par_in, (4 * L + L) * 16)

            def edges(group, s):
                act_edges(group * PG + s, s)

            def both(group):
                for s in range(PG):
                    edges(group, s)
            for e in range(EG_FIRST):
                both(e)

            with act.Fori(0, L) as l:
                act.wait_ge(ring_act, l * RING_L + (RING_A + 1))
                act.sem_inc(settle_act, 1)
                act.activation(lnc[:, :], lnp[:, ds(l * 8, 8)], ACT.Copy).then_inc(lnc_done, 1)
                act.activation(b1c[:, :], b1_s[:, ds(l * NF, NF)], ACT.Copy).then_inc(lnc_done, 1)
                act.wait_ge(lnc_done, l * 2 + 2)
                act.sem_inc(settle_act, 1)

                def ln_col(w, k):
                    return lnc[:, 2 * w + k:2 * w + k + 1]
                act.wait_ge(a_mv, l * NG + NG)
                std(stdA[:, :], mvA[:, :, 1], a_std)

                def normalised(u, loc):
                    for j in range(GT):
                        features(u + j, loc + j, j, lambda k: ln_col(0, k), lambda k: ln_col(1, k))
                normalised(l * RING_L + RING_A, 0)
                both(l * EG_L + EG_FIRST)
                with act.Fori(0, NG) as g:
                    eg = l * EG_L + g + (EG_FIRST + EG_A)
                    u0, q0 = l * RING_L + g * RING_GA + (RING_A + GT), l * (2 * NG) + g * 2
                    for pc, (a, b) in enumerate(PC):
                        act.wait_ge(cd_done, q0 + pc + 1)
                        act.activation(corr[:, pc, :], cdiff[:, pc, :], ACT.Exp).then_inc(corr_done, 1)
                        for h in range(KD):
                            act.activation(eT[:, h, a * T:b * T], RING[(2 * pc + h) % 3][:, 0:(b - a) * T], ACT.Exp,
                                           bias=nb[:, pc, h:h + 1], scale=SCALE).then_inc(ring_act, 1)
                    normalised(u0 + 4, 4)
                    edges(eg, 0)
                    for j in range(GT):
                        copy_tile(u0 + GT + 4 + j, GT + 4 + j, es[:, j, :].rearrange("p (k n) -> p k n", k=KD), 128, T)
                    edges(eg, 1)

                def q_softmax(r, n):
                    act.wait_ge(row_dve, r + GT + 1)
                    act.sem_inc(settle_act, 1)
                    act.activation(qe[:, :, :], qe[:, :, :], ACT.Exp, scale=SCALE).then_inc(q_exp, 1)
                uM, rM = l * RING_L + (RING_A + RING_M), l * ROW_L + (ROW_A + ROW_M)
                edges(l * EG_L + (EG_FIRST + EG_M), 0)
                copy_tile(uM, 0, ctxT[:, :, :], 128)
                act.wait_ge(wF_in, l * 32 + 32)
                act.sem_inc(settle_act, 1)
                for k in range(KD):
                    act.activation(W1_h[k][:, :], W1_s[:, k, :], ACT.Copy).then_inc(wF_hi, 1)
                q_softmax(rM, l * NG)
                edges(l * EG_L + (EG_FIRST + EG_M), 1)

                def second(g, last=False):
                    n0, u0 = l * NT + g * GT, l * RING_L + g * RING_GB + (RING_A + RING_B)
                    r0 = l * ROW_L + g * ROW_GB + (ROW_A + ROW_B)
                    step = lambda i: edges(l * EG_L + g * 4 + (EG_FIRST + EG_B + i // PG), i % PG)
                    for j in range(GT):
                        copy_tile(u0 + j, j, QT[:, :, j * T:(j + 1) * T], T)
                    act.wait_ge(b_aggr, n0 + GT)
                    std(std5b[:, :], mv5b[:, :, 1], b_std)
                    for j in range(GT):
                        features(u0 + GT + j, GT + j, j, lambda k: ln_col(2, k), lambda k: ln_col(3, k))
                    step(0)
                    for f in range(NF):
                        for pc, (a, b) in enumerate(PC):
                            loc = 2 * GT + 2 * f + pc
                            act.wait_ge(ring_full, u0 + loc + 1)
                            act.activation(hid[:, f, a * T:b * T], RING[loc % 3][:, 0:(b - a) * T], ACT.Gelu,
                                           bias=b1c[:, f:f + 1]).then_inc(ring_act, 1)
                        if f % 2 == 0:
                            step(f // 2 + 1)
                    if not last:
                        normalised(u0 + 2 * GT + 2 * NF, 2 * GT + 2 * NF)
                    step(5)
                    if not last:
                        q_softmax(r0 + GT, l * NG + g + 1)
                    step(6)
                    step(7)
                with act.Fori(0, NG - 1) as g:
                    second(g)
                second(NG - 1, last=True)
            with act.Fori(EG_LAST, NEG) as e:
                both(e)
            more_rounds(act, act_tables, lambda r: both(r * NEG), lambda e, ge: both(ge), lambda r: both(r * NEG + (NEG - 1)))

            def rows_T(u):
                for j in range(GT):
                    copy_tile(u + 2 * j, 2 * j, TT[:, :, j * T:(j + 1) * T], T)
                    copy_tile(u + 2 * j + 1, 2 * j + 1, QT[:, :, j * T:(j + 1) * T], T)

            def lengths(g, r):
                for j in range(GT):
                    act.wait_ge(row_dve, r + j + 2)
                    act.activation(sqj[:, j, :], HL[:, j, :], ACT.Square, accum_out=ss[:, j:j + 1]).then_inc(c_ss, 1)
                act.wait_ge(c_ss, g * GT + GT)
                act.activation(nrm[:, :], ss[:, :], ACT.Sqrt).then_inc(c_nrm, 1)

            def deviation(g):
                act.wait_ge(c_aggr, g * GT + GT)
                std(std5[:, :], mv5[:, :, 1], c_std)

            def gate_T(g, u, loc):
                for j in range(GT):
                    copy_tile(u + j, loc + j, eT[:, :, j * T:(j + 1) * T], T)
                act.activation(tile(agg, g * GT, GT), hn[:, :, :].rearrange("p j d -> p (j d)"), ACT.Copy).then_inc(c_zcp, 1)
            act.sem_inc(c_zcp, 1)
            rows_T(RING_C)
            lengths(0, ROW_C)
            with act.Fori(0, NG - 1) as g:
                u0 = g * (3 * GT) + (RING_C + 2 * GT)
                rows_T(u0)
                deviation(g)
                lengths(g + 1, g * (2 * GT) + (ROW_C + GT))
                gate_T(g, u0 + 2 * GT, 2 * GT)
            deviation(NG - 1)
            gate_T(NG - 1, RING_E - GT, 0)
            act.wait_ge(r_mask, 1)
            act.activation(e21[:, :], e21[:, :], ACT.Exp).then_inc(r_exp, 1)
            act.wait_ge(c_zcp, NG + 1)
            def staged(g, s):
                act.wait_ge(zs_free, g + 1)
                act.sem_inc(settle_act, 1)
                act.activation(ZS[s][:, :, :].rearrange("p j d -> p (j d)"), tile(agg, g * GT, GT), ACT.Copy).then_inc(zs_cp, 1)
            with act.Fori(0, NG // 2) as i:
                for s in range(2):
                    staged(i * 2 + s, s)
            staged(NG - 1, 0)

            def slots_T(u, s):
                act.wait_ge(ring_full, u + 1)
                act.activation(xT[s][:, :, :], RING[0][:, 0:KD * SL].rearrange("p (k n) -> p k n", k=KD), ACT.Copy).then_inc(ring_act, 1)

            def hidden(u, s):
                act.wait_ge(ring_full, u + 1)
                for c in range(NFE):
                    ins = act.activation(hT[s % 2][:, c, :], RING[1 + s % 2][:, c * SL:(c + 1) * SL], ACT.Relu, bias=b1e[s][:, c:c + 1])
                ins.then_inc(ring_act, 1)

            def expert_tile(m, s, last=False):
                u = m * 2 + (RING_E + 1)
                if not last:
                    slots_T(u, (s + 1) % 2)
                hidden(u + (0 if last else 1), s)
            slots_T(RING_E, 0)
            expert_tile(0, 0)
            with act.Fori(0, MT // XB - 1) as i:
                for t in range(XB):
                    expert_tile(i * XB + (1 + t), (1 + t) % XB)
            for m in range(MT - XB + 1, MT):
                expert_tile(m, m % XB, last=m == MT - 1)
            with act.Fori(0, NG) as g:
                act.wait_ge(c_aggr, g * GT + (NT + GT))
                std(std5b[:, :], mv5b[:, :, 1], c_std)

        @block.tensor
        def _(pe):
            pe.sem_inc(s_done, 2)
            pe.sem_inc(cn_done, 1)
            pe.wait_ge(consts, 16)
            pe.wait_ge(gw_in, 48)
            for k in range(KD):
                for h in range(KD):
                    ins = pe.transpose(bank[6][:, 256 * k + 128 * h:256 * k + 128 * h + 128], gW1[:, h, 128 * k:128 * k + 128], ident[:, :])
            ins.then_inc(wT_T, 1)
            for i in range(2):
                for k in range(2):
                    for h in range(KD):
                        ins = pe.transpose(bank[7 if i == 0 else 5][:, 256 * k + 128 * h:256 * k + 128 * h + 128],
                                           gW2[:, h, 128 * (2 * i + k):128 * (2 * i + k) + 128], ident[:, :])
                ins.then_inc(wT_T, 1)
            pe.wait_ge(bc_ready, 1)
            flat = spread.rearrange("p c q -> p (c q)")
            pe.matmul(bank[1][0:PQ, 0:2 * NS], ones[0:EP, 0:PQ], flat, start=True, stop=True).then_inc(bc_ready, 1)

            def slot(u, loc):
                if loc == 0:
                    pe.wait_ge(ring_act, u + 1)
                elif loc >= 3:
                    pe.wait_ge(ring_act, u - 1)
                return RING[loc % 3]

            def row_slot(u, loc):
                pe.wait_ge(row_dve, u + 1 if loc == 0 else u)
                return ROW[loc % 2]

            def tile_T(u, loc, rows, parts=T):
                to = slot(u, loc)
                for k in range(KD):
                    ins = pe.transpose(to[:, 128 * k:128 * k + parts], rows[:, 128 * k:128 * k + 128], ident[0:parts, 0:parts])
                ins.then_inc(ring_full, 1)

            def row(u, loc, products, cols=D, parts=T):
                to = row_slot(u, loc)
                for i, (a, b) in enumerate(products):
                    ins = pe.matmul(to[0:parts, 0:cols], a, b, start=i == 0, stop=i == len(products) - 1)
                ins.then_inc(row_full, 1)

            pe.wait_ge(wT_cp, 3)
            with pe.Fori(0, NG) as g:
                for j in range(GT):
                    pe.wait_ge(hn_done, g * GT + j + 1)
                    tile_T(g * GT + j, j, hn[:, j, :])
                for j in range(GT):
                    pe.wait_ge(ring_act, g * GT + j + 2)
                    row(g * GT + j, j, [(TT[:, k, j * T:(j + 1) * T], W1T[:, k, :]) for k in range(KD)])
            pe.wait_ge(ws_done, 48)
            pe.wait_ge(row_dve, NT + 1)
            for q in range(4):
                for h in range(KD):
                    ins = pe.transpose(bank[5][:, :].bitcast(bf16)[:, q * D + 128 * h:q * D + 128 * h + 128], WS[:, h, q, :], identb[:, :])
            ins.then_inc(ws_done, 1)
            pe_tables(0)
            pe.wait_ge(wT_cp, 4)
            pe.wait_ge(t_cp, 5)

            def edges(group, s, first=False):
                pe_edges(group * PG + s, group, s, first=first)

            def both(group, first=False):
                for s in range(PG):
                    edges(group, s, first=first and s == 0)
            for e in range(EG_FIRST):
                both(e, first=e == 0)
            pe.wait_ge(brow_out, 16 + 2 * L * 16)

            with pe.Fori(0, L) as l:
                pe.wait_ge(wA_in, l * 32 + 32)
                pe.sem_inc(settle_pe, 1)

                def normalised(h, u, loc):
                    for j in range(GT):
                        pe.wait_ge(hn_done, h + j + 1)
                        tile_T(u + j, loc + j, hn[:, j, :])
                normalised(l * HN_L + NT, l * RING_L + RING_A, 0)
                both(l * EG_L + EG_FIRST)
                with pe.Fori(0, NG) as g:
                    eg = l * EG_L + g + (EG_FIRST + EG_A)
                    h0, q0 = l * HN_L + g * GT + (NT + GT), l * (2 * NG) + g * 2
                    u0, r0 = l * RING_L + g * RING_GA + (RING_A + GT), l * ROW_L + g * ROW_GA + ROW_A
                    for pc, (a, b) in enumerate(PC):
                        for h in range(KD):
                            loc = 2 * pc + h
                            pe.wait_ge(ring_act, u0 + 1)
                            to = slot(u0 + loc, loc)
                            for k in range(KD):
                                ins = pe.matmul(to[:, 0:(b - a) * T], Wk_s[:, k, 128 * h:128 * h + 128], TT[:, k, TT_PIECES[pc]],
                                                start=k == 0, stop=k == KD - 1)
                            ins.then_inc(ring_full, 1)
                        for j in range(a, b):
                            row(r0 + j, j, [(TT[:, k, tt_cols(j)], Wv_s[:, k, :]) for k in range(KD)])
                    normalised(h0, u0 + 4, 4)
                    edges(eg, 0)
                    for pc, (a, b) in enumerate(PC):
                        for j in range(a, b):
                            loc = GT + 4 + j
                            pe.wait_ge(ring_act, u0 + (2 * pc + 3))
                            to = slot(u0 + loc, loc)
                            for h in range(KD):
                                ins = pe.transpose(to[0:T, 128 * h:128 * h + 128], eT[:, h, j * T:(j + 1) * T], ident[:, :])
                            ins.then_inc(ring_full, 1)
                    edges(eg, 1)
                    for pc, (a, b) in enumerate(PC):
                        to = row_slot(r0 + GT + pc, GT + pc)
                        for h in range(KD):
                            for j in range(a, b):
                                if h == 0:
                                    pe.wait_ge(ring_act, u0 + (GT + 4 + j + 2))
                                    pe.wait_ge(row_dve, r0 + j + 2)
                                ins = pe.matmul(to[:, 129 * h:129 * h + 129], es[:, j, 128 * h:128 * h + 128], V5[:, j, h, :],
                                                start=j == a, stop=j == b - 1)
                        ins.then_inc(row_full, 1)

                def queries(u, r, rloc):
                    for j in range(GT):
                        pe.wait_ge(ring_act, u + j + 2)
                        row(r + j, rloc + j, [(TT[:, k, tt_cols(j)], Wq_s[:, k, :]) for k in range(KD)])
                uM, rM = l * RING_L + (RING_A + RING_M), l * ROW_L + (ROW_A + ROW_M)
                edges(l * EG_L + (EG_FIRST + EG_M), 0)
                pe.wait_ge(cn_done, l + 2)
                to = slot(uM, 0)
                for h in range(KD):
                    ins = pe.transpose(to[:, 128 * h:128 * h + 128], ctxN[:, h, :], ident[:, :])
                ins.then_inc(ring_full, 1)
                pe.wait_ge(wQ_in, l * 32 + 32)
                queries(uM - GT, rM, 0)
                pe.wait_ge(ring_act, uM + 2)
                for h in range(KD):
                    row(rM + GT + h, GT + h, [(ctxT[:, h, :], Wo_s[:, h, :])], parts=128)
                edges(l * EG_L + (EG_FIRST + EG_M), 1)
                pe.wait_ge(wF_in, l * 32 + 32)
                pe.wait_ge(wF_lo, l * 2 + 2)
                pe.sem_inc(settle_pe, 1)

                def second(g, last=False):
                    n0, h0 = l * NG + g, l * HN_L + g * (2 * GT) + (2 * NT + GT)
                    u0 = l * RING_L + g * RING_GB + (RING_A + RING_B)
                    r0 = l * ROW_L + g * ROW_GB + (ROW_A + ROW_B)
                    rF = GT if last else 2 * GT
                    step = lambda i: edges(l * EG_L + g * 4 + (EG_FIRST + EG_B + i // PG), i % PG)
                    bias_row = lambda w: (onesb[:, 0:T], brow[:, ds(l * (2 * D) + w * D, D)])
                    pe.wait_ge(q_norm, n0 + 1)
                    for j in range(GT):
                        tile_T(u0 + j, j, qe[:, j, :])
                    for j in range(GT):
                        pe.wait_ge(ring_act, u0 + j + 2)
                        row(r0 + j, j, [(QT[:, k, j * T:(j + 1) * T], M_s[:, k, :]) for k in range(KD)] + [bias_row(0)])
                    step(0)
                    for j in range(GT):
                        pe.wait_ge(hn_done, h0 + j + 1)
                        tile_T(u0 + GT + j, GT + j, hn[:, j, :])
                    for f in range(NF):
                        part = slice(128 * f, 128 * f + 128)
                        for pc, (a, b) in enumerate(PC):
                            loc = 2 * GT + 2 * f + pc
                            if f == 0:
                                pe.wait_ge(tt_lo, n0 * GT + (b + 2))
                            to = slot(u0 + loc, loc)
                            cols = slice(0, PAD + 1) if pc == 0 else TT_PIECES[1]
                            for k in range(KD):
                                for i, (w, t) in enumerate(((W1_h[k][:, part], TTh), (W1_h[k][:, part], TTl), (W1_l[:, k, part], TTh))):
                                    ins = pe.matmul(to[:, 0:cols.stop - cols.start], w, t[:, k, cols],
                                                    start=k == 0 and i == 0, stop=k == KD - 1 and i == 2)
                            ins.then_inc(ring_full, 1)
                        if f % 2 == 0:
                            step(f // 2 + 1)
                    if not last:
                        normalised(h0 + GT, u0 + 2 * GT + 2 * NF, 2 * GT + 2 * NF)
                        queries(u0 + 2 * GT + 2 * NF, r0 + GT, GT)
                    step(5)
                    pe.wait_ge(ring_act, u0 + (2 * GT + 2 * NF + 1))
                    for j in range(GT):
                        if j % 2:
                            step(6 + j // 2)
                        row(r0 + rF + j, rF + j, [(hid[:, f, j * T:(j + 1) * T], W2_s[:, f, :]) for f in range(NF)] + [bias_row(1)])
                with pe.Fori(0, NG - 1) as g:
                    second(g)
                second(NG - 1, last=True)
            with pe.Fori(EG_LAST, NEG) as e:
                both(e)
            pe_sums(NPAIR - 1, 1)

            def pe_first(r):
                pe.wait_ge(t_cp, r * 5 + 5)
                pe.sem_inc(settle_pe, 1)
                both(r * NEG, first=True)

            def pe_last(r):
                both(r * NEG + (NEG - 1))
                pe_sums(r * NPAIR + (NPAIR - 1), 1)
            more_rounds(pe, pe_tables, pe_first, lambda e, ge: both(ge), pe_last)

            pe.wait_ge(late_in, 64)
            def graph_rows(g, u, r):
                pe.wait_ge(c_in, g * 16 + 16)
                pe.wait_ge(c_agg, g + 1)
                for j in range(GT):
                    tile_T(u + 2 * j, 2 * j, es[:, j, :])
                    tile_T(u + 2 * j + 1, 2 * j + 1, staged_sums[:, j, :])
                for j in range(GT):
                    pe.wait_ge(ring_act, u + 2 * j + 3)
                    row(r + j, j, [(TT[:, k, j * T:(j + 1) * T], W2T[:, k, :]) for k in range(KD)]
                        + [(QT[:, k, j * T:(j + 1) * T], W2T[:, KD + k, :]) for k in range(KD)])

            def gate(g, u, loc, r, rloc):
                for j in range(GT):
                    pe.wait_ge(hn_done, g * GT + (HN_C + j + 1))
                    tile_T(u + j, loc + j, hn[:, j, :])
                for j in range(GT):
                    pe.wait_ge(ring_act, u + j + 2)
                    row(r + j, rloc + j, [(eT[:, k, j * T:(j + 1) * T], gw_s[:, k, :]) for k in range(KD)], cols=NE)
            graph_rows(0, RING_C, ROW_C)
            with pe.Fori(0, NG - 1) as g:
                u0, r0 = g * (3 * GT) + (RING_C + 2 * GT), g * (2 * GT) + (ROW_C + GT)
                graph_rows(g + 1, u0, r0)
                gate(g, u0 + 2 * GT, 2 * GT, r0 + GT, GT)
            gate(NG - 1, RING_E - GT, 0, ROW_E - GT, 0)
            pe.wait_ge(r_mask, 2)
            flat = mask.rearrange("p t e -> p (t e)")
            pe.matmul(RING[0][0:T, 0:NT * NE], tri[:, :], flat, start=True, stop=True).then_inc(r_rank, 1)
            pe.matmul(RING[1][0:T, 0:NT * NE], ones[0:T, 0:T], flat, start=True, stop=True).then_inc(r_rank, 1)

            def slots_T(mi, s):
                pe.wait_ge(xs_in[s], mi * 16 + 16)
                for k in range(KD):
                    ins = pe.transpose(RING[0][:, SL * k:SL * (k + 1)], xs[s][:, 128 * k:128 * k + 128], ident[:, :])
                ins.then_inc(ring_full, 1)

            def up(mi, s):
                pe.wait_ge(w1_in[s], mi * 32 + 32)
                for c in range(NFE):
                    for k in range(KD):
                        ins = pe.matmul(RING[1 + s % 2][:, c * SL:(c + 1) * SL], W1e[s][:, k, c::NFE], xT[s % 2][:, k, :],
                                        start=k == 0, stop=k == KD - 1)
                ins.then_inc(ring_full, 1)

            def down(m, mi, s):
                pe.wait_ge(w2_in[s], mi * 32 + 32)
                pe.wait_ge(row_dve, m + ROW_E)
                for c in range(NFE):
                    ins = pe.matmul(ROW[s % 2][:, 0:D], hT[s % 2][:, c, :], W2e[s][:, c, :], start=c == 0, stop=c == NFE - 1)
                ins.then_inc(row_full, 1)

            def expert_tile(m, mi, s, first=False, last=False):
                u = m * 2 + (RING_E + 1)
                pe.wait_ge(ring_act, u + 1 if first else u)
                if not last:
                    slots_T(mi + (s + 1) // XB, (s + 1) % XB)
                up(mi, s)
                if not first:
                    pe.wait_ge(ring_act, u + 1)
                    down(m - 1, mi - (s == 0), (s - 1) % XB)
            pe.wait_ge(r_pos, 1)
            pe.wait_ge(ring_act, RING_E + 1)
            slots_T(0, 0)
            expert_tile(0, 0, 0, first=True)
            with pe.Fori(0, MT // XB - 1) as i:
                for t in range(XB):
                    s = (1 + t) % XB
                    expert_tile(i * XB + (1 + t), i + (1 + t) // XB, s)
            for m in range(MT - XB + 1, MT):
                expert_tile(m, m // XB, m % XB, last=m == MT - 1)
            pe.wait_ge(ring_act, 2 * MT + RING_E + 1)
            down(MT - 1, (MT - 1) // XB, (MT - 1) % XB)

        @block.vector
        def _(dve):
            dve.sem_inc(z_done, 4)
            dve.sem_inc(acc_done, 1)
            dve.sem_inc(lo_done, 2)
            dve.sem_inc(row_dve, 1)
            dve.sem_inc(f_u, 4 * GT)
            dve.sem_inc(f_n, 1)
            dve.sem_inc(out_done, 16)
            for i in range(2):
                dve.sem_inc(yo_out[i], 16)
            for j in range(GT):
                dve.sem_inc(p_out[j], 16)
            chain = [0]

            def link(ins):
                chain[0] += 1
                ins.then_inc(base_step, 1)
                dve.wait_ge(base_step, chain[0])

            dve.wait_ge(consts, 16)
            dve.wait_ge(dst_in, 16)
            dt = dst_tiles.rearrange("p (c e) -> p c e", e=SE)
            dve.tensor_reduce(hl[:, 0:EC], dt, AX.X, ALU.max)
            link(dve.tensor_reduce(hl[:, EC:2 * EC], dt, AX.X, ALU.min))
            link(dve.tensor_tensor(above, hl[:, :].unsqueeze(2).to_broadcast([EP, 2 * EC, NT - 1]),
                                   thr[:, :].unsqueeze(1).to_broadcast([EP, 2 * EC, NT - 1]), ALU.is_ge))
            link(dve.tensor_reduce(hlb[:, :], above, AX.X, ALU.add))
            link(dve.scalar_tensor_tensor(hlb[:, 0:EC], hlb[:, 0:EC], 1.0, hlb[:, EC:2 * EC], ALU.add, ALU.subtract))
            dve.tensor_tensor(spread, ident[0:EP, 0:EP].unsqueeze(1).to_broadcast([EP, 2 * EC, EP]),
                              hlb[:, :].unsqueeze(2).to_broadcast([EP, 2 * EC, EP]), ALU.mult).then_inc(bc_ready, 1)
            dve.wait_ge(gw_in, 48)
            dve.tensor_copy(w4[:, :, 0:EA], gW1[:, :, D:D + EA]).then_inc(wparts_done, 1)
            dve.wait_ge(wparts_done, 1)
            dve.tensor_copy(wparts[:, 0, :, :], w4[:, :, :]).then_inc(wparts_done, 1)
            dve.wait_ge(wparts_done, 2)
            dve.tensor_tensor(w4r[:, :, :], w4[:, :, :], wparts[:, 0, :, :], ALU.subtract).then_inc(wparts_done, 1)
            dve.wait_ge(wparts_done, 3)
            dve.tensor_copy(wparts[:, 1, :, :], w4r[:, :, :]).then_inc(wparts_done, 1)
            dve.wait_ge(wparts_done, 4)
            dve.tensor_tensor(wparts[:, 2, :, :], w4r[:, :, :], wparts[:, 1, :, :], ALU.subtract).then_inc(wparts_done, 1)
            dve.wait_ge(br_in, 32)
            dve.tensor_copy(bparts[:, 0, :], browf[:, :]).then_inc(brp_done, 1)
            dve.wait_ge(brp_done, 1)
            dve.tensor_tensor(browr[:, :], browf[:, :], bparts[:, 0, :], ALU.subtract).then_inc(brp_done, 1)
            dve.wait_ge(brp_done, 2)
            dve.tensor_copy(bparts[:, 1, :], browr[:, :]).then_inc(brp_done, 1)
            dve.wait_ge(brp_done, 3)
            dve.tensor_tensor(bparts[:, 2, :], browr[:, :], bparts[:, 1, :], ALU.subtract).then_inc(brp_done, 1)
            dve.wait_ge(bc_ready, 2)
            dve.tensor_copy(n_bc, bank[1][0:PQ, 0:NS])
            ins = dve.tensor_copy(lo_bc, bank[1][0:PQ, NS:2 * NS])
            link(ins)
            dve.tensor_copy(lo0[:, :], lo_bc[:, 0:1])
            link(dve.tensor_tensor_scan(cum[:, :], n_bc, n_bc, 0.0, ALU.add, ALU.max))
            dve.tensor_scalar(rjunk[:, :], thr2[:, :], cum[0:1, NS - 1:NS], None, ALU.is_lt, ALU.add, accum_out=rcnt[:, :])
            link(dve.tensor_tensor(junk, n_bc, cum[:, :], ALU.subtract))
            dve.tensor_copy(rounds_i[:, :], rcnt[:, :]).then_inc(rounds_done, 1)
            link(dve.tensor_tensor(junk, junk, lo_bc, ALU.add))
            dve.memset(dg[:, NS - 1:NS], 0.0)
            link(dve.tensor_tensor(dg[:, 0:NS - 1], junk[:, 1:NS], junk[:, 0:NS - 1], ALU.subtract))
            dve_tables_a(0)

            def aggregate(s_stat, s_aggr, n, st, mv):
                for j in range(GT):
                    dve.wait_ge(s_stat, n + j + 1)
                    dve.sem_inc(settle_dve, 1)
                    dve.bn_aggr(mv[:, j, :], st[:, j, :]).then_inc(s_aggr, 1)

            def stats(rows, s_stat, s_aggr, n, st, mv):
                dve.sem_inc(settle_dve, 1)
                for j in range(GT):
                    dve.bn_stats(st[:, j, :], rows(j)).then_inc(s_stat, 1)
                aggregate(s_stat, s_aggr, n, st, mv)

            for g in range(NG):
                dve.wait_ge(x_in[g], 16)
            def keep_stats(g, n, s_aggr, s_mv):
                dve.wait_ge(s_aggr, n + GT)
                dve.sem_inc(settle_dve, 1)
                dve.tensor_copy(mvA[:, ds(g * GT, GT), :], mv5[:, :, :]).then_inc(s_mv, 1)
            with dve.Fori(0, NG) as g:
                stats(lambda j: tile(X, g * GT + j), pstat, paggr, g * GT, st5, mv5)
                keep_stats(g, g * GT, paggr, p_mv)
            dve.wait_ge(pstd, 1)
            dve.reciprocal(rstd_t[:, :], stdA[:, :]).then_inc(prstd, 1)
            dve.wait_ge(prstd, 1)
            dve.sem_inc(settle_dve, 1)

            def normalised(g):
                for j in range(GT):
                    dve.tensor_scalar(hn[:, j, :], tile(X, g * GT + j), mvA[:, ds(g * GT + j, 1), 0], rstd_t[:, ds(g * GT + j, 1)],
                                      ALU.subtract, ALU.mult).then_inc(hn_done, 1)

            def projections(g, js):
                for j in js:
                    dve.wait_ge(row_full, g * GT + j + 1)
                    dve.wait_ge(p_out[j], g * 16 + 16)
                    dve.tensor_copy(es[:, j, :], ROW[j % 2][0:T, 0:D]).then_inc(row_dve, 1)
            normalised(0)
            with dve.Fori(0, NG - 1) as g:
                projections(g, (0, 1))
                dve.wait_ge(xcopied, g * GT + 2 * GT)
                dve.sem_inc(settle_dve, 1)
                normalised(g + 1)
                projections(g, (2, 3, 4))
            projections(NG - 1, range(GT))
            dve_tables_b(0)
            dve.wait_ge(t_cp, 5)

            def edges(e, group, s, first=False, last=False):
                dve_edges(e * PG + s, group * PG + s, group, s, first=first, last=last)

            def both(e, group, first=False, last=False):
                for s in range(PG):
                    edges(e, group, s, first=first and s == 0, last=last and s == PG - 1)
            dve.wait_ge(xcopied, NT + GT)
            with dve.Fori(0, NG) as g:
                stats(lambda j: tile(X, g * GT + j), a_stat, a_aggr, g * GT, st5, mv5)
                keep_stats(g, g * GT, a_aggr, a_mv)
            for e in range(EG_FIRST):
                both(e, e, first=e == 0)
            for i in range(AB):
                dve.wait_ge(a_out[i], len(range(i, AC, AB)) * 48)
            dve.wait_ge(xn_out, 16)

            for part in (TTh, TTl):
                dve.tensor_copy(part[:, :, PAD:PAD + 1], ident[:, 0:KD].unsqueeze(2)).then_inc(tt_lo, 1)

            def rest(of, low, high):
                return dve.tensor_tensor(low, of, high.bitcast(f32), ALU.subtract)

            with dve.Fori(0, L) as l:
                dve.wait_ge(a_std, l + 1)
                dve.reciprocal(rstd_t[:, :], stdA[:, :]).then_inc(a_rstd, 1)
                dve.memset(ctxS[:, :, :], 0.0).then_inc(l_init, 1)
                dve.memset(mO[:, :], LOW).then_inc(l_init, 1)
                dve.wait_ge(a_rstd, l + 1)
                dve.sem_inc(settle_dve, 1)

                normalised(0)
                both(l * EG_L + EG_FIRST, l * EG_L + EG_FIRST)
                dve.wait_ge(l_init, l * 2 + 2)
                dve.sem_inc(settle_dve, 1)

                def first(g, after):
                    eg = l * EG_L + g + (EG_FIRST + EG_A)
                    u0, r0, q0 = l * RING_L + g * RING_GA + (RING_A + GT), l * ROW_L + g * ROW_GA + ROW_A, l * (2 * NG) + g * 2
                    dve.wait_ge(ring_full, u0)
                    dve.sem_inc(settle_dve, 1)
                    normalised(after)
                    for pc, (a, b) in enumerate(PC):
                        for h in range(KD):
                            loc = 2 * pc + h
                            dve.wait_ge(ring_full, u0 + loc + 1)
                            dve.reduce_max(pm[:, h:h + 1], RING[loc % 3][:, 0:(b - a) * T], axis=AX.X).then_inc(k_max, 1)
                        dve.wait_ge(k_max, q0 * 2 + 2 * pc + 2)
                        if pc:
                            dve.wait_ge(m_cp, q0 + pc)
                        dve.tensor_tensor(mN[:, :], mO[:, :], pm[:, :], ALU.max).then_inc(m_new, 1)
                        dve.wait_ge(m_new, q0 + pc + 1)
                        dve.tensor_scalar(nb[:, pc, :], mN[:, :], -SCALE, None, ALU.mult).then_inc(nb_done, 1)
                        dve.wait_ge(nb_done, q0 + pc + 1)
                        dve.scalar_tensor_tensor(cdiff[:, pc, :], mO[:, :], SCALE, nb[:, pc, :], ALU.mult, ALU.add).then_inc(cd_done, 1)
                        dve.wait_ge(cd_done, q0 + pc + 1)
                        dve.tensor_copy(mO[:, :], mN[:, :]).then_inc(m_cp, 1)
                        for j in range(a, b):
                            dve.wait_ge(row_full, r0 + j + 1)
                            dve.tensor_copy(V5[:, j, :, 0:128], ROW[j % 2][0:T, 0:D].rearrange("p (k n) -> p k n", k=KD)).then_inc(row_dve, 1)
                    edges(eg, eg, 0)
                    edges(eg, eg, 1)
                    for pc in range(2):
                        dve.wait_ge(corr_done, q0 + pc + 1)
                        dve.wait_ge(row_full, r0 + (GT + pc + 1))
                        dve.wait_ge(row_dve, r0 + (GT + pc + 1))
                        for h in range(KD):
                            ins = dve.scalar_tensor_tensor(ctxS[:, h, :], ctxS[:, h, :], corr[:, pc, h:h + 1],
                                                           ROW[(GT + pc) % 2][:, 129 * h:129 * h + 129], ALU.mult, ALU.add)
                        ins.then_inc(row_dve, 1)
                with dve.Fori(0, NG - 1) as g:
                    first(g, g + 1)
                first(NG - 1, 0)

                heads = lambda ap: ap.rearrange("p (h d) -> p h d", d=DH)
                all_heads = qe[:, :, :].rearrange("p j (h d) -> p (j h) d", d=DH)
                per_head = lambda ap: ap.unsqueeze(2).to_broadcast([T, H, DH])

                def queries(r, rloc, n):
                    for j in range(GT):
                        q_ps = heads(ROW[(rloc + j) % 2][0:T, 0:D])
                        dve.wait_ge(row_full, r + j + 1)
                        dve.reduce_max(qm[:, j, :], q_ps, axis=AX.X).then_inc(q_max, 1)
                        dve.wait_ge(q_max, n * GT + j + 1)
                        dve.tensor_tensor(heads(qe[:, j, :]), q_ps, per_head(qm[:, j, :]), ALU.subtract).then_inc(row_dve, 1)

                def q_softmax(n):
                    dve.wait_ge(q_exp, n + 1)
                    dve.reduce_sum(qs[:, :, :].rearrange("p j h -> p (j h)"), all_heads, axis=AX.X).then_inc(q_sum, 1)
                    dve.wait_ge(q_sum, n + 1)
                    dve.reciprocal(qr[:, :, :], qs[:, :, :]).then_inc(q_rec, 1)
                    dve.wait_ge(q_rec, n + 1)
                    dve.tensor_tensor(all_heads, all_heads, qr[:, :, :].rearrange("p j h -> p (j h)").unsqueeze(2).to_broadcast([T, GT * H, DH]),
                                      ALU.mult).then_inc(q_norm, 1)
                rM, eM = l * ROW_L + (ROW_A + ROW_M), l * EG_L + (EG_FIRST + EG_M)
                dve.wait_ge(row_dve, rM + 1)
                dve.reciprocal(rk[:, :], ctxS[:, :, 128]).then_inc(rk_done, 1)
                dve.tensor_tensor(ctxN[:, :, :], ctxS[:, :, 0:128], headmask[:, :].unsqueeze(1).to_broadcast([128, KD, 128]),
                                  ALU.mult).then_inc(cn_done, 1)
                edges(eM, eM, 0)
                queries(rM, 0, l * NG)
                for k in range(KD):
                    dve.wait_ge(wF_hi, l * 2 + k + 1)
                    rest(W1_s[:, k, :], W1_l[:, k, :], W1_h[k][:, :]).then_inc(wF_lo, 1)
                q_softmax(l * NG)
                dve.wait_ge(rk_done, l + 1)
                for h in range(KD):
                    dve.wait_ge(row_full, rM + (GT + h + 1))
                    dve.tensor_scalar(M_s[:, h, :], ROW[(GT + h) % 2][:, 0:D], rk[:, h:h + 1], None, ALU.mult).then_inc(row_dve, 1)
                edges(eM, eM, 1)

                def second(g, last=False):
                    n0, lg = l * NT + g * GT, l * NG + g
                    u0 = l * RING_L + g * RING_GB + (RING_A + RING_B)
                    r0 = l * ROW_L + g * ROW_GB + (ROW_A + ROW_B)
                    rF = GT if last else 2 * GT
                    eg = lambda i: l * EG_L + g * 4 + (EG_FIRST + EG_B + i // PG)
                    step = lambda i: edges(eg(i), eg(i), i % PG)

                    def with_stats(write, written, s_stat, s_aggr, n, st, mv):
                        def stat(j):
                            dve.wait_ge(row_dve, written(j))
                            dve.sem_inc(settle_dve, 1)
                            dve.bn_stats(st[:, j, :], tile(X, g * GT + j)).then_inc(s_stat, 1)
                        for j in range(GT):
                            write(j)
                            if j:
                                stat(j - 1)
                        stat(GT - 1)
                        aggregate(s_stat, s_aggr, n, st, mv)

                    def residual(j, loc):
                        dve.wait_ge(row_full, r0 + loc + 1)
                        dve.tensor_tensor(tile(X, g * GT + j), ROW[loc % 2][0:T, 0:D], tile(X, g * GT + j), ALU.add).then_inc(row_dve, 1)
                    with_stats(lambda j: residual(j, j), lambda j: r0 + j + 2, b_stat, b_aggr, n0, st5b, mv5b)
                    dve.wait_ge(b_std, lg + 1)
                    dve.reciprocal(rs5b[:, :], std5b[:, :]).then_inc(b_rstd, 1)
                    dve.wait_ge(b_rstd, lg + 1)
                    dve.wait_ge(b_aggr, n0 + GT)
                    for j in range(GT):
                        dve.tensor_scalar(hn[:, j, :], tile(X, g * GT + j), mv5b[:, j, 0:1], rs5b[:, j:j + 1],
                                          ALU.subtract, ALU.mult).then_inc(hn_done, 1)
                    for j in range(GT):
                        cols = tt_cols(j)
                        dve.wait_ge(ring_act, u0 + GT + j + 2)
                        dve.tensor_copy(TTh[:, :, cols], TT[:, :, cols]).then_inc(tt_hi, 1)
                        dve.wait_ge(tt_hi, n0 + j + 1)
                        rest(TT[:, :, cols], TTl[:, :, cols], TTh[:, :, cols]).then_inc(tt_lo, 1)
                    step(0)
                    step(1)
                    if not last:
                        dve.wait_ge(ring_full, u0 + 2 * GT)
                        dve.sem_inc(settle_dve, 1)
                        normalised(g + 1)
                    step(2)
                    step(3)
                    step(4)
                    if not last:
                        queries(r0 + GT, GT, lg + 1)
                    step(5)

                    def output(j):
                        if j % 2:
                            step(6 + j // 2)
                        if j == 1 and not last:
                            q_softmax(lg + 1)
                        residual(j, rF + j)
                    with_stats(output, lambda j: r0 + rF + j + 2, a_stat, a_aggr, n0 + NT, st5, mv5)
                    keep_stats(g, n0 + NT, a_aggr, a_mv)
                with dve.Fori(0, NG - 1) as g:
                    second(g)
                second(NG - 1, last=True)

            for e in range(EG_LAST, NEG):
                both(e, e, last=e == NEG - 1)
            dve_acc(NPAIR - 1, block_of(NPAIR - 1))

            def dve_last(r):
                both(NEG - 1, r * NEG + (NEG - 1), last=True)
                dve_acc(r * NPAIR + (NPAIR - 1), block_of(NPAIR - 1))

            def tables(r):
                dve_tables_a(r)
                dve_tables_b(r)
                dve.wait_ge(t_cp, r * 5 + 5)
            more_rounds(dve, tables, lambda r: both(0, r * NEG, first=True), lambda e, ge: both(e, ge), dve_last)

            dve.wait_ge(late_in, 64)
            def stage_sums(g):
                dve.tensor_copy(staged_sums.rearrange("p j d -> p (j d)"), tile(agg, g * GT, GT)).then_inc(c_agg, 1)

            def positive(r):
                for j in range(GT):
                    dve.wait_ge(row_full, r + j + 1)
                    dve.tensor_scalar(HL[:, j, :], ROW[j % 2][0:T, 0:D], 0.0, None, ALU.max).then_inc(row_dve, 1)

            def experts_input(g):
                dve.wait_ge(c_nrm, g + 1)
                dve.tensor_scalar(nrm[:, :], nrm[:, :], 1e-12, None, ALU.max).then_inc(c_rn, 1)
                dve.wait_ge(c_rn, g * 2 + 1)
                dve.reciprocal(rn[:, :], nrm[:, :]).then_inc(c_rn, 1)
                dve.wait_ge(c_rn, g * 2 + 2)
                dve.wait_ge(q_in, g * 16 + 16)
                for j in range(GT):
                    dve.scalar_tensor_tensor(HL[:, j, :], HL[:, j, :], rn[:, j:j + 1], qe[:, j, :], ALU.mult, ALU.add).then_inc(c_y, 1)
                for j in range(GT):
                    dve.wait_ge(c_y, g * (2 * GT) + j + 1)
                    dve.tensor_tensor(tile(X, g * GT + j), HL[:, j, :], tile(X, g * GT + j), ALU.add).then_inc(c_y, 1)
                dve.wait_ge(c_y, g * (2 * GT) + 2 * GT)
                stats(lambda j: tile(X, g * GT + j), c_stat, c_aggr, g * GT, st5, mv5)
                dve.wait_ge(c_std, g + 1)
                dve.reciprocal(rs5b[:, :], std5[:, :]).then_inc(c_rstd, 1)
                dve.wait_ge(c_rstd, g + 1)
                dve.wait_ge(c_zcp, g + 1)
                for j in range(GT):
                    dve.tensor_scalar(hn[:, j, :], tile(X, g * GT + j), mv5[:, j, 0:1], rs5b[:, j:j + 1],
                                      ALU.subtract, ALU.mult).then_inc(hn_done, 1)

            def logits(g, r, rloc):
                for j in range(GT):
                    dve.wait_ge(row_full, r + j + 1)
                    dve.tensor_tensor(LG[:, ds((g * GT + j) * NE, NE)], ROW[(rloc + j) % 2][0:T, 0:NE], gb_s[:, :], ALU.add).then_inc(row_dve, 1)

            def group_end(g, last=False):
                r0 = g * (2 * GT) + (ROW_C + GT)
                experts_input(g)
                positive(r0)
                if not last:
                    stage_sums(g + 2)
                logits(g, r0 + GT, GT)
            stage_sums(0)
            positive(ROW_C)
            stage_sums(1)
            with dve.Fori(0, NG - 2) as g:
                group_end(g)
            group_end(NG - 2, last=True)
            experts_input(NG - 1)
            logits(NG - 1, ROW_E - GT, 0)
            dve.wait_ge(c_zcp, NG + 1)
            steps = [0]

            def then(ins):
                steps[0] += 1
                ins.then_inc(r_step, 1)
                dve.wait_ge(r_step, steps[0])

            dve.wait_ge(row_dve, ROW_E + 1)
            lg = LG[:, :].rearrange("p (t e) -> p t e", e=NE)
            per_tile = lambda ap: ap.unsqueeze(2).to_broadcast([T, NT, NE])
            per_expert = lambda ap: ap.unsqueeze(1).to_broadcast([T, NT, NE])
            flat = lambda ap: ap.rearrange("p t e -> p (t e)")
            for logits, most, sel in ((lg, m1, sel1), (lg2, m2, sel2)):
                then(dve.reduce_max(most[:, :], logits, axis=AX.X))
                then(dve.tensor_tensor(sel, logits, per_tile(most[:, :]), ALU.is_equal))
                then(dve.tensor_tensor(rtmp, sel, per_expert(iota_e[:, :]), ALU.mult))
                then(dve.tensor_reduce(i1[:, :], rtmp, AX.X, ALU.min))
                then(dve.tensor_tensor(sel, per_expert(iota_e[:, :]), per_tile(i1[:, :]), ALU.is_equal))
                if sel is sel1:
                    then(dve.scalar_tensor_tensor(flat(lg2), flat(sel1), LOW, LG[:, :], ALU.mult, ALU.add))
            dve.tensor_tensor(e21[:, :], m2[:, :], m1[:, :], ALU.subtract).then_inc(r_mask, 1)
            dve.tensor_tensor(mask, sel1, sel2, ALU.add).then_inc(r_mask, 1)
            dve.wait_ge(r_exp, 1)
            then(dve.tensor_scalar(w1t[:, :], e21[:, :], 1.0, None, ALU.add))
            then(dve.reciprocal(w1t[:, :], w1t[:, :]))
            then(dve.tensor_tensor(w2t[:, :], w1t[:, :], e21[:, :], ALU.mult))
            dve.wait_ge(r_rank, 2)
            tiles3 = lambda b: b[0:T, 0:NT * NE].rearrange("p (t e) -> p t e", e=NE)
            then(dve.tensor_copy(tot, tiles3(RING[1])))
            for x_ in range(NE):
                ins = dve.tensor_tensor_scan(cumt[:, :, x_], onee[:, :], tot[:, :, x_], 0.0, ALU.mult, ALU.add)
            then(ins)
            then(dve.tensor_tensor(nge, cumt[:, NT - 1, :].unsqueeze(2).to_broadcast([T, NE, NT]),
                                   thr3[:, :].unsqueeze(1).to_broadcast([T, NE, NT]), ALU.is_gt))
            then(dve.tensor_reduce(te[:, :], nge, AX.X, ALU.add))
            then(dve.tensor_tensor_scan(ce[:, :], onee[:, 0:NE], te[:, :], 0.0, ALU.mult, ALU.add))
            then(dve.tensor_tensor(ste[:, :], ce[:, :], te[:, :], ALU.subtract))
            then(dve.tensor_scalar(ste[:, :], ste[:, :], float(SL), None, ALU.mult))
            then(dve.tensor_tensor(slotp, tiles3(RING[0]), cumt, ALU.add))
            then(dve.tensor_tensor(slotp, slotp, tot, ALU.subtract))
            then(dve.tensor_tensor(slotp, slotp, per_expert(ste[:, :]), ALU.add))
            for sel, posf, pos in ((sel1, pos1f, pos1), (sel2, pos2f, pos2)):
                then(dve.tensor_tensor(rtmp, sel, slotp, ALU.mult))
                then(dve.tensor_reduce(posf[:, :], rtmp, AX.X, ALU.add))
                dve.tensor_copy(pos[:, :], posf[:, :]).then_inc(r_pos, 1)
            then(dve.tensor_tensor(ejc, ce[0:1, :].unsqueeze(1).to_broadcast([1, MT, NE]),
                                   jt[0:1, :].unsqueeze(2).to_broadcast([1, MT, NE]), ALU.is_le))
            then(dve.tensor_reduce(ejf[:, :], ejc, AX.X, ALU.add))
            dve.tensor_scalar(ej_row[:, :], ejf[:, :], float(NE - 1), None, ALU.min).then_inc(r_pos, 1)

            with dve.Fori(0, MT // XB) as i:
                for s in range(XB):
                    dve.wait_ge(row_full, i * XB + (s + ROW_E + 1))
                    dve.wait_ge(w2_in[s], i * 32 + 32)
                    dve.wait_ge(yo_out[s % 2], i * (XB // 2 * 16) + (s // 2 * 16 + 16))
                    dve.tensor_tensor(yo[s % 2][:, :], ROW[s % 2][:, 0:D], b2e[s], ALU.add).then_inc(row_dve, 1)
            dve.wait_ge(xb_done, 1)

            def finish(g, i, s):
                res1, res2 = RES[s]
                dve.wait_ge(fi_in[s], i * (2 * GT * 16) + 2 * GT * 16)
                dve.wait_ge(f_n, g * (2 * GT) + 1)
                dve.sem_inc(settle_dve, 1)
                for j in range(GT):
                    dve.scalar_tensor_tensor(u5[:, j, :], res1[:, j, :], w1t[:, ds(g * GT + j, 1)], tile(agg, g * GT + j), ALU.mult, ALU.add).then_inc(f_u, 1)
                    dve.wait_ge(f_u, g * (2 * GT) + 4 * GT + 2 * j + 1)
                    dve.sem_inc(settle_dve, 1)
                    dve.scalar_tensor_tensor(u5[:, j, :], res2[:, j, :], w2t[:, ds(g * GT + j, 1)], u5[:, j, :], ALU.mult, ALU.add).then_inc(f_u, 1)
                dve.wait_ge(f_u, g * (2 * GT) + 6 * GT)
                stats(lambda j: u5[:, j, :], c_stat, c_aggr, g * GT + NT, st5b, mv5b)
                dve.wait_ge(c_std, g + (NG + 1))
                dve.reciprocal(rs5b[:, :], std5b[:, :]).then_inc(c_rstd, 1)
                dve.wait_ge(c_rstd, g + (NG + 1))
                dve.wait_ge(c_aggr, g * GT + (NT + GT))
                dve.wait_ge(out_done, g * (GT * 16) + 16)
                for j in range(GT):
                    dve.scalar_tensor_tensor(u5[:, j, :], u5[:, j, :], mv5b[:, j, 0:1], gam_s[:, :], ALU.subtract, ALU.mult).then_inc(f_n, 1)
                for j in range(GT):
                    dve.wait_ge(f_n, g * (2 * GT) + j + 2)
                    dve.sem_inc(settle_dve, 1)
                    dve.scalar_tensor_tensor(fo[:, j, :], u5[:, j, :], rs5b[:, j:j + 1], tile(X, g * GT + j), ALU.mult, ALU.add).then_inc(f_n, 1)
            with dve.Fori(0, NG // 2) as i:
                for s in range(2):
                    finish(i * 2 + s, i, s)
            finish(NG - 1, NG // 2, 0)


def kernel(**inputs):
    import numpy as np
    import concourse.bacc as bacc
    from concourse.bass_utils import run_bass_kernel_spmd
    nc = bacc.Bacc("TRN2", target_bir_lowering=False, num_devices=1)
    arrays, args = {}, []
    for name in INPUTS:
        a = np.ascontiguousarray(inputs[name])
        arrays[f"in_{name}"] = a
        args.append(nc.dram_tensor(f"in_{name}", a.shape, mybir.dt.from_np(a.dtype), kind="ExternalInput").ap())
    out = nc.dram_tensor("out_0", inputs["x"].shape, mybir.dt.float32, kind="ExternalOutput").ap()
    build(nc, *args, out)
    result = run_bass_kernel_spmd(nc, [arrays], core_ids=[0])
    return result.results[0]["out_0"]
```
